# Optimizing a Trainium2 kernel written in Bass

```python
import numpy as np
import jax
import jax.numpy as jnp

def _softmax(x, axis=-1):
    return jax.nn.softmax(x, axis=axis)

def _gelu(x):
    return jax.nn.gelu(x, approximate=True)

def _silu(x):
    return jax.nn.silu(x)

def _sigmoid(x):
    return jax.nn.sigmoid(x)

def _layernorm(x, axis=-1, eps=1e-05):
    m = jnp.mean(x, axis=axis, keepdims=True)
    v = jnp.var(x, axis=axis, keepdims=True)
    return (x - m) / jnp.sqrt(v + eps)

def _scatter_add(tgt, idx, src, axis=0):
    return tgt.at[idx].add(src)

def _segment_sum(src, seg, n):
    return jax.ops.segment_sum(src, seg, n)
kernel_name = 'mk_seq_preln_d1_jaxref_r2_fae7c4'

def setup_inputs(seed: int=0):
    np.random.seed(seed)
    _w = jnp.asarray

    def _L0_attn_setup():
        import jax, jax.numpy as jnp
        import numpy as np
        from jax import lax
        D_MODEL = 512
        SEQ_LEN = 4096
        ORDER = 2
        BATCH = 2

        def _hyena_fwd(x, in_proj_w, in_proj_b, short_w, short_b, fw1, fb1, fw2, fb2, fw3, fb3, out_w, out_b):
            B, L, C = x.shape
            proj = (x @ in_proj_w + in_proj_b).reshape(B, L, C, ORDER + 1)
            v = proj[..., 0]
            x_branches = [proj[..., i] for i in range(1, ORDER + 1)]
            vc = v.transpose(0, 2, 1)
            vc = lax.conv_general_dilated(vc, short_w, window_strides=(1,), padding=((1, 1),), feature_group_count=C, dimension_numbers=('NCH', 'OIH', 'NCH'))
            v = (vc + short_b[None, :, None]).transpose(0, 2, 1)
            pos = jnp.linspace(0.0, 1.0, L, dtype=x.dtype)[:, None]
            h = jax.nn.gelu(pos @ fw1 + fb1, approximate=False)
            h = jax.nn.gelu(h @ fw2 + fb2, approximate=False)
            coefs = (h @ fw3 + fb3).reshape(L, C, ORDER)
            n = 2 * L
            v_fft = jnp.fft.rfft(v, n=n, axis=1)
            output = v
            for i in range(ORDER):
                h_fft = jnp.fft.rfft(coefs[:, :, i], n=n, axis=0)
                conv = jnp.fft.irfft(v_fft * h_fft[None], n=n, axis=1)[:, :L, :]
                output = x_branches[i] * conv
            return output @ out_w + out_b
        key = jax.random.key(seed)
        ks = jax.random.split(key, 16)
        s = 0.02
        return {'x': jax.random.normal(ks[0], (BATCH, SEQ_LEN, D_MODEL), jnp.float32), 'in_proj_w': jax.random.normal(ks[1], (D_MODEL, D_MODEL * (ORDER + 1)), jnp.float32) * s, 'in_proj_b': jax.random.normal(ks[2], (D_MODEL * (ORDER + 1),), jnp.float32) * s, 'short_w': jax.random.normal(ks[3], (D_MODEL, 1, 3), jnp.float32) * 0.5, 'short_b': jax.random.normal(ks[4], (D_MODEL,), jnp.float32) * s, 'fw1': jax.random.normal(ks[5], (1, 64), jnp.float32) * 0.5, 'fb1': jax.random.normal(ks[6], (64,), jnp.float32) * s, 'fw2': jax.random.normal(ks[7], (64, 128), jnp.float32) * 0.1, 'fb2': jax.random.normal(ks[8], (128,), jnp.float32) * s, 'fw3': jax.random.normal(ks[9], (128, D_MODEL * ORDER), jnp.float32) * 0.05, 'fb3': jax.random.normal(ks[10], (D_MODEL * ORDER,), jnp.float32) * s, 'out_w': jax.random.normal(ks[11], (D_MODEL, D_MODEL), jnp.float32) * s, 'out_b': jax.random.normal(ks[12], (D_MODEL,), jnp.float32) * s}
    _L0_attn_in = _L0_attn_setup()

    def _L0_ffn_setup():
        import jax, jax.numpy as jnp
        import numpy as np
        key = jax.random.key(seed)
        k_x, k_W, k_b, k_ids, k_w = jax.random.split(key, 5)
        N_ADAPTERS, D_OUT, D_IN = (32, 512, 512)
        B, S = (2, 1024)
        K = 8
        x = jax.random.normal(k_x, (B, S, D_IN), dtype=jnp.float32)
        W = jax.random.normal(k_W, (N_ADAPTERS, D_OUT, D_IN), dtype=jnp.float32)
        b = jax.random.normal(k_b, (N_ADAPTERS, D_OUT), dtype=jnp.float32)
        ids = jax.random.randint(k_ids, (K,), 0, N_ADAPTERS, dtype=jnp.int64)
        weights = jax.random.uniform(k_w, (K,), dtype=jnp.float32)
        return {'x': x, 'W': W, 'b': b, 'ids': ids, 'weights': weights}
    _L0_ffn_in = _L0_ffn_setup()
    _d = {'L0_attn_x': _L0_attn_in['x'], 'L0_attn_in_proj_w': _L0_attn_in['in_proj_w'], 'L0_attn_in_proj_b': _L0_attn_in['in_proj_b'], 'L0_attn_short_w': _L0_attn_in['short_w'], 'L0_attn_short_b': _L0_attn_in['short_b'], 'L0_attn_fw1': _L0_attn_in['fw1'], 'L0_attn_fb1': _L0_attn_in['fb1'], 'L0_attn_fw2': _L0_attn_in['fw2'], 'L0_attn_fb2': _L0_attn_in['fb2'], 'L0_attn_fw3': _L0_attn_in['fw3'], 'L0_attn_fb3': _L0_attn_in['fb3'], 'L0_attn_out_w': _L0_attn_in['out_w'], 'L0_attn_out_b': _L0_attn_in['out_b'], 'L0_ffn_W': _L0_ffn_in['W'], 'L0_ffn_b': _L0_ffn_in['b'], 'L0_ffn_ids': _L0_ffn_in['ids'], 'L0_ffn_weights': _L0_ffn_in['weights']}
    _x0 = _d['L0_attn_x']
    _d['L0_attn_x'] = jax.random.normal(jax.random.fold_in(jax.random.key(seed), 1), (8, 2048, 512), dtype=_x0.dtype)
    del _x0
    return _d

def reference(L0_attn_x, L0_attn_in_proj_w, L0_attn_in_proj_b, L0_attn_short_w, L0_attn_short_b, L0_attn_fw1, L0_attn_fb1, L0_attn_fw2, L0_attn_fb2, L0_attn_fw3, L0_attn_fb3, L0_attn_out_w, L0_attn_out_b, L0_ffn_W, L0_ffn_b, L0_ffn_ids, L0_ffn_weights):

    def _L0_attn_ref(x, in_proj_w, in_proj_b, short_w, short_b, fw1, fb1, fw2, fb2, fw3, fb3, out_w, out_b):
        import jax, jax.numpy as jnp
        import numpy as np
        from jax import lax
        D_MODEL = 512
        SEQ_LEN = 4096
        ORDER = 2
        BATCH = 2

        def _hyena_fwd(x, in_proj_w, in_proj_b, short_w, short_b, fw1, fb1, fw2, fb2, fw3, fb3, out_w, out_b):
            B, L, C = x.shape
            proj = (x @ in_proj_w + in_proj_b).reshape(B, L, C, ORDER + 1)
            v = proj[..., 0]
            x_branches = [proj[..., i] for i in range(1, ORDER + 1)]
            vc = v.transpose(0, 2, 1)
            vc = lax.conv_general_dilated(vc, short_w, window_strides=(1,), padding=((1, 1),), feature_group_count=C, dimension_numbers=('NCH', 'OIH', 'NCH'))
            v = (vc + short_b[None, :, None]).transpose(0, 2, 1)
            pos = jnp.linspace(0.0, 1.0, L, dtype=x.dtype)[:, None]
            h = jax.nn.gelu(pos @ fw1 + fb1, approximate=False)
            h = jax.nn.gelu(h @ fw2 + fb2, approximate=False)
            coefs = (h @ fw3 + fb3).reshape(L, C, ORDER)
            n = 2 * L
            v_fft = jnp.fft.rfft(v, n=n, axis=1)
            output = v
            for i in range(ORDER):
                h_fft = jnp.fft.rfft(coefs[:, :, i], n=n, axis=0)
                conv = jnp.fft.irfft(v_fft * h_fft[None], n=n, axis=1)[:, :L, :]
                output = x_branches[i] * conv
            return output @ out_w + out_b
        return _hyena_fwd(x, in_proj_w, in_proj_b, short_w, short_b, fw1, fb1, fw2, fb2, fw3, fb3, out_w, out_b)

    def _L0_ffn_ref(x, W, b, ids, weights):
        import jax, jax.numpy as jnp
        import numpy as np
        Wsel = W[ids]
        bsel = b[ids]
        out = jnp.einsum('k,kod,bsd->bso', weights, Wsel, x)
        out = out + jnp.einsum('k,ko->o', weights, bsel)
        return out
    x = L0_attn_x
    x = x + _L0_attn_ref(_layernorm(x, axis=-1), L0_attn_in_proj_w, L0_attn_in_proj_b, L0_attn_short_w, L0_attn_short_b, L0_attn_fw1, L0_attn_fb1, L0_attn_fw2, L0_attn_fb2, L0_attn_fw3, L0_attn_fb3, L0_attn_out_w, L0_attn_out_b)
    x = x + _L0_ffn_ref(_layernorm(x, axis=-1), L0_ffn_W, L0_ffn_b, L0_ffn_ids, L0_ffn_weights)
    return x

_drawn_inputs = setup_inputs


def setup_inputs(seed=0):
    import zlib

    import numpy as np

    out = dict(_drawn_inputs(seed))
    spreads = {}
    factors = {'L0_attn_out_b': 2.973}
    for name, (base, spread) in spreads.items():
        noise = np.random.default_rng([zlib.crc32(name.encode()), seed]).standard_normal(out[name].shape)
        drawn = base * np.exp(spread * noise) if base else spread * noise
        out[name] = jnp.asarray(drawn.astype(out[name].dtype))
    for name, factor in factors.items():
        out[name] = (out[name] * factor).astype(out[name].dtype)
    return out
```

```python
from contextlib import ExitStack

import numpy as np

import concourse.bass as bass
from concourse import mybir

F32 = mybir.dt.float32
F32R = mybir.dt.float32r
I32 = mybir.dt.int32
ALU = mybir.AluOpType
ACT = mybir.ActivationFunctionType

P = 128
B = 8
L = 2048
C = 512
CT = C // P
N1H = P
N2 = L // N1H
N = 2 * L
SLOTS = P
ROWS = 2 * SLOTS
KG = 4
GROUPS = SLOTS // KG
GB = B + 1
NIDS = 8
NADAPT = 32
EPS = 1e-5
SUB = 4


def stage_matrices():
    n1 = np.arange(N1H)[:, None, None]
    n2 = np.arange(N2)[None, :, None]
    k1 = np.arange(SLOTS)[None, None, :]
    n = n1 * N2 + n2
    ang = 2 * np.pi * ((n * k1) % N) / N
    sign = np.where(n1[:, :, 0] % 2 == 0, 1.0, -1.0)
    s1 = np.zeros((N1H, N2, SLOTS, 2))
    s1[..., 0] = np.cos(ang)
    s1[..., 1] = -np.sin(ang)
    s1[:, :, 0, 0] = 1.0
    s1[:, :, 0, 1] = sign
    s1x = np.zeros((1, SLOTS, 2))
    ax = 2 * np.pi * (((N - 1) * np.arange(SLOTS)) % N) / N
    s1x[0, :, 0] = np.cos(ax)
    s1x[0, :, 1] = -np.sin(ax)
    s1x[0, 0] = [1.0, -1.0]
    s4 = np.zeros((SLOTS, 2, N2, N1H))
    a4 = ang.transpose(2, 1, 0)
    s4[:, 0] = 2 * np.cos(a4) / N
    s4[:, 1] = -2 * np.sin(a4) / N
    s4[0, 0] = 1.0 / N
    s4[0, 1] = sign.T / N

    m = np.arange(N2)
    a = 2 * np.pi * ((m[:, None] * m[None, :]) % N2) / N2
    c, s = np.cos(a), np.sin(a)
    fwd = np.zeros((2, N2, 2, N2))
    fwd[0, :, 0], fwd[1, :, 0] = c, s
    fwd[0, :, 1], fwd[1, :, 1] = -s, c
    inv = np.zeros((2, N2, 2, N2))
    inv[0, :, 0], inv[1, :, 0] = c, -s
    inv[0, :, 1], inv[1, :, 1] = s, c
    half = N2 // 2
    fsp = np.zeros((2, N2, 2, N2))
    isp = np.zeros((2, N2, 2, N2))
    fsp[0, :, 0, 0] = 1.0
    fsp[0, :, 1, 0] = (-1.0) ** m
    isp[0, 0, 0, :] = 1.0
    isp[1, 0, 0, :] = (-1.0) ** m
    for k in range(1, half):
        fsp[0, :, 0, k], fsp[0, :, 1, k] = c[:, k], -s[:, k]
        isp[0, k, 0, :], isp[1, k, 0, :] = 2 * c[:, k], -2 * s[:, k]
    for k in range(half):
        b = 2 * np.pi * m * (k + 0.5) / N2
        fsp[1, :, 0, half + k], fsp[1, :, 1, half + k] = np.cos(b), -np.sin(b)
        isp[0, half + k, 1, :], isp[1, half + k, 1, :] = 2 * np.cos(b), -2 * np.sin(b)

    def same(f):
        out = np.zeros_like(f)
        out[:, :, 0] = out[:, :, 1] = f[:, :, 0]
        return out

    def cross(f):
        out = np.zeros_like(f)
        out[:, :, 0] = out[:, :, 1] = f[:, :, 1]
        return out

    def turned(f):
        out = np.zeros_like(f)
        out[0], out[1] = f[1], -f[0]
        return out

    same_sp, cross_sp = same(fsp), cross(fsp)
    same_sp[:, :, 1, 0] = fsp[:, :, 1, 0]
    cross_sp[:, :, :, 0] = 0.0

    def tile(first, rest):
        out = np.zeros((KG, 2 * N2, KG, 2 * N2))
        for g in range(KG):
            out[g, :, g, :] = (first if g == 0 else rest).reshape(2 * N2, 2 * N2)
        return out.reshape(P, P)

    kinds = [(fwd, fsp), (same(fwd), same_sp), (cross(fwd), cross_sp), (inv, isp), (turned(inv), turned(isp))]
    mid = np.stack([tile(sp, g) for g, sp in kinds] + [tile(g, g) for g, sp in kinds], axis=1)
    return {
        "pos": np.linspace(0.0, 1.0, L).astype(np.float32).reshape(1, L),
        "s1": s1.reshape(N1H, N2, ROWS).astype(np.float32),
        "s1x": s1x.reshape(1, ROWS).astype(np.float32),
        "s4": s4.reshape(ROWS, N2, N1H).astype(np.float32),
        "mid": mid.astype(np.float32),
        "ident": np.eye(P, dtype=np.float32),
    }


def pipelined(eng, outer, tiles, stages):
    fill = max(lag for _, lag in stages)

    def step(i, s, last):
        for stage, lag in stages:
            t = s - lag
            if t >= tiles and not last:
                stage(i + 1, t - tiles)
            elif 0 <= t < tiles:
                stage(i, t)

    for s in range(fill):
        step(0, s, False)

    def one_pass(i, last):
        for s in range(fill, tiles + fill):
            step(i, s, last)

    one_pass(0, False)
    with eng.Fori(1, outer - 1) as i:
        one_pass(i, False)
    one_pass(outer - 1, True)


def old(b, t, n):
    return not (isinstance(b, int) and b * N2 + t < n)


def hyena_adapter_kernel(nc, x, in_w, in_b, short_w, short_b, fw1, fb1, fw2, fb2, fw3, fb3,
                         out_w, out_b, w_ad, b_ad, ids, weights, consts, out):
    ctx = ExitStack()
    spec1 = nc.dram_tensor("spec1", [GB, ROWS * N2, C], F32, kind="Internal").ap()
    spec3 = nc.dram_tensor("spec3", [B, ROWS * N2, C], F32, kind="Internal").ap()
    gate_t = nc.dram_tensor("gate_t", [B, N2, P, C], F32, kind="Internal").ap()
    first_v = nc.dram_tensor("first_v", [B, C], F32, kind="Internal").ap()
    edge_f = nc.dram_tensor("edge_f", [2, P, N2 * C], F32, kind="Internal").ap()
    ad_wt = nc.dram_tensor("ad_wt", [P, CT * C], F32, kind="Internal").ap()
    ad_bias = nc.dram_tensor("ad_bias", [P, C], F32, kind="Internal").ap()

    def sem(name):
        return ctx.enter_context(nc.semaphore(name))

    def mm3(pe, out_ps, w_hi, w_lo, d_hi, d_lo, first, last):
        pe.matmul(out_ps, w_hi, d_hi, start=first, stop=False)
        pe.matmul(out_ps, w_hi, d_lo, start=False, stop=False)
        return pe.matmul(out_ps, w_lo, d_hi, start=False, stop=last)

    def prep():
        with ExitStack() as st:
            def sb(name, shape, dt=F32):
                return st.enter_context(nc.sbuf_tensor(name, shape, dt))

            def ps(name):
                return st.enter_context(nc.psum_tensor(name, [P, C], F32))

            LP = L + 2
            pos = sb("pos", [64, L])
            w1c = sb("w1c", [64, 1])
            b1c = sb("b1c", [64, 1])
            w2s = sb("w2s", [64, P])
            b2c = sb("b2c", [P, 1])
            w3 = sb("w3", [P, 2 * C])
            w3s = sb("w3s", [P, C])
            b3r = sb("b3r", [1, 2 * C])
            b3s = sb("b3s", [1, C])
            b3c = sb("b3c", [P, CT])
            tapr = sb("tapr", [P, 3 * C])
            tapc = sb("tapc", [P, CT, 3])
            sbc = sb("sbc", [P, CT])
            h1 = sb("h1", [64, L])
            h2 = sb("h2", [P, LP])
            inside = sb("inside", [1, LP])
            H = sb("H", [P, N2 + 2, C])
            g = H
            gx = sb("gx", [P, 2, C])
            g_before = sb("g_before", [1, C])
            s1 = sb("ps1", [P, N2, ROWS])
            s1x = sb("ps1x", [1, ROWS])
            s1o = sb("s1o", [P, 2, C])
            ht = sb("ht", [P, L + 1])
            cum = sb("cum", [P, L])
            ones = sb("ones", [P, L])
            edge = sb("edge", [P, N2, P])
            edge2 = sb("edge2", [P, N2, P])
            ident = sb("pident", [P, P])
            wsum = sb("wsum", [P, CT, C])
            wt = sb("wt", [P, CT, C])
            wload = sb("wload", [P, CT, C])
            bload = sb("bload", [P, C])
            bsum = sb("bsum", [P, C])
            wgt = sb("wgt", [P, NIDS])
            idst = sb("idst", [1, NIDS], I32)
            pA = [ps("pA0"), ps("pA1")]
            pB = [ps("pB0"), ps("pB1")]

            loaded = sem("p_loaded")
            ids_in = sem("p_ids_in")
            zeroed = sem("p_zeroed")
            h1_done = sem("p_h1_done")
            h2_ps = sem("p_h2_ps")
            h2_done = sem("p_h2_done")
            sliced = sem("p_sliced")
            H_ps = sem("p_H_ps")
            H_done = sem("p_H_done")
            tap_step = sem("p_tap_step")
            g_done = sem("p_g_done")
            s1_ps = sem("p_s1_ps")
            s1_out = sem("p_s1_out")
            s1_stored = sem("p_s1_stored")
            ht_ps = sem("p_ht_ps")
            ht_done = sem("p_ht_done")
            cum_done = sem("p_cum_done")
            edge_done = sem("p_edge_done")
            edge_stored = sem("p_edge_stored")
            w_in = sem("p_w_in")
            w_used = sem("p_w_used")
            wt_ps = sem("p_wt_ps")
            wt_done = sem("p_wt_done")
            ad_stored = sem("p_ad_stored")

            block = st.enter_context(nc.Block())
            LOADS = 15 * 16

            @block.sync
            def _(sp):
                sp.dma_start(pos[:], consts["pos"].partition_broadcast(64)).then_inc(loaded, 16)
                sp.dma_start(w1c[:], fw1.rearrange("a (p b) -> p (a b)", b=1)).then_inc(loaded, 16)
                sp.dma_start(b1c[:], fb1.rearrange("(p b) -> p b", b=1)).then_inc(loaded, 16)
                sp.dma_start(w2s[:], fw2).then_inc(loaded, 16)
                sp.dma_start(b2c[:], fb2.rearrange("(p b) -> p b", b=1)).then_inc(loaded, 16)
                sp.dma_start(w3[:], fw3).then_inc(loaded, 16)
                sp.dma_start(b3r[:], fb3.rearrange("(a n) -> a n", a=1)).then_inc(loaded, 16)
                with nc.allow_non_contiguous_dma(reason="512 words of bias, once"):
                    sp.dma_start(b3c[:], fb3.rearrange("(c p two) -> p c two", p=P, two=2)[:, :, 1]).then_inc(loaded, 16)
                    sp.dma_start(tapc[:], short_w.rearrange("(c p) a w -> p c (a w)", p=P)).then_inc(loaded, 16)
                    sp.dma_start(sbc[:], short_b.rearrange("(c p) -> p c", p=P)).then_inc(loaded, 16)
                sp.dma_start(tapr[:], short_w.rearrange("(o c) a w -> o (c a w)", o=1).partition_broadcast(P)).then_inc(loaded, 16)
                sp.dma_start(wgt[:], weights.rearrange("(a n) -> a n", a=1).partition_broadcast(P)).then_inc(loaded, 16)
                sp.dma_start(ident[:], consts["ident"]).then_inc(loaded, 16)
                sp.dma_start(s1[:], consts["s1"]).then_inc(loaded, 16)
                sp.dma_start(s1x[:], consts["s1x"]).then_inc(loaded, 16)
                sp.dma_start(idst[:], ids.rearrange("(a n) -> a n", a=1)).then_inc(ids_in, 16)
                sp.wait_ge(ids_in, 16)
                for k in range(NIDS):
                    which = sp.value_load(idst[0:1, k:k + 1], min_val=0, max_val=NADAPT - 1)
                    if k >= 1:
                        sp.wait_ge(w_used, 2 * k)
                    sp.dma_start(wload[:], w_ad[bass.ds(which, 1)].rearrange("a (t p) d -> (a p) t d", p=P)).then_inc(w_in, 16)
                    sp.dma_start(bload[:], b_ad[bass.ds(which, 1)].partition_broadcast(P)).then_inc(w_in, 16)
                for n2 in range(N2):
                    sp.wait_ge(s1_out, 2 * n2 + 2)
                    for j in range(2):
                        sp.dma_start(spec1[B].rearrange("(j p n) c -> n p j c", j=2, n=N2)[n2][:, j, :],
                                     s1o[:, j, :]).then_inc(s1_stored, 16)
                sp.wait_ge(s1_stored, 2 * 16 * N2)
                sp.wait_ge(wt_done, CT)
                sp.dma_start(ad_wt, wt[:].rearrange("p t c -> p (t c)")).then_inc(ad_stored, 16)
                sp.wait_ge(w_used, 2 * NIDS)
                sp.dma_start(ad_bias, bsum[:]).then_inc(ad_stored, 16)
                sp.wait_ge(ad_stored, 32)

            @block.gpsimd
            def _(pool):
                pool.memset(ones[:], 1.0).then_inc(zeroed, 1)
                pool.memset(inside[:], 1.0).then_inc(zeroed, 1)
                pool.wait_ge(zeroed, 2)
                pool.memset(inside[:, 0:1], 0.0).then_inc(zeroed, 1)
                pool.memset(inside[:, LP - 1:LP], 0.0).then_inc(zeroed, 1)
                pool.memset(h2[:, 0:1], 0.0).then_inc(zeroed, 1)
                pool.memset(h2[:, LP - 1:LP], 0.0).then_inc(zeroed, 1)
                pool.memset(ht[:, L:L + 1], 0.0).then_inc(zeroed, 1)
                for ct in range(CT):
                    pool.wait_ge(edge_done, 2 * ct + 2)
                    for q, buf in ((0, edge), (1, edge2)):
                        pool.dma_start(edge_f[q].rearrange("p (n c r) -> c p n r", n=N2, c=CT)[ct], buf[:]).then_inc(edge_stored, 16)
                    pool.wait_ge(edge_stored, 32 * (ct + 1))

            @block.scalar
            def _(act):
                act.wait_ge(loaded, LOADS)
                act.activation(h1[:], pos[:], ACT.Gelu, bias=b1c[:], scale=w1c[:]).then_inc(h1_done, 1)
                for q in range(L // C):
                    act.wait_ge(h2_ps, q + 1)
                    act.activation(h2[:, 1 + q * C:1 + (q + 1) * C], pA[q % 2][:], ACT.Gelu, bias=b2c[:]).then_inc(h2_done, 1)
                for e in range(N2 + 2):
                    act.wait_ge(H_ps, e + 1)
                    act.activation(H[:, e, :], pA[e % 2][:], ACT.Copy).then_inc(H_done, 1)
                for ct in range(CT):
                    if ct >= 1:
                        act.wait_ge(edge_done, 2 * ct)
                    for q in range(L // C):
                        act.wait_ge(ht_ps, ct * (L // C) + q + 1)
                        act.activation(ht[:, q * C:(q + 1) * C], pA[q % 2][:], ACT.Identity,
                                       bias=b3c[:, ct:ct + 1]).then_inc(ht_done, 1)
                for n2 in range(N2):
                    for j in range(2):
                        act.wait_ge(s1_ps, 2 * n2 + j + 1)
                        if n2 >= 1:
                            act.wait_ge(s1_stored, 32 * n2)
                        act.activation(s1o[:, j, :], pB[j][:], ACT.Copy).then_inc(s1_out, 1)

            @block.tensor
            def _(pe):
                pe.wait_ge(loaded, LOADS)
                pe.wait_ge(h1_done, 1)
                for q in range(L // C):
                    if q >= 2:
                        pe.wait_ge(h2_done, q - 1)
                    pe.matmul(pA[q % 2][:], w2s[:], h1[:, q * C:(q + 1) * C], start=True, stop=True).then_inc(h2_ps, 1)
                pe.wait_ge(h2_done, L // C)
                pe.wait_ge(sliced, 2)
                pe.wait_ge(zeroed, 7)
                for e in range(N2 + 2):
                    if e >= 2:
                        pe.wait_ge(H_done, e - 1)
                    cols = slice(e, e + (N1H - 1) * N2 + 1, N2)
                    pe.matmul(pA[e % 2][:], h2[:, cols], w3s[:], start=True, stop=False)
                    pe.matmul(pA[e % 2][:], inside[:, cols], b3s[:], start=False, stop=True).then_inc(H_ps, 1)
                pe.wait_ge(H_done, N2 + 2)
                for ct in range(CT):
                    for q in range(L // C):
                        n = ct * (L // C) + q
                        if n >= 2:
                            pe.wait_ge(ht_done, n - 1)
                        pe.matmul(pA[q % 2][:], w3s[:, ct * P:(ct + 1) * P], h2[:, 1 + q * C:1 + (q + 1) * C],
                                  start=True, stop=True).then_inc(ht_ps, 1)
                pe.wait_ge(g_done, 2)
                for n2 in range(N2):
                    edge_row = n2 == N2 - 1
                    for j in range(2):
                        if n2 >= 1:
                            pe.wait_ge(s1_out, 2 * n2 + j - 1)
                        mm = pe.matmul(pB[j][:], s1[:, n2, j * P:(j + 1) * P], g[:, n2, :], start=True, stop=not edge_row)
                        if edge_row:
                            mm = pe.matmul(pB[j][:], s1x[:, j * P:(j + 1) * P], g_before[:], start=False, stop=True)
                        mm.then_inc(s1_ps, 1)
                pe.wait_ge(w_used, 2 * NIDS)
                pe.wait_ge(H_done, N2 + 2)
                pe.wait_ge(ht_done, CT * L // C)
                for d in range(CT):
                    if d >= 2:
                        pe.wait_ge(wt_done, d - 1)
                    for o in range(CT):
                        mm = pe.transpose(pA[d % 2][:, o * P:(o + 1) * P], wsum[:, o, d * P:(d + 1) * P], ident[:])
                    mm.then_inc(wt_ps, 1)

            @block.vector
            def _(dve):
                dve.wait_ge(loaded, LOADS)
                dve.tensor_copy(w3s[:], w3[:].rearrange("p (c two) -> p c two", two=2)[:, :, 1]).then_inc(sliced, 1)
                dve.tensor_copy(b3s[:], b3r[:].rearrange("p (c two) -> p c two", two=2)[:, :, 1]).then_inc(sliced, 1)
                dve.wait_ge(H_done, N2 + 2)
                tap = tapr[:].rearrange("p (c w) -> p w c", w=3)
                steps = 0
                dve.tensor_tensor(g_before[:], H[0:1, 1, :], tap[0:1, 2, :], ALU.mult).then_inc(g_done, 1)
                for n2 in range(N2):
                    dve.tensor_tensor(g[:, n2, :], H[:, n2, :], tap[:, 0, :], ALU.mult).then_inc(tap_step, 1)
                    for w in (1, 2):
                        dve.tensor_tensor(gx[:, w - 1, :], H[:, n2 + w, :], tap[:, w, :], ALU.mult).then_inc(tap_step, 1)
                    steps += 3
                    for w in (1, 2):
                        dve.wait_ge(tap_step, steps)
                        last = dve.tensor_tensor(g[:, n2, :], g[:, n2, :], gx[:, w - 1, :], ALU.add)
                        last.then_inc(tap_step, 1)
                        steps += 1
                    dve.wait_ge(tap_step, steps)
                dve.sem_inc(g_done, 1)
                for ct in range(CT):
                    dve.wait_ge(ht_done, (ct + 1) * (L // C))
                    dve.wait_ge(zeroed, 7)
                    if ct >= 1:
                        dve.wait_ge(edge_stored, 32 * ct)
                    dve.tensor_tensor_scan(cum[:], ones[:], ht[:, 0:L], 0.0, ALU.mult, ALU.add).then_inc(cum_done, 1)
                    dve.tensor_scalar(edge[:], ht[:, 1:L + 1].rearrange("p (r n) -> p n r", n=N2), tapc[:, ct, 2:3], -1.0,
                                      ALU.mult, ALU.mult).then_inc(edge_done, 1)
                    dve.wait_ge(cum_done, ct + 1)
                    dve.tensor_scalar(edge2[:], cum[:].rearrange("p (r n) -> p n r", n=N2), sbc[:, ct:ct + 1], None,
                                      ALU.mult).then_inc(edge_done, 1)
                for k in range(NIDS):
                    dve.wait_ge(w_in, 32 * (k + 1))
                    if k == 0:
                        dve.tensor_scalar(wsum[:], wload[:], wgt[:, 0:1], None, ALU.mult).then_inc(w_used, 1)
                        dve.tensor_scalar(bsum[:], bload[:], wgt[:, 0:1], None, ALU.mult).then_inc(w_used, 1)
                        continue
                    dve.wait_ge(w_used, 2 * k)
                    dve.scalar_tensor_tensor(wsum[:], wload[:], wgt[:, k:k + 1], wsum[:], ALU.mult, ALU.add).then_inc(w_used, 1)
                    dve.scalar_tensor_tensor(bsum[:], bload[:], wgt[:, k:k + 1], bsum[:], ALU.mult, ALU.add).then_inc(w_used, 1)
                for d in range(CT):
                    dve.wait_ge(wt_ps, d + 1)
                    dve.tensor_copy(wt[:, d, :], pA[d % 2][:]).then_inc(wt_done, 1)

    def front():
        with ExitStack() as st:
            def sb(name, shape, dt=F32):
                return st.enter_context(nc.sbuf_tensor(name, shape, dt))

            def ps(name):
                return st.enter_context(nc.psum_tensor(name, [P, C], F32))

            s1h = sb("s1h", [P, N2, ROWS], F32R)
            s1l = sb("s1l", [P, N2, ROWS], F32R)
            wvh = sb("wvh", [P, CT, C], F32R)
            wvl = sb("wvl", [P, CT, C], F32R)
            wgh = sb("wgh", [P, CT, C], F32R)
            wgl = sb("wgl", [P, CT, C], F32R)
            ident = sb("fident", [P, P])
            bv3 = sb("bv3", [P, 3 * C])
            bvr = bv3[:].rearrange("p (c w) -> p w c", w=3)[:, 0, :]
            bgc = sb("bgc", [P, CT])
            xg = sb("xg", [P, 2, SUB, C])
            stats = sb("fstats", [P, 2, SUB, 6])
            mv = sb("fmv", [P, 2, SUB, 2])
            rstd = sb("frstd", [P, 2, SUB])
            shift = sb("fshift", [P, 2, SUB])
            power = sb("fpower", [P, SUB])
            eps = sb("feps", [P, SUB])
            minus = sb("fminus", [P, SUB])
            xn = sb("xn", [P, 2, C])
            nth = sb("nth", [P, 2, CT, SUB * P], F32R)
            ntl = sb("ntl", [P, 2, CT, SUB * P], F32R)
            v = sb("v", [P, 2, C])
            vh = sb("vh", [P, 2, C], F32R)
            vl = sb("vl", [P, 2, C], F32R)
            s1o = sb("fs1o", [P, 2, 2, SUB, C])
            gto = sb("gto", [P, 2, SUB, CT, P])
            raw = s1o[:].rearrange("p a b c d -> p (a b c d)")
            psT = [ps("psT0"), ps("psT1")]
            psV = [ps("psV0"), ps("psV1")]
            psS = [ps("psS0"), ps("psS1")]
            psX = [ps("psX0"), ps("psX1")]

            w_in = sem("f_w_in")
            w_split = sem("f_w_split")
            power_set = sem("f_power_set")
            passed = sem("f_passed")
            passed_sp = sem("f_passed_sp")
            hi_split = sem("f_hi_split")
            small_in = sem("f_small_in")
            x_in = [sem(f"f_x_in{i}") for i in range(2)]
            x_free = sem("f_x_free")
            bn_step = sem("f_bn_step")
            mv_done = sem("f_mv_done")
            pow_step = sem("f_pow_step")
            norm_ready = sem("f_norm_ready")
            xn_done = sem("f_xn_done")
            t_ps = sem("f_t_ps")
            nt_hi = sem("f_nt_hi")
            nt_lo = sem("f_nt_lo")
            v_ps = sem("f_v_ps")
            v_done = sem("f_v_done")
            v0_out = sem("f_v0_out")
            v_hi = sem("f_v_hi")
            v_lo = sem("f_v_lo")
            s_ps = sem("f_s_ps")
            s_out0 = sem("f_s_out0")
            s_out1 = sem("f_s_out1")
            s_stored = [sem(f"f_s_stored{i}") for i in range(2)]
            x2_ps = sem("f_x2_ps")
            x2_out = sem("f_x2_out")
            x2_stored = [sem(f"f_x2_stored{i}") for i in range(2)]

            block = st.enter_context(nc.Block())
            Q = N2 // SUB

            def tile_no(b, t):
                return b * N2 + t

            def group_no(b, t):
                return b * Q + t // SUB

            @block.sync
            def _(sp):
                W3 = 3 * C
                for kt in range(CT):
                    sp.dma_start(raw[:, kt * W3:(kt + 1) * W3], in_w[kt * P:(kt + 1) * P, :]).then_inc(w_in, 16)
                sp.dma_start(bv3[:], in_b.rearrange("(a c) -> a c", a=1).partition_broadcast(P)).then_inc(small_in, 16)
                with nc.allow_non_contiguous_dma(reason="512 words of bias, once"):
                    sp.dma_start(bgc[:], in_b.rearrange("(c p w) -> p c w", p=P, w=3)[:, :, 2]).then_inc(small_in, 16)
                sp.dma_start(ident[:], consts["ident"]).then_inc(small_in, 16)
                sp.wait_ge(w_split, 2)
                sp.dma_start(raw[:, 0:N2 * ROWS], consts["s1"].rearrange("p n r -> p (n r)")).then_inc(w_in, 16)

                def load_x(b, t):
                    if t % SUB:
                        return
                    slot = (t // SUB) % 2
                    sp.wait_ge(x_free, group_no(b, t) + 1)
                    sp.dma_start(xg[:, slot], x[b].rearrange("(p n) c -> p n c", n=N2)[:, t:t + SUB, :]).then_inc(x_in[slot], 16)

                def store(b, t):
                    if t == 0:
                        sp.wait_ge(v_done, tile_no(b, 0) + 1)
                        sp.dma_start(first_v[b].rearrange("(a c) -> a c", a=1), v[0:1, 0, :]).then_inc(v0_out, 16)
                    if t % SUB != SUB - 1:
                        return
                    slot = (t // SUB) % 2
                    sp.wait_ge(s_out0, tile_no(b, t) + 1)
                    sp.wait_ge(s_out1, tile_no(b, t) + 1)
                    for j in range(2):
                        sp.dma_start(spec1[b].rearrange("(j p n) c -> j p n c", j=2, n=N2)[j, :, t - SUB + 1:t + 1, :],
                                     s1o[:, slot, j]).then_inc(s_stored[slot], 16)

                def store_x2(b, t):
                    if t % SUB != SUB - 1:
                        return
                    slot = (t // SUB) % 2
                    sp.wait_ge(x2_out, tile_no(b, t) + 1)
                    sp.sem_inc(passed_sp, 1)
                    sp.dma_start(gate_t[b].rearrange("n p c -> p n c")[:, t - SUB + 1:t + 1, :],
                                 gto[:, slot].rearrange("p n c r -> p n (c r)")).then_inc(x2_stored[slot], 16)

                pipelined(sp, B, N2, [(load_x, 0), (store, 6), (store_x2, 8)])
                for slot in range(2):
                    sp.wait_ge(s_stored[slot], 16 * 2 * B * Q // 2)
                    sp.wait_ge(x2_stored[slot], 16 * B * Q // 2)
                sp.wait_ge(v0_out, 16 * B)

            @block.scalar
            def _(act):
                wraw = raw[:, 0:CT * 3 * C].rearrange("p (k c w) -> p k c w", k=CT, w=3)
                act.wait_ge(w_in, 16 * CT)
                act.activation(wvh[:], wraw[:, :, :, 0], ACT.Copy).then_inc(hi_split, 1)
                act.activation(wgh[:], wraw[:, :, :, 2], ACT.Copy).then_inc(hi_split, 1)
                act.wait_ge(w_in, 16 * (CT + 1))
                act.activation(s1h[:].rearrange("p n r -> p (n r)"), raw[:, 0:N2 * ROWS], ACT.Copy).then_inc(hi_split, 1)
                act.wait_ge(small_in, 48)

                def norm(b, t):
                    slot = (t // SUB) % 2
                    act.wait_ge(norm_ready, group_no(b, t) + 1)
                    if old(b, t, 2):
                        act.wait_ge(t_ps, tile_no(b, t) - 1)
                    op = act.activation(xn[:, t % 2], xg[:, slot, t % SUB], ACT.Identity,
                                        bias=shift[:, slot, t % SUB:t % SUB + 1],
                                        scale=rstd[:, slot, t % SUB:t % SUB + 1])
                    op.then_inc(xn_done, 1)

                def nt_high(b, t):
                    g = (t // SUB) % 2
                    act.wait_ge(t_ps, tile_no(b, t) + 1)
                    if old(b, t, 2 * SUB):
                        act.wait_ge(x2_ps, (group_no(b, t) - 1) * SUB)
                    act.activation(nth[:, g, :, (t % SUB) * P:(t % SUB + 1) * P],
                                   psT[t % 2][:].rearrange("p (k r) -> p k r", k=CT), ACT.Copy).then_inc(nt_hi, 1)

                def v_high(b, t):
                    act.wait_ge(v_done, tile_no(b, t) + 1)
                    if old(b, t, 2):
                        act.wait_ge(s_ps, 2 * (tile_no(b, t) - 1))
                    act.activation(vh[:, t % 2], v[:, t % 2], ACT.Copy).then_inc(v_hi, 1)

                def s_copy(b, t):
                    slot = (t // SUB) % 2
                    act.wait_ge(s_ps, 2 * tile_no(b, t) + 1)
                    if t % SUB == 0 and old(b, t, 2 * SUB):
                        act.wait_ge(s_stored[slot], 32 * (b * (Q // 2) + t // (2 * SUB)))
                    act.activation(s1o[:, slot, 0, t % SUB], psS[0][:], ACT.Copy).then_inc(s_out0, 1)

                def x2_copy(b, t):
                    slot, ct = (t // SUB) % 2, t % SUB
                    act.wait_ge(x2_ps, tile_no(b, t) + 1)
                    if ct == 0 and old(b, t, 2 * SUB):
                        act.wait_ge(x2_stored[slot], 16 * (b * (Q // 2) + t // (2 * SUB)))
                    act.activation(gto[:, slot, :, ct, :], psX[ct % 2][:].rearrange("p (n r) -> p n r", n=SUB),
                                   ACT.Identity, bias=bgc[:, ct:ct + 1]).then_inc(x2_out, 1)

                pipelined(act, B, N2, [(norm, 0), (nt_high, 0), (v_high, 1), (x2_copy, 4), (s_copy, 2)])

            @block.gpsimd
            def _(pool):
                pool.memset(power[:], -0.5).then_inc(power_set, 1)
                pool.memset(eps[:], EPS).then_inc(power_set, 1)
                pool.memset(minus[:], -1.0).then_inc(power_set, 1)
                pool.wait_ge(w_split, 3)
                pool.wait_ge(power_set, 3)

                def scalars(b, t):
                    if t % SUB:
                        return
                    slot = (t // SUB) % 2
                    n = group_no(b, t)
                    pool.wait_ge(mv_done, (n + 1) * SUB)
                    if old(b, t, 2 * SUB):
                        pool.wait_ge(xn_done, (n - 1) * SUB)
                    pool.tensor_tensor(rstd[:, slot], mv[:, slot, :, 1], eps[:], ALU.add).then_inc(pow_step, 1)
                    pool.tensor_tensor(shift[:, slot], mv[:, slot, :, 0], minus[:], ALU.mult).then_inc(pow_step, 1)
                    pool.wait_ge(pow_step, 3 * n + 2)
                    pool.tensor_tensor(rstd[:, slot], rstd[:, slot], power[:], ALU.pow).then_inc(pow_step, 1)
                    pool.wait_ge(pow_step, 3 * n + 3)
                    pool.tensor_tensor(shift[:, slot], shift[:, slot], rstd[:, slot], ALU.mult).then_inc(norm_ready, 1)

                def v_low(b, t):
                    pool.wait_ge(v_hi, tile_no(b, t) + 1)
                    pool.tensor_tensor(vl[:, t % 2], v[:, t % 2], vh[:, t % 2].bitcast(F32), ALU.subtract).then_inc(v_lo, 1)

                pipelined(pool, B, N2, [(scalars, 0), (v_low, 1)])

            @block.tensor
            def _(pe):
                pe.wait_ge(w_split, 3)
                pe.wait_ge(small_in, 48)

                def turn(b, t):
                    pe.wait_ge(xn_done, tile_no(b, t) + 1)
                    if old(b, t, 2):
                        pe.wait_ge(nt_lo, tile_no(b, t) - 1)
                    for kt in range(CT):
                        mm = pe.transpose(psT[t % 2][:, kt * P:(kt + 1) * P], xn[:, t % 2, kt * P:(kt + 1) * P], ident[:])
                    mm.then_inc(t_ps, 1)

                def project_v(b, t):
                    g = (t // SUB) % 2
                    pe.wait_ge(nt_lo, tile_no(b, t) + 1)
                    if old(b, t, 2):
                        pe.wait_ge(v_done, tile_no(b, t) - 1)
                    cols = slice((t % SUB) * P, (t % SUB + 1) * P)
                    for kt in range(CT):
                        mm = mm3(pe, psV[t % 2][:], nth[:, g, kt, cols], ntl[:, g, kt, cols], wvh[:, kt], wvl[:, kt],
                                 kt == 0, kt == CT - 1)
                    mm.then_inc(v_ps, 1)

                def project_x2(b, t):
                    g, ct = (t // SUB) % 2, t % SUB
                    if old(b, t, 2):
                        pe.wait_ge(x2_out, tile_no(b, t) - 1)
                    for kt in range(CT):
                        mm = mm3(pe, psX[ct % 2][:], wgh[:, kt, ct * P:(ct + 1) * P], wgl[:, kt, ct * P:(ct + 1) * P],
                                 nth[:, g, kt], ntl[:, g, kt], kt == 0, kt == CT - 1)
                    mm.then_inc(x2_ps, 1)

                def stage1(b, t):
                    pe.wait_ge(v_lo, tile_no(b, t) + 1)
                    for j in range(2):
                        if old(b, t, 1):
                            pe.wait_ge((s_out0, s_out1)[j], tile_no(b, t))
                        mm = mm3(pe, psS[j][:], s1h[:, t, j * P:(j + 1) * P], s1l[:, t, j * P:(j + 1) * P],
                                 vh[:, t % 2], vl[:, t % 2], True, True)
                        mm.then_inc(s_ps, 1)

                pipelined(pe, B, N2, [(turn, 0), (project_v, 1), (project_x2, 4), (stage1, 2)])

            @block.vector
            def _(dve):
                wraw = raw[:, 0:CT * 3 * C].rearrange("p (k c w) -> p k c w", k=CT, w=3)
                dve.wait_ge(hi_split, 2)
                dve.tensor_tensor(wvl[:], wraw[:, :, :, 0], wvh[:].bitcast(F32), ALU.subtract).then_inc(w_split, 1)
                dve.tensor_tensor(wgl[:], wraw[:, :, :, 2], wgh[:].bitcast(F32), ALU.subtract).then_inc(w_split, 1)
                dve.wait_ge(hi_split, 3)
                dve.tensor_tensor(s1l[:].rearrange("p n r -> p (n r)"), raw[:, 0:N2 * ROWS],
                                  s1h[:].rearrange("p n r -> p (n r)").bitcast(F32), ALU.subtract).then_inc(w_split, 1)
                dve.wait_ge(w_split, 3)
                dve.wait_ge(small_in, 48)
                dve.sem_inc(x_free, 2)

                def moments(b, t):
                    if t % SUB:
                        return
                    slot = (t // SUB) % 2
                    n = group_no(b, t)
                    dve.wait_ge(x_in[slot], 16 * (b * (Q // 2) + t // (2 * SUB) + 1))
                    for i in range(SUB):
                        dve.bn_stats(stats[:, slot, i], xg[:, slot, i]).then_inc(bn_step, 1)
                    dve.wait_ge(bn_step, n * SUB + SUB)
                    if old(b, t, 2 * SUB):
                        dve.wait_ge(norm_ready, n - 1)
                    dve.sem_inc(passed, 1)
                    for i in range(SUB):
                        dve.bn_aggr(mv[:, slot, i], stats[:, slot, i]).then_inc(mv_done, 1)

                def nt_low(b, t):
                    g = (t // SUB) % 2
                    cols = slice((t % SUB) * P, (t % SUB + 1) * P)
                    dve.wait_ge(nt_hi, tile_no(b, t) + 1)
                    dve.tensor_tensor(ntl[:, g, :, cols], psT[t % 2][:].rearrange("p (k r) -> p k r", k=CT),
                                      nth[:, g, :, cols].bitcast(F32), ALU.subtract).then_inc(nt_lo, 1)
                    if t % SUB == SUB - 1:
                        dve.sem_inc(x_free, 1)

                def v_bias(b, t):
                    dve.wait_ge(v_ps, tile_no(b, t) + 1)
                    if old(b, t, 2):
                        dve.wait_ge(v_lo, tile_no(b, t) - 1)
                    if t == 2:
                        dve.wait_ge(v0_out, 16 * (b + 1))
                    dve.tensor_tensor(v[:, t % 2], psV[t % 2][:], bvr, ALU.add).then_inc(v_done, 1)

                def s_copy(b, t):
                    slot = (t // SUB) % 2
                    dve.wait_ge(s_ps, 2 * tile_no(b, t) + 2)
                    if t % SUB == 0 and old(b, t, 2 * SUB):
                        dve.wait_ge(s_stored[slot], 32 * (b * (Q // 2) + t // (2 * SUB)))
                    dve.tensor_copy(s1o[:, slot, 1, t % SUB], psS[1][:]).then_inc(s_out1, 1)

                pipelined(dve, B, N2, [(moments, 0), (nt_low, 0), (v_bias, 1), (s_copy, 2)])

    def middle():
        with ExitStack() as st:
            def sb(name, shape, dt=F32):
                return st.enter_context(nc.sbuf_tensor(name, shape, dt))

            def ps(name):
                return st.enter_context(nc.psum_tensor(name, [P, C], F32))

            mats = sb("mats", [P, 10, P])
            xin = sb("m_xin", [P, 2, GB, C])
            spec = sb("m_spec", [P, 2, 2, C])
            u = sb("m_u", [P, 2, 2, C])
            wo = sb("m_wo", [P, 2, B, C])
            psZ = [ps("m_psZ0"), ps("m_psZ1")]
            psF = [ps("m_psF0"), ps("m_psF1")]
            psW = [ps("m_psW0"), ps("m_psW1")]
            small_in = sem("m_small_in")
            x_in = [sem(f"m_x_in{i}") for i in range(2)]
            f_ps = sem("m_f_ps")
            f_done = sem("m_f_done")
            z_ps = sem("m_z_ps")
            u_done = sem("m_u_done")
            w_ps = sem("m_w_ps")
            w_out = sem("m_w_out")
            stored = [sem(f"m_stored{i}") for i in range(2)]
            block = st.enter_context(nc.Block())

            T = 2 * GB

            def group(i, t):
                return i * 2 + t // GB

            def data_no(i, t):
                return group(i, t) * B + t % GB - 1

            def kind(m, i, t):
                first = isinstance(i, int) and i == 0 and t < GB
                return mats[:, m if first else m + 5, :]

            def early(i, t, first_groups=2):
                return isinstance(i, int) and i == 0 and t // GB < first_groups

            @block.sync
            def _(sp):
                sp.dma_start(mats[:], consts["mid"]).then_inc(small_in, 16)

                def load(i, t):
                    if t % GB:
                        return
                    par = t // GB
                    if not early(i, t):
                        sp.wait_ge(z_ps, (group(i, t) - 1) * B)
                    sp.dma_start(xin[:, par], spec1.rearrange("b (g p) c -> g p b c", p=P)[group(i, t)]
                                 if isinstance(i, int) else
                                 spec1.rearrange("b (g p) c -> g p b c", p=P)[bass.ds(group(i, t), 1)].rearrange(
                                     "g p b c -> (g p) b c")).then_inc(x_in[par], 16)

                def store(i, t):
                    if t % GB != GB - 1:
                        return
                    par = t // GB
                    sp.wait_ge(w_out, data_no(i, t) + 1)
                    sp.dma_start(spec3.rearrange("b (g p) c -> g p b c", p=P)[group(i, t)]
                                 if isinstance(i, int) else
                                 spec3.rearrange("b (g p) c -> g p b c", p=P)[bass.ds(group(i, t), 1)].rearrange(
                                     "g p b c -> (g p) b c"), wo[:, par]).then_inc(stored[par], 16)

                pipelined(sp, GROUPS // 2, T, [(load, 0), (store, 2)])
                for par in range(2):
                    sp.wait_ge(stored[par], 16 * GROUPS // 2)

            @block.tensor
            def _(pe):
                pe.wait_ge(small_in, 16)

                def stage2(i, t):
                    par = t // GB
                    if t % GB == 0:
                        pe.wait_ge(x_in[par], 16 * (i + 1))
                        if not early(i, t, 1):
                            pe.wait_ge(f_done, 2 * group(i, t))
                        for m in (1, 2):
                            pe.matmul(psF[m - 1][:], kind(m, i, t), xin[:, par, B, :], start=True, stop=True).then_inc(f_ps, 1)
                        return
                    n = data_no(i, t)
                    if not (early(i, t, 1) and t < 3):
                        pe.wait_ge(u_done, 2 * (n - 1))
                    pe.matmul(psZ[(t % GB - 1) % 2][:], kind(0, i, t), xin[:, par, t % GB - 1, :],
                              start=True, stop=True).then_inc(z_ps, 1)

                def stage3(i, t):
                    if t % GB == 0:
                        return
                    n = data_no(i, t)
                    k = (t % GB - 1) % 2
                    pe.wait_ge(u_done, 2 * n + 2)
                    if not (early(i, t, 1) and t < 3):
                        pe.wait_ge(w_out, n - 1)
                    pe.matmul(psW[k][:], kind(3, i, t), u[:, k, 0, :], start=True, stop=False)
                    pe.matmul(psW[k][:], kind(4, i, t), u[:, k, 1, :], start=False, stop=True).then_inc(w_ps, 1)

                pipelined(pe, GROUPS // 2, T, [(stage2, 0), (stage3, 1)])

            @block.scalar
            def _(act):
                def spectrum(i, t):
                    if t % GB:
                        return
                    par = t // GB
                    for m in range(2):
                        act.wait_ge(f_ps, 2 * group(i, t) + m + 1)
                        if m == 0 and not early(i, t):
                            act.wait_ge(u_done, 2 * (group(i, t) - 1) * B)
                        act.activation(spec[:, par, m, :], psF[m][:], ACT.Copy).then_inc(f_done, 1)

                def out_copy(i, t):
                    if t % GB == 0:
                        return
                    par, b = t // GB, t % GB - 1
                    act.wait_ge(w_ps, data_no(i, t) + 1)
                    if b == 0 and not early(i, t):
                        act.wait_ge(stored[par], 16 * i)
                    act.activation(wo[:, par, b, :], psW[b % 2][:], ACT.Copy).then_inc(w_out, 1)

                pipelined(act, GROUPS // 2, T, [(spectrum, 0), (out_copy, 1)])

            @block.vector
            def _(dve):
                def product(i, t):
                    if t % GB == 0:
                        return
                    par, b = t // GB, t % GB - 1
                    n = data_no(i, t)
                    dve.wait_ge(z_ps, n + 1)
                    if b == 0:
                        dve.wait_ge(f_done, 2 * group(i, t) + 2)
                    if not (early(i, t, 1) and b < 2):
                        dve.wait_ge(w_ps, n - 1)
                    for m in range(2):
                        dve.tensor_tensor(u[:, b % 2, m, :], psZ[b % 2][:], spec[:, par, m, :], ALU.mult).then_inc(u_done, 1)

                pipelined(dve, GROUPS // 2, T, [(product, 0)])

    def back():
        with ExitStack() as st:
            def sb(name, shape, dt=F32):
                return st.enter_context(nc.sbuf_tensor(name, shape, dt))

            def ps(name):
                return st.enter_context(nc.psum_tensor(name, [P, C], F32))

            s4 = sb("b_s4", [P, 2, N2, P])
            woh = sb("woh", [P, CT, C], F32R)
            wol = sb("wol", [P, CT, C], F32R)
            wfh = sb("wfh", [P, CT, C], F32R)
            wfl = sb("wfl", [P, CT, C], F32R)
            raw = sb("b_raw", [P, CT, C])
            edge = sb("b_edge", [P, 2, N2, C])
            v0 = sb("b_v0", [P, CT, B])
            bor = sb("bor", [P, C])
            bfr = sb("bfr", [P, C])
            ident = sb("b_ident", [P, P])
            D = 4
            fin = sb("b_fin", [P, 2, 2, C])
            gin = sb("b_gin", [P, 2, CT, P])
            xin = sb("b_xin", [P, D, C])
            corr = sb("b_corr", [P, 2, C])
            o = sb("b_o", [P, C])
            oh = sb("b_oh", [P, 2, C], F32R)
            ol = sb("b_ol", [P, 2, C], F32R)
            y = sb("b_y", [P, 2, C])
            stats = sb("b_stats", [P, 6])
            mv = sb("b_mv", [P, 2])
            rstd = sb("b_rstd", [P, 2])
            shift = sb("b_shift", [P, 2])
            power = sb("b_power", [P, 1])
            eps = sb("b_eps", [P, 1])
            minus = sb("b_minus", [P, 1])
            z = sb("b_z", [P, 2, C])
            yb = sb("b_yb", [P, 2, C])
            zh = sb("b_zh", [P, 2, C], F32R)
            zl = sb("b_zl", [P, 2, C], F32R)
            res = sb("b_res", [P, 2, C])
            psC = [ps("b_psC0"), ps("b_psC1")]
            psO = [ps("b_psO0"), ps("b_psO1")]
            psT = [ps("b_psT0"), ps("b_psT1")]
            psF = [ps("b_psF0"), ps("b_psF1")]

            small_in = sem("b_small_in")
            power_set = sem("b_power_set")
            passed = sem("b_passed")
            passed_pool = sem("b_passed_pool")
            raw_in = sem("b_raw_in")
            hi_split = sem("b_hi_split")
            lo_split = sem("b_lo_split")
            f_in = [sem(f"b_f_in{i}") for i in range(2)]
            g_in = [sem(f"b_g_in{i}") for i in range(2)]
            x_in = [sem(f"b_x_in{i}") for i in range(D)]
            corr_step = sem("b_corr_step")
            corr_done = sem("b_corr_done")
            xb_done = sem("b_xb_done")
            c_ps = sem("b_c_ps")
            a_done = sem("b_a_done")
            o_done = sem("b_o_done")
            o_hi = sem("b_o_hi")
            o_lo = sem("b_o_lo")
            o_ps = sem("b_o_ps")
            y_done = sem("b_y_done")
            bn_step = sem("b_bn_step")
            mv_done = sem("b_mv_done")
            pow_step = sem("b_pow_step")
            norm_ready = sem("b_norm_ready")
            z_done = sem("b_z_done")
            yb_done = sem("b_yb_done")
            t_ps = sem("b_t_ps")
            z_hi = sem("b_z_hi")
            z_lo = sem("b_z_lo")
            ff_ps = sem("b_ff_ps")
            res_done = sem("b_res_done")
            out_stored = [sem(f"b_out_stored{i}") for i in range(2)]
            block = st.enter_context(nc.Block())

            def no(b, t):
                return b * N2 + t

            @block.sync
            def _(sp):
                sp.dma_start(s4[:], consts["s4"].rearrange("(j p) n r -> p j n r", p=P)).then_inc(small_in, 16)
                for q in range(2):
                    sp.dma_start(edge[:, q], edge_f[q].rearrange("p (n c) -> p n c", n=N2)).then_inc(small_in, 16)
                with nc.allow_non_contiguous_dma(reason="4096 words, once"):
                    for ct in range(CT):
                        sp.dma_start(v0[:, ct], first_v.rearrange("b (c p) -> c p b", p=P)[ct]).then_inc(small_in, 16)
                sp.dma_start(bor[:], out_b.rearrange("(a c) -> a c", a=1).partition_broadcast(P)).then_inc(small_in, 16)
                sp.dma_start(bfr[:], ad_bias).then_inc(small_in, 16)
                sp.dma_start(ident[:], consts["ident"]).then_inc(small_in, 16)
                sp.dma_start(raw[:], out_w.rearrange("(k p) c -> p k c", p=P)).then_inc(raw_in, 16)
                sp.wait_ge(lo_split, 1)
                sp.dma_start(raw[:], ad_wt.rearrange("p (k c) -> p k c", k=CT)).then_inc(raw_in, 16)

                def load_conv(b, t):
                    if old(b, t, 2):
                        sp.wait_ge(c_ps, no(b, t) - 1)
                    sp.dma_start(fin[:, t % 2], spec3[b].rearrange("(j p n) c -> n p j c", j=2, n=N2)[t]).then_inc(f_in[t % 2], 16)

                def load_gate(b, t):
                    if old(b, t, 2):
                        sp.wait_ge(o_done, no(b, t) - 1)
                    sp.dma_start(gin[:, t % 2], gate_t[b, t].rearrange("p (c r) -> p c r", c=CT)).then_inc(g_in[t % 2], 16)

                def load_x(b, t):
                    if old(b, t, D):
                        sp.wait_ge(y_done, no(b, t) - D + 1)
                    sp.dma_start(xin[:, t % D], x[b].rearrange("(p n) c -> n p c", n=N2)[t]).then_inc(x_in[t % D], 16)

                pipelined(sp, B, N2, [(load_conv, 0), (load_gate, 0), (load_x, 0)])

            @block.gpsimd
            def _(pool):
                pool.memset(power[:], -0.5).then_inc(power_set, 1)
                pool.memset(eps[:], EPS).then_inc(power_set, 1)
                pool.memset(minus[:], -1.0).then_inc(power_set, 1)
                pool.wait_ge(small_in, 16 * 10)
                pool.wait_ge(power_set, 3)

                def scalars(b, t):
                    pool.wait_ge(mv_done, no(b, t) + 1)
                    if old(b, t, 2):
                        pool.wait_ge(z_done, no(b, t) - 1)
                    r, m = rstd[:, t % 2:t % 2 + 1], shift[:, t % 2:t % 2 + 1]
                    pool.tensor_tensor(r, mv[:, 1:2], eps[:], ALU.add).then_inc(pow_step, 1)
                    pool.tensor_tensor(m, mv[:, 0:1], minus[:], ALU.mult).then_inc(pow_step, 1)
                    pool.wait_ge(pow_step, 3 * no(b, t) + 2)
                    pool.tensor_tensor(r, r, power[:], ALU.pow).then_inc(pow_step, 1)
                    pool.wait_ge(pow_step, 3 * no(b, t) + 3)
                    pool.tensor_tensor(m, m, r, ALU.mult).then_inc(norm_ready, 1)

                def correct(b, t):
                    if old(b, t, 2):
                        pool.wait_ge(o_done, no(b, t) - 1)
                    pool.sem_inc(passed_pool, 1)
                    v0b = v0[:, :, b:b + 1] if isinstance(b, int) else v0[:, :, bass.ds(b, 1)]
                    pool.tensor_tensor(corr[:, t % 2].rearrange("p (c r) -> p c r", c=CT),
                                       edge[:, 0, t].rearrange("p (c r) -> p c r", c=CT),
                                       v0b.to_broadcast([P, CT, P]), ALU.mult).then_inc(corr_step, 1)
                    pool.wait_ge(corr_step, no(b, t) + 1)
                    pool.tensor_tensor(corr[:, t % 2], corr[:, t % 2], edge[:, 1, t], ALU.add).then_inc(corr_done, 1)

                def bias_x(b, t):
                    pool.wait_ge(x_in[t % D], 16 * (b * (N2 // D) + t // D + 1))
                    pool.tensor_tensor(xin[:, t % D], xin[:, t % D], bor[:], ALU.add).then_inc(xb_done, 1)

                def bias_y(b, t):
                    pool.wait_ge(y_done, no(b, t) + 1)
                    if old(b, t, 2):
                        pool.wait_ge(res_done, no(b, t) - 1)
                    pool.tensor_tensor(yb[:, t % 2], y[:, t % 2], bfr[:], ALU.add).then_inc(yb_done, 1)

                pipelined(pool, B, N2, [(scalars, 1), (correct, 0), (bias_x, 0), (bias_y, 1)])

            @block.scalar
            def _(act):
                act.wait_ge(raw_in, 16)
                act.activation(woh[:], raw[:], ACT.Copy).then_inc(hi_split, 1)
                act.wait_ge(raw_in, 32)
                act.activation(wfh[:], raw[:], ACT.Copy).then_inc(hi_split, 1)

                def o_high(b, t):
                    act.wait_ge(o_done, no(b, t) + 1)
                    if old(b, t, 2):
                        act.wait_ge(o_ps, no(b, t) - 1)
                    act.activation(oh[:, t % 2], o[:], ACT.Copy).then_inc(o_hi, 1)

                def norm(b, t):
                    act.wait_ge(norm_ready, no(b, t) + 1)
                    if old(b, t, 2):
                        act.wait_ge(t_ps, no(b, t) - 1)
                    act.activation(z[:, t % 2], y[:, t % 2], ACT.Identity, bias=shift[:, t % 2:t % 2 + 1],
                                   scale=rstd[:, t % 2:t % 2 + 1]).then_inc(z_done, 1)

                def z_high(b, t):
                    act.wait_ge(t_ps, no(b, t) + 1)
                    if old(b, t, 2):
                        act.wait_ge(ff_ps, no(b, t) - 1)
                    act.activation(zh[:, t % 2], psT[t % 2][:], ACT.Copy).then_inc(z_hi, 1)

                def store(b, t):
                    act.wait_ge(res_done, no(b, t) + 1)
                    act.dma_start(out[b].rearrange("(p n) c -> n p c", n=N2)[t], res[:, t % 2]).then_inc(out_stored[t % 2], 16)

                pipelined(act, B, N2, [(norm, 1), (o_high, 0), (z_high, 1), (store, 3)])
                for i in range(2):
                    act.wait_ge(out_stored[i], 16 * B * N2 // 2)

            @block.tensor
            def _(pe):
                pe.wait_ge(small_in, 16 * 10)
                pe.wait_ge(lo_split, 2)

                def conv(b, t):
                    pe.wait_ge(f_in[t % 2], 16 * (b * (N2 // 2) + t // 2 + 1))
                    if old(b, t, 2):
                        pe.wait_ge(a_done, no(b, t) - 1)
                    for ct in range(CT):
                        for j in range(2):
                            mm = pe.matmul(psC[t % 2][:, ct * P:(ct + 1) * P], fin[:, t % 2, j, ct * P:(ct + 1) * P],
                                           s4[:, j, t, :], start=(j == 0), stop=(j == 1))
                    mm.then_inc(c_ps, 1)

                def project(b, t):
                    pe.wait_ge(o_lo, no(b, t) + 1)
                    if old(b, t, 2):
                        pe.wait_ge(y_done, no(b, t) - 1)
                    for ct in range(CT):
                        mm = mm3(pe, psO[t % 2][:], oh[:, t % 2, ct * P:(ct + 1) * P], ol[:, t % 2, ct * P:(ct + 1) * P],
                                 woh[:, ct], wol[:, ct], ct == 0, ct == CT - 1)
                    mm.then_inc(o_ps, 1)

                def turn(b, t):
                    pe.wait_ge(z_done, no(b, t) + 1)
                    if old(b, t, 2):
                        pe.wait_ge(z_lo, no(b, t) - 1)
                    for ct in range(CT):
                        mm = pe.transpose(psT[t % 2][:, ct * P:(ct + 1) * P], z[:, t % 2, ct * P:(ct + 1) * P], ident[:])
                    mm.then_inc(t_ps, 1)

                def adapt(b, t):
                    pe.wait_ge(z_lo, no(b, t) + 1)
                    if old(b, t, 2):
                        pe.wait_ge(res_done, no(b, t) - 1)
                    for ct in range(CT):
                        mm = mm3(pe, psF[t % 2][:], zh[:, t % 2, ct * P:(ct + 1) * P], zl[:, t % 2, ct * P:(ct + 1) * P],
                                 wfh[:, ct], wfl[:, ct], ct == 0, ct == CT - 1)
                    mm.then_inc(ff_ps, 1)

                pipelined(pe, B, N2, [(project, 1), (conv, 0), (adapt, 2), (turn, 1)])

            @block.vector
            def _(dve):
                for k, (hi, lo) in enumerate(((woh, wol), (wfh, wfl))):
                    dve.wait_ge(hi_split, k + 1)
                    dve.tensor_tensor(lo[:], raw[:], hi[:].bitcast(F32), ALU.subtract).then_inc(lo_split, 1)

                def gate(b, t):
                    dve.wait_ge(corr_done, no(b, t) + 1)
                    dve.wait_ge(c_ps, no(b, t) + 1)
                    dve.tensor_tensor(corr[:, t % 2], psC[t % 2][:], corr[:, t % 2], ALU.add).then_inc(a_done, 1)
                    dve.wait_ge(a_done, no(b, t) + 1)
                    dve.wait_ge(g_in[t % 2], 16 * (b * (N2 // 2) + t // 2 + 1))
                    if old(b, t, 1):
                        dve.wait_ge(o_lo, no(b, t))
                    dve.tensor_tensor(o[:], corr[:, t % 2], gin[:, t % 2].rearrange("p c r -> p (c r)"),
                                      ALU.mult).then_inc(o_done, 1)

                def o_low(b, t):
                    dve.wait_ge(o_hi, no(b, t) + 1)
                    dve.tensor_tensor(ol[:, t % 2], o[:], oh[:, t % 2].bitcast(F32), ALU.subtract).then_inc(o_lo, 1)

                def residual(b, t):
                    dve.wait_ge(o_ps, no(b, t) + 1)
                    dve.wait_ge(xb_done, no(b, t) + 1)
                    if old(b, t, 2):
                        dve.wait_ge(yb_done, no(b, t) - 1)
                        dve.wait_ge(z_done, no(b, t) - 1)
                    dve.tensor_tensor(y[:, t % 2], psO[t % 2][:], xin[:, t % D], ALU.add).then_inc(y_done, 1)
                    dve.wait_ge(y_done, no(b, t) + 1)
                    dve.bn_stats(stats[:], y[:, t % 2]).then_inc(bn_step, 1)
                    dve.wait_ge(bn_step, no(b, t) + 1)
                    if old(b, t, 1):
                        dve.wait_ge(norm_ready, no(b, t))
                    dve.sem_inc(passed, 1)
                    dve.bn_aggr(mv[:], stats[:]).then_inc(mv_done, 1)

                def z_low(b, t):
                    dve.wait_ge(z_hi, no(b, t) + 1)
                    dve.tensor_tensor(zl[:, t % 2], psT[t % 2][:], zh[:, t % 2].bitcast(F32), ALU.subtract).then_inc(z_lo, 1)

                def finish(b, t):
                    dve.wait_ge(ff_ps, no(b, t) + 1)
                    dve.wait_ge(yb_done, no(b, t) + 1)
                    if old(b, t, 2):
                        dve.wait_ge(out_stored[t % 2], 16 * (b * (N2 // 2) + t // 2))
                    dve.tensor_tensor(res[:, t % 2], psF[t % 2][:], yb[:, t % 2], ALU.add).then_inc(res_done, 1)

                pipelined(dve, B, N2, [(residual, 1), (gate, 0), (o_low, 0), (finish, 2), (z_low, 1)])

    prep()
    front()
    middle()
    back()


_INS = ['L0_attn_x', 'L0_attn_in_proj_w', 'L0_attn_in_proj_b', 'L0_attn_short_w', 'L0_attn_short_b', 'L0_attn_fw1',
        'L0_attn_fb1', 'L0_attn_fw2', 'L0_attn_fb2', 'L0_attn_fw3', 'L0_attn_fb3', 'L0_attn_out_w', 'L0_attn_out_b',
        'L0_ffn_W', 'L0_ffn_b', 'L0_ffn_ids', 'L0_ffn_weights']


def kernel(**inputs):
    import concourse.bacc as _bacc
    from concourse.bass_utils import run_bass_kernel_spmd as _run

    nc = _bacc.Bacc("TRN2", target_bir_lowering=False, num_devices=1)
    arrays, args, consts = {}, [], {}
    for name in _INS:
        a = np.ascontiguousarray(inputs[name])
        arrays[f"in_{name}_dram"] = a
        args.append(nc.dram_tensor(f"in_{name}_dram", a.shape, mybir.dt.from_np(a.dtype), kind="ExternalInput").ap())
    for name, a in stage_matrices().items():
        a = np.ascontiguousarray(a)
        arrays[f"const_{name}_dram"] = a
        consts[name] = nc.dram_tensor(f"const_{name}_dram", a.shape, mybir.dt.from_np(a.dtype), kind="ExternalInput").ap()
    out = nc.dram_tensor("out_0_dram", (B, L, C), F32, kind="ExternalOutput").ap()
    hyena_adapter_kernel(nc, *args, consts, out)
    r = _run(nc, [arrays], core_ids=[0])
    return r.results[0]["out_0_dram"]
```

```python
from contextlib import ExitStack

import numpy as np

import concourse.bass as bass
from concourse import mybir

F32 = mybir.dt.float32
F32R = mybir.dt.float32r
I32 = mybir.dt.int32
ALU = mybir.AluOpType
ACT = mybir.ActivationFunctionType

P = 128
B = 8
L = 2048
C = 512
CT = C // P
N1H = P
N2 = L // N1H
N = 2 * L
SLOTS = P
ROWS = 2 * SLOTS
KG = 4
GROUPS = SLOTS // KG
GB = B + 1
NIDS = 8
NADAPT = 32
EPS = 1e-5
SUB = 4


def stage_matrices():
    n1 = np.arange(N1H)[:, None, None]
    n2 = np.arange(N2)[None, :, None]
    k1 = np.arange(SLOTS)[None, None, :]
    n = n1 * N2 + n2
    ang = 2 * np.pi * ((n * k1) % N) / N
    sign = np.where(n1[:, :, 0] % 2 == 0, 1.0, -1.0)
    s1 = np.zeros((N1H, N2, SLOTS, 2))
    s1[..., 0] = np.cos(ang)
    s1[..., 1] = -np.sin(ang)
    s1[:, :, 0, 0] = 1.0
    s1[:, :, 0, 1] = sign
    s1x = np.zeros((1, SLOTS, 2))
    ax = 2 * np.pi * (((N - 1) * np.arange(SLOTS)) % N) / N
    s1x[0, :, 0] = np.cos(ax)
    s1x[0, :, 1] = -np.sin(ax)
    s1x[0, 0] = [1.0, -1.0]
    s4 = np.zeros((SLOTS, 2, N2, N1H))
    a4 = ang.transpose(2, 1, 0)
    s4[:, 0] = 2 * np.cos(a4) / N
    s4[:, 1] = -2 * np.sin(a4) / N
    s4[0, 0] = 1.0 / N
    s4[0, 1] = sign.T / N

    m = np.arange(N2)
    a = 2 * np.pi * ((m[:, None] * m[None, :]) % N2) / N2
    c, s = np.cos(a), np.sin(a)
    fwd = np.zeros((2, N2, 2, N2))
    fwd[0, :, 0], fwd[1, :, 0] = c, s
    fwd[0, :, 1], fwd[1, :, 1] = -s, c
    inv = np.zeros((2, N2, 2, N2))
    inv[0, :, 0], inv[1, :, 0] = c, -s
    inv[0, :, 1], inv[1, :, 1] = s, c
    half = N2 // 2
    fsp = np.zeros((2, N2, 2, N2))
    isp = np.zeros((2, N2, 2, N2))
    fsp[0, :, 0, 0] = 1.0
    fsp[0, :, 1, 0] = (-1.0) ** m
    isp[0, 0, 0, :] = 1.0
    isp[1, 0, 0, :] = (-1.0) ** m
    for k in range(1, half):
        fsp[0, :, 0, k], fsp[0, :, 1, k] = c[:, k], -s[:, k]
        isp[0, k, 0, :], isp[1, k, 0, :] = 2 * c[:, k], -2 * s[:, k]
    for k in range(half):
        b = 2 * np.pi * m * (k + 0.5) / N2
        fsp[1, :, 0, half + k], fsp[1, :, 1, half + k] = np.cos(b), -np.sin(b)
        isp[0, half + k, 1, :], isp[1, half + k, 1, :] = 2 * np.cos(b), -2 * np.sin(b)

    def same(f):
        out = np.zeros_like(f)
        out[:, :, 0] = out[:, :, 1] = f[:, :, 0]
        return out

    def cross(f):
        out = np.zeros_like(f)
        out[:, :, 0], out[:, :, 1] = -f[:, :, 1], f[:, :, 1]
        return out

    same_sp, cross_sp = same(fsp), cross(fsp)
    same_sp[:, :, 1, 0] = fsp[:, :, 1, 0]
    cross_sp[:, :, :, 0] = 0.0

    def tile(first, rest):
        out = np.zeros((2, KG, N2, 2, KG, N2))
        for g in range(KG):
            out[:, g, :, :, g, :] = first if g == 0 else rest
        return out.reshape(P, P)

    kinds = [(fwd, fsp), (same(fwd), same_sp), (cross(fwd), cross_sp), (inv, isp)]
    mid = np.stack([tile(sp, g) for g, sp in kinds] + [tile(g, g) for g, sp in kinds], axis=1)
    return {
        "pos": np.linspace(0.0, 1.0, L).astype(np.float32).reshape(1, L),
        "s1": in_groups(s1.reshape(N1H, N2, ROWS), 2).astype(np.float32),
        "s1x": in_groups(s1x.reshape(1, ROWS), 1).astype(np.float32),
        "s4": in_groups(s4.reshape(ROWS, N2, N1H), 0).astype(np.float32),
        "mid": mid.astype(np.float32),
        "ident": np.eye(P, dtype=np.float32),
    }


def in_groups(a, axis):
    shape = a.shape
    a = a.reshape(shape[:axis] + (GROUPS, KG, 2) + shape[axis + 1:])
    return np.ascontiguousarray(a.swapaxes(axis + 1, axis + 2)).reshape(shape)


def pipelined(eng, outer, tiles, stages):
    fill = max(lag for _, lag in stages)

    def step(i, s, last):
        for stage, lag in stages:
            t = s - lag
            if t >= tiles and not last:
                stage(i + 1, t - tiles)
            elif 0 <= t < tiles:
                stage(i, t)

    for s in range(fill):
        step(0, s, False)

    def one_pass(i, last):
        for s in range(fill, tiles + fill):
            step(i, s, last)

    one_pass(0, False)
    with eng.Fori(1, outer - 1) as i:
        one_pass(i, False)
    one_pass(outer - 1, True)


def old(b, t, n):
    return not (isinstance(b, int) and b * N2 + t < n)


def hyena_adapter_kernel(nc, x, in_w, in_b, short_w, short_b, fw1, fb1, fw2, fb2, fw3, fb3,
                         out_w, out_b, w_ad, b_ad, ids, weights, consts, out):
    ctx = ExitStack()
    spec1 = nc.dram_tensor("spec1", [GB, ROWS * N2, C], F32, kind="Internal").ap()
    spec3 = nc.dram_tensor("spec3", [B, ROWS * N2, C], F32, kind="Internal").ap()
    gate_t = nc.dram_tensor("gate_t", [B, N2, P, C], F32, kind="Internal").ap()
    first_v = nc.dram_tensor("first_v", [B, C], F32, kind="Internal").ap()
    edge_f = nc.dram_tensor("edge_f", [2, P, N2 * C], F32, kind="Internal").ap()
    ad_mix = nc.dram_tensor("ad_mix", [P, CT, C], F32, kind="Internal").ap()
    ad_bias = nc.dram_tensor("ad_bias", [P, C], F32, kind="Internal").ap()

    def sem(name):
        return ctx.enter_context(nc.semaphore(name))

    def mm3(pe, out_ps, w_hi, w_lo, d_hi, d_lo, first, last):
        pe.matmul(out_ps, w_hi, d_hi, start=first, stop=False)
        pe.matmul(out_ps, w_hi, d_lo, start=False, stop=False)
        return pe.matmul(out_ps, w_lo, d_hi, start=False, stop=last)

    def prep():
        with ExitStack() as st:
            def sb(name, shape, dt=F32):
                return st.enter_context(nc.sbuf_tensor(name, shape, dt))

            def ps(name):
                return st.enter_context(nc.psum_tensor(name, [P, C], F32))

            LP = L + 2
            TQ = L // C
            pos = sb("pos", [64, L])
            w1c = sb("w1c", [64, 1])
            b1c = sb("b1c", [64, 1])
            w2s = sb("w2s", [64, P])
            b2c = sb("b2c", [P, 1])
            w3 = sb("w3", [P, 2 * C])
            w3s = sb("w3s", [P, C])
            b3r = sb("b3r", [1, 2 * C])
            b3s = sb("b3s", [1, C])
            b3c = sb("b3c", [P, CT])
            tapr = sb("tapr", [P, 3 * C])
            tapc = sb("tapc", [P, CT, 3])
            minus_w2 = sb("minus_w2", [P, CT])
            sbc = sb("sbc", [P, CT])
            h1 = sb("h1", [64, L])
            h2 = sb("h2", [P, LP])
            inside = sb("inside", [1, LP])
            H = sb("H", [P, N2 + 2, C])
            g = sb("g", [P, 2, C])
            gx = sb("gx", [P, 2, C])
            gy = sb("gy", [P, 2, C])
            g_before = sb("g_before", [1, C])
            s1 = sb("ps1", [P, N2, ROWS])
            s1x = sb("ps1x", [1, ROWS])
            s1o = sb("s1o", [P, 2, 2, C])
            ht = sb("ht", [P, L + 1])
            cum = sb("cum", [P, L])
            ones = sb("ones", [P, L])
            edge = sb("edge", [P, N2, P])
            edge2 = sb("edge2", [P, N2, P])
            pA = [ps("pA0"), ps("pA1")]
            pT = [ps("pT0"), ps("pT1")]
            pB = [ps(f"pB{i}") for i in range(4)]

            net_in = sem("p_net_in")
            taps_in = sem("p_taps_in")
            mats_in = sem("p_mats_in")
            cols_in = sem("p_cols_in")
            zeroed = sem("p_zeroed")
            h1_done = sem("p_h1_done")
            h2_ps = sem("p_h2_ps")
            h2_done = sem("p_h2_done")
            sliced = sem("p_sliced")
            H_ps = sem("p_H_ps")
            H_done = sem("p_H_done")
            tap0 = sem("p_tap0")
            tap1 = sem("p_tap1")
            tap2 = sem("p_tap2")
            tap01 = sem("p_tap01")
            g_done = sem("p_g_done")
            before_done = sem("p_before_done")
            s1_ps = sem("p_s1_ps")
            s1_out = sem("p_s1_out")
            s1_stored = [sem(f"p_s1_stored{i}") for i in range(2)]
            ht_ps = sem("p_ht_ps")
            ht_done = sem("p_ht_done")
            neg_done = sem("p_neg_done")
            cum_done = sem("p_cum_done")
            edge_done = sem("p_edge_done")
            edge_stored = sem("p_edge_stored")

            block = st.enter_context(nc.Block())

            @block.sync
            def _(sp):
                sp.dma_start(pos[:], consts["pos"].partition_broadcast(64)).then_inc(net_in, 16)
                sp.dma_start(w1c[:], fw1.rearrange("a (p b) -> p (a b)", b=1)).then_inc(net_in, 16)
                sp.dma_start(b1c[:], fb1.rearrange("(p b) -> p b", b=1)).then_inc(net_in, 16)
                sp.dma_start(w2s[:], fw2).then_inc(net_in, 16)
                sp.dma_start(b2c[:], fb2.rearrange("(p b) -> p b", b=1)).then_inc(net_in, 16)
                sp.dma_start(w3[:], fw3).then_inc(net_in, 16)
                sp.dma_start(b3r[:], fb3.rearrange("(a n) -> a n", a=1)).then_inc(net_in, 16)
                sp.dma_start(tapr[:], short_w.rearrange("(o c) a w -> o (c a w)", o=1).partition_broadcast(P)).then_inc(taps_in, 16)
                sp.dma_start(s1[:], consts["s1"]).then_inc(mats_in, 16)
                sp.dma_start(s1x[:], consts["s1x"]).then_inc(mats_in, 16)
                with nc.allow_non_contiguous_dma(reason="words of bias and taps by channel, once"):
                    sp.dma_start(b3c[:], fb3.rearrange("(c p two) -> p c two", p=P, two=2)[:, :, 1]).then_inc(cols_in, 16)
                    sp.dma_start(tapc[:], short_w.rearrange("(c p) a w -> p c (a w)", p=P)).then_inc(cols_in, 16)
                    sp.dma_start(sbc[:], short_b.rearrange("(c p) -> p c", p=P)).then_inc(cols_in, 16)
                for n2 in range(N2):
                    sp.wait_ge(s1_out, 2 * n2 + 2)
                    for j in range(2):
                        sp.dma_start(spec1[B].rearrange("(j p n) c -> n p j c", j=2, n=N2)[n2][:, j, :],
                                     s1o[:, n2 % 2, j, :]).then_inc(s1_stored[n2 % 2], 16)
                for i in range(2):
                    sp.wait_ge(s1_stored[i], 16 * N2)
                for ct in range(CT):
                    sp.wait_ge(edge_done, 2 * ct + 2)
                    for q, buf in ((0, edge), (1, edge2)):
                        sp.dma_start(edge_f[q].rearrange("p (n c r) -> c p n r", n=N2, c=CT)[ct], buf[:]).then_inc(edge_stored, 16)
                sp.wait_ge(edge_stored, 32 * CT)

            @block.gpsimd
            def _(pool):
                pool.memset(inside[:], 1.0).then_inc(zeroed, 1)
                pool.memset(h2[:, 0:1], 0.0).then_inc(zeroed, 1)
                pool.memset(h2[:, LP - 1:LP], 0.0).then_inc(zeroed, 1)
                pool.memset(ht[:, L:L + 1], 0.0).then_inc(zeroed, 1)
                pool.memset(ones[:], 1.0).then_inc(zeroed, 1)
                pool.wait_ge(zeroed, 5)
                pool.memset(inside[:, 0:1], 0.0).then_inc(zeroed, 1)
                pool.memset(inside[:, LP - 1:LP], 0.0).then_inc(zeroed, 1)
                tap = tapr[:].rearrange("p (c w) -> p w c", w=3)
                pool.wait_ge(taps_in, 16)
                for n2 in range(N2):
                    pool.wait_ge(H_done, n2 + 3)
                    if n2 >= 2:
                        pool.wait_ge(g_done, n2 - 1)
                    pool.tensor_tensor(gy[:, n2 % 2], H[:, n2 + 2], tap[:, 2], ALU.mult).then_inc(tap2, 1)

            @block.scalar
            def _(act):
                act.wait_ge(net_in, 16 * 7)
                act.activation(h1[:], pos[:], ACT.Gelu, bias=b1c[:], scale=w1c[:]).then_inc(h1_done, 1)
                for q in range(TQ):
                    act.wait_ge(h2_ps, q + 1)
                    act.activation(h2[:, 1 + q * C:1 + (q + 1) * C], pA[q % 2][:], ACT.Gelu, bias=b2c[:]).then_inc(h2_done, 1)

                def s1_copy(n2):
                    for j in range(2):
                        act.wait_ge(s1_ps, 2 * n2 + j + 1)
                        if n2 >= 2:
                            act.wait_ge(s1_stored[n2 % 2], 32 * (n2 // 2))
                        act.activation(s1o[:, n2 % 2, j, :], pB[2 * (n2 % 2) + j][:], ACT.Copy).then_inc(s1_out, 1)

                for e in range(N2 + 4):
                    if e < N2 + 2:
                        act.wait_ge(H_ps, e + 1)
                        act.activation(H[:, e, :], pA[e % 2][:], ACT.Copy).then_inc(H_done, 1)
                    if e >= 4:
                        s1_copy(e - 4)
                act.wait_ge(cols_in, 48)
                act.activation(minus_w2[:], tapc[:, :, 2], ACT.Copy, scale=-1.0).then_inc(neg_done, 1)
                act.wait_ge(neg_done, 1)
                for ct in range(CT):
                    if ct >= 1:
                        act.wait_ge(cum_done, ct)
                        act.wait_ge(edge_done, 2 * ct)
                    for q in range(TQ):
                        act.wait_ge(ht_ps, ct * TQ + q + 1)
                        act.activation(ht[:, q * C:(q + 1) * C], pT[q % 2][:], ACT.Identity,
                                       bias=b3c[:, ct:ct + 1]).then_inc(ht_done, 1)
                    act.wait_ge(ht_done, (ct + 1) * TQ)
                    act.wait_ge(zeroed, 7)
                    if ct >= 1:
                        act.wait_ge(edge_stored, 32 * ct)
                    act.activation(edge[:], ht[:, 1:L + 1].rearrange("p (r n) -> p n r", n=N2), ACT.Copy,
                                   scale=minus_w2[:, ct:ct + 1]).then_inc(edge_done, 1)
                    act.wait_ge(cum_done, ct + 1)
                    act.activation(edge2[:], cum[:].rearrange("p (r n) -> p n r", n=N2), ACT.Copy,
                                   scale=sbc[:, ct:ct + 1]).then_inc(edge_done, 1)

            @block.tensor
            def _(pe):
                pe.wait_ge(net_in, 16 * 7)
                pe.wait_ge(h1_done, 1)
                for q in range(TQ):
                    if q >= 2:
                        pe.wait_ge(h2_done, q - 1)
                    pe.matmul(pA[q % 2][:], w2s[:], h1[:, q * C:(q + 1) * C], start=True, stop=True).then_inc(h2_ps, 1)
                pe.wait_ge(h2_done, TQ)
                pe.wait_ge(sliced, 2)
                pe.wait_ge(zeroed, 7)

                def stage1(n2):
                    edge_row = n2 == N2 - 1
                    pe.wait_ge(g_done, n2 + 1)
                    for j in range(2):
                        bank = pB[2 * (n2 % 2) + j]
                        if n2 >= 2:
                            pe.wait_ge(s1_out, 2 * (n2 - 1))
                        mm = pe.matmul(bank[:], s1[:, n2, j * P:(j + 1) * P], g[:, n2 % 2, :], start=True, stop=not edge_row)
                        if edge_row:
                            pe.wait_ge(before_done, 1)
                            mm = pe.matmul(bank[:], s1x[:, j * P:(j + 1) * P], g_before[:], start=False, stop=True)
                        mm.then_inc(s1_ps, 1)

                for e in range(N2 + 4):
                    if e < N2 + 2:
                        if e >= 2:
                            pe.wait_ge(H_done, e - 1)
                        cols = slice(e, e + (N1H - 1) * N2 + 1, N2)
                        pe.matmul(pA[e % 2][:], h2[:, cols], w3s[:], start=True, stop=False)
                        pe.matmul(pA[e % 2][:], inside[:, cols], b3s[:], start=False, stop=True).then_inc(H_ps, 1)
                    if e == 4:
                        pe.wait_ge(mats_in, 32)
                    if e >= 4:
                        stage1(e - 4)
                for ct in range(CT):
                    for q in range(TQ):
                        n = ct * TQ + q
                        if n >= 2:
                            pe.wait_ge(ht_done, n - 1)
                        pe.matmul(pT[q % 2][:], w3s[:, ct * P:(ct + 1) * P], h2[:, 1 + q * C:1 + (q + 1) * C],
                                  start=True, stop=True).then_inc(ht_ps, 1)

            @block.vector
            def _(dve):
                dve.wait_ge(net_in, 16 * 7)
                dve.tensor_copy(w3s[:], w3[:].rearrange("p (c two) -> p c two", two=2)[:, :, 1]).then_inc(sliced, 1)
                dve.tensor_copy(b3s[:], b3r[:].rearrange("p (c two) -> p c two", two=2)[:, :, 1]).then_inc(sliced, 1)
                dve.wait_ge(taps_in, 16)
                tap = tapr[:].rearrange("p (c w) -> p w c", w=3)
                for n2 in range(N2):
                    k = n2 % 2
                    dve.wait_ge(H_done, n2 + 2)
                    if n2 >= 2:
                        dve.wait_ge(s1_ps, 2 * (n2 - 1))
                    dve.tensor_tensor(g[:, k], H[:, n2], tap[:, 0], ALU.mult).then_inc(tap0, 1)
                    if n2 >= 2:
                        dve.wait_ge(tap01, n2 - 1)
                    dve.tensor_tensor(gx[:, k], H[:, n2 + 1], tap[:, 1], ALU.mult).then_inc(tap1, 1)
                    dve.wait_ge(tap0, n2 + 1)
                    dve.wait_ge(tap1, n2 + 1)
                    dve.tensor_tensor(gx[:, k], g[:, k], gx[:, k], ALU.add).then_inc(tap01, 1)
                    dve.wait_ge(tap01, n2 + 1)
                    dve.wait_ge(tap2, n2 + 1)
                    dve.tensor_tensor(g[:, k], gx[:, k], gy[:, k], ALU.add).then_inc(g_done, 1)
                    if n2 == 0:
                        dve.tensor_tensor(g_before[:], H[0:1, 1, :], tap[0:1, 2, :], ALU.mult).then_inc(before_done, 1)
                dve.wait_ge(zeroed, 7)
                for ct in range(CT):
                    dve.wait_ge(ht_done, (ct + 1) * TQ)
                    if ct >= 1:
                        dve.wait_ge(edge_done, 2 * ct)
                    dve.tensor_tensor_scan(cum[:], ones[:], ht[:, 0:L], 0.0, ALU.mult, ALU.add).then_inc(cum_done, 1)

    def front():
        with ExitStack() as st:
            def sb(name, shape, dt=F32):
                return st.enter_context(nc.sbuf_tensor(name, shape, dt))

            def ps(name):
                return st.enter_context(nc.psum_tensor(name, [P, C], F32))

            s1h = sb("s1h", [P, N2, ROWS], F32R)
            s1l = sb("s1l", [P, N2, ROWS], F32R)
            wvh = sb("wvh", [P, CT, C], F32R)
            wvl = sb("wvl", [P, CT, C], F32R)
            wgh = sb("wgh", [P, CT, C], F32R)
            wgl = sb("wgl", [P, CT, C], F32R)
            ident = sb("fident", [P, P])
            bv3 = sb("bv3", [P, 3 * C])
            bvr = bv3[:].rearrange("p (c w) -> p w c", w=3)[:, 0, :]
            bgc = sb("bgc", [P, CT])
            xg = sb("xg", [P, 2, SUB, C])
            stats = sb("fstats", [P, 2, SUB, 6])
            mv = sb("fmv", [P, 2, SUB, 2])
            rstd = sb("frstd", [P, 2, SUB])
            shift = sb("fshift", [P, 2, SUB])
            power = sb("fpower", [P, SUB])
            eps = sb("feps", [P, SUB])
            minus = sb("fminus", [P, SUB])
            xn = sb("xn", [P, 2, C])
            nth = sb("nth", [P, 2, CT, SUB * P], F32R)
            ntl = sb("ntl", [P, 2, CT, SUB * P], F32R)
            v = sb("v", [P, 2, C])
            vh = sb("vh", [P, 2, C], F32R)
            vl = sb("vl", [P, 2, C], F32R)
            s1o = sb("fs1o", [P, 2, 2, SUB, C])
            gto = sb("gto", [P, 2, SUB, CT, P])
            raw = s1o[:].rearrange("p a b c d -> p (a b c d)")[:, 0:CT * 3 * C]
            raw_s1 = gto[:].rearrange("p a n c r -> p (a n c r)")
            ad_load = sb("ad_load", [P, CT, C])
            ad_sum = sb("ad_sum", [P, CT, C])
            adb_load = sb("adb_load", [P, C])
            adb_sum = sb("adb_sum", [P, C])
            wgt = sb("wgt", [P, NIDS])
            idst = sb("idst", [1, NIDS], I32)
            psT = [ps("psT0"), ps("psT1")]
            psV = [ps("psV0"), ps("psV1")]
            psS = [ps("psS0"), ps("psS1")]
            psX = [ps("psX0"), ps("psX1")]

            w_in = sem("f_w_in")
            s1_in = sem("f_s1_in")
            ids_in = sem("f_ids_in")
            ad_in = sem("f_ad_in")
            ad_clear = sem("f_ad_clear")
            ad_used = sem("f_ad_used")
            ad_stored = sem("f_ad_stored")
            w_split = sem("f_w_split")
            power_set = sem("f_power_set")
            passed = sem("f_passed")
            passed_sp = sem("f_passed_sp")
            hi_split = sem("f_hi_split")
            small_in = sem("f_small_in")
            x_in = [sem(f"f_x_in{i}") for i in range(2)]
            x_free = sem("f_x_free")
            bn_step = sem("f_bn_step")
            mv_done = sem("f_mv_done")
            pow_step = sem("f_pow_step")
            norm_ready = sem("f_norm_ready")
            xn_done = sem("f_xn_done")
            t_ps = sem("f_t_ps")
            nt_hi = sem("f_nt_hi")
            nt_lo = sem("f_nt_lo")
            v_ps = sem("f_v_ps")
            v_done = sem("f_v_done")
            v0_out = sem("f_v0_out")
            v_hi = sem("f_v_hi")
            v_lo = sem("f_v_lo")
            s_ps = sem("f_s_ps")
            s_out0 = sem("f_s_out0")
            s_out1 = sem("f_s_out1")
            s_stored = [sem(f"f_s_stored{i}") for i in range(2)]
            x2_ps = sem("f_x2_ps")
            x2_out = sem("f_x2_out")
            x2_stored = [sem(f"f_x2_stored{i}") for i in range(2)]

            block = st.enter_context(nc.Block())
            Q = N2 // SUB
            MIX = CT + 1

            def tile_no(b, t):
                return b * N2 + t

            def group_no(b, t):
                return b * Q + t // SUB

            @block.sync
            def _(sp):
                W3 = 3 * C
                for kt in range(CT):
                    sp.dma_start(raw[:, kt * W3:(kt + 1) * W3], in_w[kt * P:(kt + 1) * P, :]).then_inc(w_in, 16)
                sp.dma_start(bv3[:], in_b.rearrange("(a c) -> a c", a=1).partition_broadcast(P)).then_inc(small_in, 16)
                with nc.allow_non_contiguous_dma(reason="512 words of bias, once"):
                    sp.dma_start(bgc[:], in_b.rearrange("(c p w) -> p c w", p=P, w=3)[:, :, 2]).then_inc(small_in, 16)
                sp.dma_start(ident[:], consts["ident"]).then_inc(small_in, 16)
                sp.dma_start(raw_s1, consts["s1"].rearrange("p n r -> p (n r)")).then_inc(s1_in, 16)
                sp.dma_start(wgt[:], weights.rearrange("(a n) -> a n", a=1).partition_broadcast(P)).then_inc(ids_in, 16)
                sp.dma_start(idst[:], ids.rearrange("(a n) -> a n", a=1)).then_inc(ids_in, 16)
                sp.wait_ge(ids_in, 32)

                def load_adapter(b, t):
                    if t != 1:
                        return
                    which = sp.value_load(idst[0:1, b:b + 1] if isinstance(b, int) else idst[0:1, bass.ds(b, 1)],
                                          min_val=0, max_val=NADAPT - 1)
                    if old(b, t, N2):
                        sp.wait_ge(ad_used, MIX * b)
                    sp.dma_start(ad_load[:], w_ad[bass.ds(which, 1)].rearrange("a (t p) d -> (a p) t d", p=P)).then_inc(ad_in, 16)
                    sp.dma_start(adb_load[:], b_ad[bass.ds(which, 1)].partition_broadcast(P)).then_inc(ad_in, 16)

                def load_x(b, t):
                    if t % SUB:
                        return
                    slot = (t // SUB) % 2
                    sp.wait_ge(x_free, group_no(b, t) + 1)
                    sp.dma_start(xg[:, slot], x[b].rearrange("(p n) c -> p n c", n=N2)[:, t:t + SUB, :]).then_inc(x_in[slot], 16)

                def save_v0(b, t):
                    if t == 0:
                        sp.wait_ge(v_done, tile_no(b, 0) + 1)
                        sp.dma_start(first_v[b].rearrange("(a c) -> a c", a=1), v[0:1, 0, :]).then_inc(v0_out, 16)

                def store(b, t):
                    if t % SUB != SUB - 1:
                        return
                    slot = (t // SUB) % 2
                    sp.wait_ge(s_out0, tile_no(b, t) + 1)
                    sp.wait_ge(s_out1, tile_no(b, t) + 1)
                    for j in range(2):
                        sp.dma_start(spec1[b].rearrange("(j p n) c -> j p n c", j=2, n=N2)[j, :, t - SUB + 1:t + 1, :],
                                     s1o[:, slot, j]).then_inc(s_stored[slot], 16)

                def store_x2(b, t):
                    if t % SUB != SUB - 1:
                        return
                    slot = (t // SUB) % 2
                    sp.wait_ge(x2_out, tile_no(b, t) + 1)
                    sp.sem_inc(passed_sp, 1)
                    sp.dma_start(gate_t[b].rearrange("n p c -> p n c")[:, t - SUB + 1:t + 1, :],
                                 gto[:, slot].rearrange("p n c r -> p n (c r)")).then_inc(x2_stored[slot], 16)

                pipelined(sp, B, N2, [(load_x, 0), (save_v0, 4), (load_adapter, 5), (store, 8), (store_x2, 10)])
                sp.wait_ge(ad_used, MIX * B)
                sp.dma_start(ad_mix, ad_sum[:]).then_inc(ad_stored, 16)
                sp.dma_start(ad_bias, adb_sum[:]).then_inc(ad_stored, 16)
                sp.wait_ge(ad_stored, 32)
                for slot in range(2):
                    sp.wait_ge(s_stored[slot], 16 * 2 * B * Q // 2)
                    sp.wait_ge(x2_stored[slot], 16 * B * Q // 2)
                sp.wait_ge(v0_out, 16 * B)

            @block.scalar
            def _(act):
                wraw = raw.rearrange("p (k c w) -> p k c w", k=CT, w=3)
                act.wait_ge(w_in, 16 * CT)
                act.activation(wvh[:], wraw[:, :, :, 0], ACT.Copy).then_inc(hi_split, 1)
                act.activation(wgh[:], wraw[:, :, :, 2], ACT.Copy).then_inc(hi_split, 1)
                act.wait_ge(s1_in, 16)
                act.activation(s1h[:].rearrange("p n r -> p (n r)"), raw_s1, ACT.Copy).then_inc(hi_split, 1)
                act.wait_ge(small_in, 48)

                def norm(b, t):
                    slot = (t // SUB) % 2
                    act.wait_ge(norm_ready, group_no(b, t) + 1)
                    if old(b, t, 2):
                        act.wait_ge(t_ps, tile_no(b, t) - 1)
                    op = act.activation(xn[:, t % 2], xg[:, slot, t % SUB], ACT.Identity,
                                        bias=shift[:, slot, t % SUB:t % SUB + 1],
                                        scale=rstd[:, slot, t % SUB:t % SUB + 1])
                    op.then_inc(xn_done, 1)

                def nt_high(b, t):
                    g = (t // SUB) % 2
                    act.wait_ge(t_ps, tile_no(b, t) + 1)
                    if old(b, t, 2 * SUB):
                        act.wait_ge(x2_ps, (group_no(b, t) - 1) * SUB)
                    act.activation(nth[:, g, :, (t % SUB) * P:(t % SUB + 1) * P],
                                   psT[t % 2][:].rearrange("p (k r) -> p k r", k=CT), ACT.Copy).then_inc(nt_hi, 1)

                def v_high(b, t):
                    act.wait_ge(v_done, tile_no(b, t) + 1)
                    if old(b, t, 2):
                        act.wait_ge(s_ps, 2 * (tile_no(b, t) - 1))
                    act.activation(vh[:, t % 2], v[:, t % 2], ACT.Copy).then_inc(v_hi, 1)

                def s_copy(b, t):
                    slot = (t // SUB) % 2
                    act.wait_ge(s_ps, 2 * tile_no(b, t) + 1)
                    if t % SUB == 0 and old(b, t, 2 * SUB):
                        act.wait_ge(s_stored[slot], 32 * (b * (Q // 2) + t // (2 * SUB)))
                    act.activation(s1o[:, slot, 0, t % SUB], psS[0][:], ACT.Copy).then_inc(s_out0, 1)

                def x2_copy(b, t):
                    slot, ct = (t // SUB) % 2, t % SUB
                    act.wait_ge(x2_ps, tile_no(b, t) + 1)
                    if ct == 0 and old(b, t, 2 * SUB):
                        act.wait_ge(x2_stored[slot], 16 * (b * (Q // 2) + t // (2 * SUB)))
                    act.activation(gto[:, slot, :, ct, :], psX[ct % 2][:].rearrange("p (n r) -> p n r", n=SUB),
                                   ACT.Identity, bias=bgc[:, ct:ct + 1]).then_inc(x2_out, 1)

                pipelined(act, B, N2, [(nt_high, 2), (v_high, 3), (norm, 1), (x2_copy, 6), (s_copy, 4)])

            @block.gpsimd
            def _(pool):
                pool.memset(power[:], -0.5).then_inc(power_set, 1)
                pool.memset(eps[:], EPS).then_inc(power_set, 1)
                pool.memset(minus[:], -1.0).then_inc(power_set, 1)
                pool.memset(ad_sum[:], 0.0).then_inc(ad_clear, 1)
                pool.memset(adb_sum[:], 0.0).then_inc(ad_clear, 1)
                pool.wait_ge(w_split, 3)
                pool.wait_ge(power_set, 3)

                def scalars(b, t):
                    if t % SUB:
                        return
                    slot = (t // SUB) % 2
                    n = group_no(b, t)
                    pool.wait_ge(mv_done, (n + 1) * SUB)
                    if old(b, t, 2 * SUB):
                        pool.wait_ge(xn_done, (n - 1) * SUB)
                    pool.tensor_tensor(rstd[:, slot], mv[:, slot, :, 1], eps[:], ALU.add).then_inc(pow_step, 1)
                    pool.tensor_tensor(shift[:, slot], mv[:, slot, :, 0], minus[:], ALU.mult).then_inc(pow_step, 1)
                    pool.wait_ge(pow_step, 3 * n + 2)
                    pool.tensor_tensor(rstd[:, slot], rstd[:, slot], power[:], ALU.pow).then_inc(pow_step, 1)
                    pool.wait_ge(pow_step, 3 * n + 3)
                    pool.tensor_tensor(shift[:, slot], shift[:, slot], rstd[:, slot], ALU.mult).then_inc(norm_ready, 1)

                def v_low(b, t):
                    pool.wait_ge(v_hi, tile_no(b, t) + 1)
                    pool.tensor_tensor(vl[:, t % 2], v[:, t % 2], vh[:, t % 2].bitcast(F32), ALU.subtract).then_inc(v_lo, 1)

                pipelined(pool, B, N2, [(scalars, 0), (v_low, 3)])

            @block.tensor
            def _(pe):
                pe.wait_ge(w_split, 3)
                pe.wait_ge(small_in, 48)

                def turn(b, t):
                    pe.wait_ge(xn_done, tile_no(b, t) + 1)
                    if old(b, t, 2):
                        pe.wait_ge(nt_lo, tile_no(b, t) - 1)
                    for kt in range(CT):
                        mm = pe.transpose(psT[t % 2][:, kt * P:(kt + 1) * P], xn[:, t % 2, kt * P:(kt + 1) * P], ident[:])
                    mm.then_inc(t_ps, 1)

                def project_v(b, t):
                    g = (t // SUB) % 2
                    pe.wait_ge(nt_lo, tile_no(b, t) + 1)
                    if old(b, t, 2):
                        pe.wait_ge(v_done, tile_no(b, t) - 1)
                    cols = slice((t % SUB) * P, (t % SUB + 1) * P)
                    for kt in range(CT):
                        mm = mm3(pe, psV[t % 2][:], nth[:, g, kt, cols], ntl[:, g, kt, cols], wvh[:, kt], wvl[:, kt],
                                 kt == 0, kt == CT - 1)
                    mm.then_inc(v_ps, 1)

                def project_x2(b, t):
                    g, ct = (t // SUB) % 2, t % SUB
                    if old(b, t, 2):
                        pe.wait_ge(x2_out, tile_no(b, t) - 1)
                    for kt in range(CT):
                        mm = mm3(pe, psX[ct % 2][:], wgh[:, kt, ct * P:(ct + 1) * P], wgl[:, kt, ct * P:(ct + 1) * P],
                                 nth[:, g, kt], ntl[:, g, kt], kt == 0, kt == CT - 1)
                    mm.then_inc(x2_ps, 1)

                def stage1(b, t):
                    pe.wait_ge(v_lo, tile_no(b, t) + 1)
                    for j in range(2):
                        if old(b, t, 1):
                            pe.wait_ge((s_out0, s_out1)[j], tile_no(b, t))
                        mm = mm3(pe, psS[j][:], s1h[:, t, j * P:(j + 1) * P], s1l[:, t, j * P:(j + 1) * P],
                                 vh[:, t % 2], vl[:, t % 2], True, True)
                        mm.then_inc(s_ps, 1)

                pipelined(pe, B, N2, [(turn, 2), (project_v, 3), (project_x2, 6), (stage1, 4)])

            @block.vector
            def _(dve):
                wraw = raw.rearrange("p (k c w) -> p k c w", k=CT, w=3)
                dve.wait_ge(hi_split, 2)
                dve.tensor_tensor(wvl[:], wraw[:, :, :, 0], wvh[:].bitcast(F32), ALU.subtract).then_inc(w_split, 1)
                dve.tensor_tensor(wgl[:], wraw[:, :, :, 2], wgh[:].bitcast(F32), ALU.subtract).then_inc(w_split, 1)
                dve.wait_ge(hi_split, 3)
                dve.tensor_tensor(s1l[:].rearrange("p n r -> p (n r)"), raw_s1,
                                  s1h[:].rearrange("p n r -> p (n r)").bitcast(F32), ALU.subtract).then_inc(w_split, 1)
                dve.wait_ge(w_split, 3)
                dve.wait_ge(small_in, 48)
                dve.wait_ge(ids_in, 32)
                dve.sem_inc(x_free, 2)

                def moments(b, t):
                    if t % SUB:
                        return
                    slot = (t // SUB) % 2
                    n = group_no(b, t)
                    dve.wait_ge(x_in[slot], 16 * (b * (Q // 2) + t // (2 * SUB) + 1))
                    for i in range(SUB):
                        dve.bn_stats(stats[:, slot, i], xg[:, slot, i]).then_inc(bn_step, 1)
                    dve.wait_ge(bn_step, n * SUB + SUB)
                    if old(b, t, 2 * SUB):
                        dve.wait_ge(norm_ready, n - 1)
                    dve.sem_inc(passed, 1)
                    for i in range(SUB):
                        dve.bn_aggr(mv[:, slot, i], stats[:, slot, i]).then_inc(mv_done, 1)

                def nt_low(b, t):
                    g = (t // SUB) % 2
                    cols = slice((t % SUB) * P, (t % SUB + 1) * P)
                    dve.wait_ge(nt_hi, tile_no(b, t) + 1)
                    dve.tensor_tensor(ntl[:, g, :, cols], psT[t % 2][:].rearrange("p (k r) -> p k r", k=CT),
                                      nth[:, g, :, cols].bitcast(F32), ALU.subtract).then_inc(nt_lo, 1)
                    if t % SUB == SUB - 1:
                        dve.sem_inc(x_free, 1)

                def v_bias(b, t):
                    dve.wait_ge(v_ps, tile_no(b, t) + 1)
                    if old(b, t, 2):
                        dve.wait_ge(v_lo, tile_no(b, t) - 1)
                    if t == 2:
                        dve.wait_ge(v0_out, 16 * (b + 1))
                    dve.tensor_tensor(v[:, t % 2], psV[t % 2][:], bvr, ALU.add).then_inc(v_done, 1)

                def mix(b, t):
                    if t % SUB and t != 2:
                        return
                    k = 1 if t == 2 else t // SUB + (t > 2)
                    dve.wait_ge(ad_in, 32 * (b + 1))
                    dve.wait_ge(ad_clear, 2)
                    if old(b, t, 1):
                        dve.wait_ge(ad_used, MIX * b + k)
                    w = wgt[:, b:b + 1] if isinstance(b, int) else wgt[:, bass.ds(b, 1)]
                    src, dst = (adb_load[:], adb_sum[:]) if t == 2 else (ad_load[:, t // SUB], ad_sum[:, t // SUB])
                    dve.scalar_tensor_tensor(dst, src, w, dst, ALU.mult, ALU.add).then_inc(ad_used, 1)

                def s_copy(b, t):
                    slot = (t // SUB) % 2
                    dve.wait_ge(s_ps, 2 * tile_no(b, t) + 2)
                    if t % SUB == 0 and old(b, t, 2 * SUB):
                        dve.wait_ge(s_stored[slot], 32 * (b * (Q // 2) + t // (2 * SUB)))
                    dve.tensor_copy(s1o[:, slot, 1, t % SUB], psS[1][:]).then_inc(s_out1, 1)

                pipelined(dve, B, N2, [(nt_low, 2), (v_bias, 3), (moments, 0), (s_copy, 4), (mix, 8)])

    def middle():
        with ExitStack() as st:
            def sb(name, shape, dt=F32):
                return st.enter_context(nc.sbuf_tensor(name, shape, dt))

            def ps(name):
                return st.enter_context(nc.psum_tensor(name, [P, C], F32))

            R = 4
            mats = sb("mats", [P, 8, P])
            xin = sb("m_xin", [P, 2, GB, C])
            spec = sb("m_spec", [P, 2, 2, C])
            zs = sb("m_zs", [P, R, C])
            m1 = sb("m_m1", [P, R, C])
            m2 = sb("m_m2", [P, R, C])
            u = sb("m_u", [P, R, C])
            wo = sb("m_wo", [P, 2, B, C])
            psZ = [ps(f"m_psZ{i}") for i in range(R)]
            psF = [ps("m_psF0"), ps("m_psF1")]
            psW = [ps("m_psW0"), ps("m_psW1")]
            small_in = sem("m_small_in")
            x_in = [sem(f"m_x_in{i}") for i in range(2)]
            f_ps = sem("m_f_ps")
            f_done = sem("m_f_done")
            z_ps = sem("m_z_ps")
            zs_done = sem("m_zs_done")
            m1_done = sem("m_m1_done")
            m2_done = sem("m_m2_done")
            u_done = sem("m_u_done")
            w_ps = sem("m_w_ps")
            w_out = sem("m_w_out")
            stored = [sem(f"m_stored{i}") for i in range(2)]
            block = st.enter_context(nc.Block())

            T = 2 * GB

            def group(i, t):
                return i * 2 + t // GB

            def data_no(i, t):
                return group(i, t) * B + t % GB - 1

            def kind(m, i, t):
                first = isinstance(i, int) and i == 0 and t < GB
                return mats[:, m if first else m + 4, :]

            def rows_of(spec_dram, g):
                by_group = spec_dram.rearrange("b (g p) c -> g p b c", p=P)
                if isinstance(g, int):
                    return by_group[g]
                return by_group[bass.ds(g, 1)].rearrange("g p b c -> (g p) b c")

            def early(i, t, first_groups=2):
                return isinstance(i, int) and i == 0 and t // GB < first_groups

            @block.sync
            def _(sp):
                sp.dma_start(mats[:], consts["mid"]).then_inc(small_in, 16)

                def load(i, t):
                    if t % GB:
                        return
                    par = t // GB
                    if not early(i, t):
                        sp.wait_ge(z_ps, (group(i, t) - 1) * B)
                    sp.dma_start(xin[:, par], rows_of(spec1, group(i, t))).then_inc(x_in[par], 16)

                pipelined(sp, GROUPS // 2, T, [(load, 0)])

            @block.tensor
            def _(pe):
                pe.wait_ge(small_in, 16)

                def stage2(i, t):
                    par = t // GB
                    if t % GB == 0:
                        pe.wait_ge(x_in[par], 16 * (i + 1))
                        if not early(i, t, 1):
                            pe.wait_ge(f_done, 2 * group(i, t))
                        for m in (1, 2):
                            pe.matmul(psF[m - 1][:], kind(m, i, t), xin[:, par, B, :], start=True, stop=True).then_inc(f_ps, 1)
                        return
                    n = data_no(i, t)
                    if not (early(i, t, 1) and t <= R):
                        pe.wait_ge(zs_done, 2 * (n - 3))
                    pe.matmul(psZ[(t % GB - 1) % R][:], kind(0, i, t), xin[:, par, t % GB - 1, :],
                              start=True, stop=True).then_inc(z_ps, 1)

                def stage3(i, t):
                    if t % GB == 0:
                        return
                    n = data_no(i, t)
                    k = (t % GB - 1) % 2
                    pe.wait_ge(u_done, n + 1)
                    if not (early(i, t, 1) and t < 3):
                        pe.wait_ge(w_out, n - 1)
                    pe.matmul(psW[k][:], kind(3, i, t), u[:, (t % GB - 1) % R, :], start=True, stop=True).then_inc(w_ps, 1)

                pipelined(pe, GROUPS // 2, T, [(stage2, 0), (stage3, 4)])

            @block.scalar
            def _(act):
                def spectrum(i, t):
                    if t % GB:
                        return
                    par = t // GB
                    for m in range(2):
                        act.wait_ge(f_ps, 2 * group(i, t) + m + 1)
                        if m == 0 and not early(i, t):
                            act.wait_ge(u_done, (group(i, t) - 1) * B)
                        act.activation(spec[:, par, m, :], psF[m][:], ACT.Copy).then_inc(f_done, 1)

                def swap(i, t):
                    if t % GB == 0:
                        return
                    k = (t % GB - 1) % R
                    act.wait_ge(m1_done, data_no(i, t) + 1)
                    if not (early(i, t, 1) and t <= R):
                        act.wait_ge(m2_done, data_no(i, t) - R + 1)
                    for half in range(2):
                        act.activation(zs[(1 - half) * 64:(2 - half) * 64, k, :], psZ[(t % GB - 1) % R][half * 64:(half + 1) * 64, :],
                                       ACT.Copy).then_inc(zs_done, 1)

                def out_copy(i, t):
                    if t % GB == 0:
                        return
                    par, b = t // GB, t % GB - 1
                    act.wait_ge(w_ps, data_no(i, t) + 1)
                    if b == 0 and not early(i, t):
                        act.wait_ge(stored[par], 16 * i)
                    act.activation(wo[:, par, b, :], psW[b % 2][:], ACT.Copy).then_inc(w_out, 1)

                def store(i, t):
                    if t % GB != GB - 1:
                        return
                    par = t // GB
                    act.wait_ge(w_out, data_no(i, t) + 1)
                    act.dma_start(rows_of(spec3, group(i, t)), wo[:, par]).then_inc(stored[par], 16)

                pipelined(act, GROUPS // 2, T, [(spectrum, 0), (out_copy, 4), (swap, 0), (store, 5)])
                for par in range(2):
                    act.wait_ge(stored[par], 16 * GROUPS // 2)

            @block.gpsimd
            def _(pool):
                def cross_part(i, t):
                    if t % GB == 0:
                        return
                    par, b = t // GB, t % GB - 1
                    n = data_no(i, t)
                    if b == 0:
                        pool.wait_ge(f_done, 2 * group(i, t) + 2)
                    if not (early(i, t, 1) and b < R):
                        pool.wait_ge(u_done, n - R + 1)
                    pool.wait_ge(zs_done, 2 * n + 2)
                    pool.tensor_tensor(m2[:, b % R, :], zs[:, b % R, :], spec[:, par, 1, :], ALU.mult).then_inc(m2_done, 1)

                pipelined(pool, GROUPS // 2, T, [(cross_part, 0)])

            @block.vector
            def _(dve):
                def same_part(i, t):
                    if t % GB == 0:
                        return
                    par, b = t // GB, t % GB - 1
                    n = data_no(i, t)
                    dve.wait_ge(z_ps, n + 1)
                    if b == 0:
                        dve.wait_ge(f_done, 2 * group(i, t) + 2)
                    if not (early(i, t, 1) and b < R):
                        dve.wait_ge(u_done, n - R + 1)
                    dve.tensor_tensor(m1[:, b % R, :], psZ[b % R][:], spec[:, par, 0, :], ALU.mult).then_inc(m1_done, 1)

                def product(i, t):
                    if t % GB == 0:
                        return
                    b = t % GB - 1
                    n = data_no(i, t)
                    dve.wait_ge(m1_done, n + 1)
                    dve.wait_ge(m2_done, n + 1)
                    if not (early(i, t, 1) and b < R):
                        dve.wait_ge(w_ps, n - R + 1)
                    dve.tensor_tensor(u[:, b % R, :], m1[:, b % R, :], m2[:, b % R, :], ALU.add).then_inc(u_done, 1)

                pipelined(dve, GROUPS // 2, T, [(same_part, 0), (product, 2)])

    def back():
        with ExitStack() as st:
            def sb(name, shape, dt=F32):
                return st.enter_context(nc.sbuf_tensor(name, shape, dt))

            def ps(name):
                return st.enter_context(nc.psum_tensor(name, [P, C], F32))

            s4 = sb("b_s4", [P, 2, N2, P])
            woh = sb("woh", [P, CT, C], F32R)
            wol = sb("wol", [P, CT, C], F32R)
            wfh = sb("wfh", [P, CT, C], F32R)
            wfl = sb("wfl", [P, CT, C], F32R)
            raw = sb("b_raw", [P, CT, C])
            edge = sb("b_edge", [P, 2, N2, C])
            v0 = sb("b_v0", [P, CT, B])
            bor = sb("bor", [P, C])
            bfr = sb("bfr", [P, C])
            ident = sb("b_ident", [P, P])
            ad_raw = sb("b_ad_raw", [P, CT, C])
            D = 4
            fin = sb("b_fin", [P, 2, 2, C])
            gin = sb("b_gin", [P, 2, CT, P])
            xin = sb("b_xin", [P, D, C])
            corr = sb("b_corr", [P, 2, C])
            o = sb("b_o", [P, C])
            oh = sb("b_oh", [P, 2, C], F32R)
            ol = sb("b_ol", [P, 2, C], F32R)
            y = sb("b_y", [P, 2, C])
            stats = sb("b_stats", [P, 6])
            mv = sb("b_mv", [P, 2])
            rstd = sb("b_rstd", [P, 2])
            shift = sb("b_shift", [P, 2])
            power = sb("b_power", [P, 1])
            eps = sb("b_eps", [P, 1])
            minus = sb("b_minus", [P, 1])
            z = sb("b_z", [P, 2, C])
            yb = sb("b_yb", [P, D, C])
            zh = sb("b_zh", [P, 2, C], F32R)
            zl = sb("b_zl", [P, 2, C], F32R)
            res = sb("b_res", [P, D, C])
            psC = [ps("b_psC0"), ps("b_psC1")]
            psO = [ps("b_psO0"), ps("b_psO1")]
            psT = [ps("b_psT0"), ps("b_psT1")]
            psF = [ps("b_psF0"), ps("b_psF1")]

            turned = [psC[0], psC[1], psO[0], psO[1]]

            small_in = sem("b_small_in")
            power_set = sem("b_power_set")
            passed = sem("b_passed")
            passed_pool = sem("b_passed_pool")
            raw_in = sem("b_raw_in")
            ad_in = sem("b_ad_in")
            ad_turned = sem("b_ad_turned")
            hi_split = sem("b_hi_split")
            lo_split = sem("b_lo_split")
            f_in = [sem(f"b_f_in{i}") for i in range(2)]
            g_in = [sem(f"b_g_in{i}") for i in range(2)]
            x_in = [sem(f"b_x_in{i}") for i in range(D)]
            corr_step = sem("b_corr_step")
            corr_done = sem("b_corr_done")
            xb_done = sem("b_xb_done")
            c_ps = sem("b_c_ps")
            a_done = sem("b_a_done")
            o_done = sem("b_o_done")
            o_hi = sem("b_o_hi")
            o_lo = sem("b_o_lo")
            o_ps = sem("b_o_ps")
            y_done = sem("b_y_done")
            bn_step = sem("b_bn_step")
            mv_done = sem("b_mv_done")
            pow_step = sem("b_pow_step")
            norm_ready = sem("b_norm_ready")
            z_done = sem("b_z_done")
            yb_done = sem("b_yb_done")
            t_ps = sem("b_t_ps")
            z_hi = sem("b_z_hi")
            z_lo = sem("b_z_lo")
            ff_ps = sem("b_ff_ps")
            res_done = sem("b_res_done")
            out_stored = [sem(f"b_out_stored{i}") for i in range(D)]
            block = st.enter_context(nc.Block())

            def no(b, t):
                return b * N2 + t

            @block.sync
            def _(sp):
                sp.dma_start(s4[:], consts["s4"].rearrange("(j p) n r -> p j n r", p=P)).then_inc(small_in, 16)
                for q in range(2):
                    sp.dma_start(edge[:, q], edge_f[q].rearrange("p (n c) -> p n c", n=N2)).then_inc(small_in, 16)
                with nc.allow_non_contiguous_dma(reason="4096 words, once"):
                    for ct in range(CT):
                        sp.dma_start(v0[:, ct], first_v.rearrange("b (c p) -> c p b", p=P)[ct]).then_inc(small_in, 16)
                sp.dma_start(bor[:], out_b.rearrange("(a c) -> a c", a=1).partition_broadcast(P)).then_inc(small_in, 16)
                sp.dma_start(bfr[:], ad_bias).then_inc(small_in, 16)
                sp.dma_start(ident[:], consts["ident"]).then_inc(small_in, 16)
                sp.dma_start(raw[:], out_w.rearrange("(k p) c -> p k c", p=P)).then_inc(raw_in, 16)
                sp.dma_start(ad_raw[:], ad_mix).then_inc(ad_in, 16)

                def load_conv(b, t):
                    if old(b, t, 2):
                        sp.wait_ge(c_ps, no(b, t) - 1)
                    sp.dma_start(fin[:, t % 2], spec3[b].rearrange("(j p n) c -> n p j c", j=2, n=N2)[t]).then_inc(f_in[t % 2], 16)

                def load_gate(b, t):
                    if old(b, t, 2):
                        sp.wait_ge(o_done, no(b, t) - 1)
                    sp.dma_start(gin[:, t % 2], gate_t[b, t].rearrange("p (c r) -> p c r", c=CT)).then_inc(g_in[t % 2], 16)

                def load_x(b, t):
                    if old(b, t, D):
                        sp.wait_ge(y_done, no(b, t) - D + 1)
                    sp.dma_start(xin[:, t % D], x[b].rearrange("(p n) c -> n p c", n=N2)[t]).then_inc(x_in[t % D], 16)

                pipelined(sp, B, N2, [(load_conv, 0), (load_gate, 0), (load_x, 0)])

            @block.gpsimd
            def _(pool):
                pool.memset(power[:], -0.5).then_inc(power_set, 1)
                pool.memset(eps[:], EPS).then_inc(power_set, 1)
                pool.memset(minus[:], -1.0).then_inc(power_set, 1)
                pool.wait_ge(small_in, 16 * 10)
                pool.wait_ge(power_set, 3)

                def scalars(b, t):
                    pool.wait_ge(mv_done, no(b, t) + 1)
                    if old(b, t, 2):
                        pool.wait_ge(z_done, no(b, t) - 1)
                    r, m = rstd[:, t % 2:t % 2 + 1], shift[:, t % 2:t % 2 + 1]
                    pool.tensor_tensor(r, mv[:, 1:2], eps[:], ALU.add).then_inc(pow_step, 1)
                    pool.tensor_tensor(m, mv[:, 0:1], minus[:], ALU.mult).then_inc(pow_step, 1)
                    pool.wait_ge(pow_step, 3 * no(b, t) + 2)
                    pool.tensor_tensor(r, r, power[:], ALU.pow).then_inc(pow_step, 1)
                    pool.wait_ge(pow_step, 3 * no(b, t) + 3)
                    pool.tensor_tensor(m, m, r, ALU.mult).then_inc(norm_ready, 1)

                def correct(b, t):
                    if old(b, t, 2):
                        pool.wait_ge(o_done, no(b, t) - 1)
                    pool.sem_inc(passed_pool, 1)
                    v0b = v0[:, :, b:b + 1] if isinstance(b, int) else v0[:, :, bass.ds(b, 1)]
                    pool.tensor_tensor(corr[:, t % 2].rearrange("p (c r) -> p c r", c=CT),
                                       edge[:, 0, t].rearrange("p (c r) -> p c r", c=CT),
                                       v0b.to_broadcast([P, CT, P]), ALU.mult).then_inc(corr_step, 1)
                    pool.wait_ge(corr_step, no(b, t) + 1)
                    pool.tensor_tensor(corr[:, t % 2], corr[:, t % 2], edge[:, 1, t], ALU.add).then_inc(corr_done, 1)

                def bias_y(b, t):
                    pool.wait_ge(y_done, no(b, t) + 1)
                    if old(b, t, D):
                        pool.wait_ge(res_done, no(b, t) - D + 1)
                    pool.tensor_tensor(yb[:, t % D], y[:, t % 2], bfr[:], ALU.add).then_inc(yb_done, 1)

                pipelined(pool, B, N2, [(correct, 0), (scalars, 2), (bias_y, 2)])

            @block.scalar
            def _(act):
                act.wait_ge(raw_in, 16)
                act.activation(woh[:], raw[:], ACT.Copy).then_inc(hi_split, 1)
                for d in range(CT):
                    act.wait_ge(ad_turned, d + 1)
                    act.activation(wfh[:, d], turned[d][:], ACT.Copy).then_inc(hi_split, 1)

                def o_high(b, t):
                    act.wait_ge(o_done, no(b, t) + 1)
                    if old(b, t, 2):
                        act.wait_ge(o_ps, no(b, t) - 1)
                    act.activation(oh[:, t % 2], o[:], ACT.Copy).then_inc(o_hi, 1)

                def norm(b, t):
                    act.wait_ge(norm_ready, no(b, t) + 1)
                    if old(b, t, 2):
                        act.wait_ge(t_ps, no(b, t) - 1)
                    act.activation(z[:, t % 2], y[:, t % 2], ACT.Identity, bias=shift[:, t % 2:t % 2 + 1],
                                   scale=rstd[:, t % 2:t % 2 + 1]).then_inc(z_done, 1)

                def z_high(b, t):
                    act.wait_ge(t_ps, no(b, t) + 1)
                    if old(b, t, 2):
                        act.wait_ge(ff_ps, no(b, t) - 1)
                    act.activation(zh[:, t % 2], psT[t % 2][:], ACT.Copy).then_inc(z_hi, 1)

                def store(b, t):
                    act.wait_ge(res_done, no(b, t) + 1)
                    act.dma_start(out[b].rearrange("(p n) c -> n p c", n=N2)[t], res[:, t % D]).then_inc(out_stored[t % D], 16)

                pipelined(act, B, N2, [(o_high, 1), (z_high, 3), (norm, 2), (store, 6)])
                for i in range(D):
                    act.wait_ge(out_stored[i], 16 * B * N2 // D)

            @block.tensor
            def _(pe):
                pe.wait_ge(small_in, 16 * 10)
                pe.wait_ge(ad_in, 16)
                for d in range(CT):
                    for ot in range(CT):
                        mm = pe.transpose(turned[d][:, ot * P:(ot + 1) * P], ad_raw[:, ot, d * P:(d + 1) * P], ident[:])
                    mm.then_inc(ad_turned, 1)
                pe.wait_ge(lo_split, 1 + CT)

                def conv(b, t):
                    pe.wait_ge(f_in[t % 2], 16 * (b * (N2 // 2) + t // 2 + 1))
                    if old(b, t, 2):
                        pe.wait_ge(a_done, no(b, t) - 1)
                    for ct in range(CT):
                        for j in range(2):
                            mm = pe.matmul(psC[t % 2][:, ct * P:(ct + 1) * P], fin[:, t % 2, j, ct * P:(ct + 1) * P],
                                           s4[:, j, t, :], start=(j == 0), stop=(j == 1))
                    mm.then_inc(c_ps, 1)

                def project(b, t):
                    pe.wait_ge(o_lo, no(b, t) + 1)
                    if old(b, t, 2):
                        pe.wait_ge(y_done, no(b, t) - 1)
                    for ct in range(CT):
                        mm = mm3(pe, psO[t % 2][:], oh[:, t % 2, ct * P:(ct + 1) * P], ol[:, t % 2, ct * P:(ct + 1) * P],
                                 woh[:, ct], wol[:, ct], ct == 0, ct == CT - 1)
                    mm.then_inc(o_ps, 1)

                def turn(b, t):
                    pe.wait_ge(z_done, no(b, t) + 1)
                    if old(b, t, 2):
                        pe.wait_ge(z_lo, no(b, t) - 1)
                    for ct in range(CT):
                        mm = pe.transpose(psT[t % 2][:, ct * P:(ct + 1) * P], z[:, t % 2, ct * P:(ct + 1) * P], ident[:])
                    mm.then_inc(t_ps, 1)

                def adapt(b, t):
                    pe.wait_ge(z_lo, no(b, t) + 1)
                    if old(b, t, 2):
                        pe.wait_ge(res_done, no(b, t) - 1)
                    for ct in range(CT):
                        mm = mm3(pe, psF[t % 2][:], zh[:, t % 2, ct * P:(ct + 1) * P], zl[:, t % 2, ct * P:(ct + 1) * P],
                                 wfh[:, ct], wfl[:, ct], ct == 0, ct == CT - 1)
                    mm.then_inc(ff_ps, 1)

                pipelined(pe, B, N2, [(conv, 1), (project, 2), (turn, 3), (adapt, 4)])

            @block.vector
            def _(dve):
                dve.wait_ge(hi_split, 1)
                dve.tensor_tensor(wol[:], raw[:], woh[:].bitcast(F32), ALU.subtract).then_inc(lo_split, 1)
                for d in range(CT):
                    dve.wait_ge(hi_split, d + 2)
                    dve.tensor_tensor(wfl[:, d], turned[d][:], wfh[:, d].bitcast(F32), ALU.subtract).then_inc(lo_split, 1)

                def bias_x(b, t):
                    dve.wait_ge(x_in[t % D], 16 * (b * (N2 // D) + t // D + 1))
                    dve.tensor_tensor(xin[:, t % D], xin[:, t % D], bor[:], ALU.add).then_inc(xb_done, 1)

                def gate(b, t):
                    dve.wait_ge(corr_done, no(b, t) + 1)
                    dve.wait_ge(c_ps, no(b, t) + 1)
                    dve.tensor_tensor(corr[:, t % 2], psC[t % 2][:], corr[:, t % 2], ALU.add).then_inc(a_done, 1)
                    dve.wait_ge(a_done, no(b, t) + 1)
                    dve.wait_ge(g_in[t % 2], 16 * (b * (N2 // 2) + t // 2 + 1))
                    if old(b, t, 1):
                        dve.wait_ge(o_lo, no(b, t))
                    dve.tensor_tensor(o[:], corr[:, t % 2], gin[:, t % 2].rearrange("p c r -> p (c r)"),
                                      ALU.mult).then_inc(o_done, 1)

                def o_low(b, t):
                    dve.wait_ge(o_hi, no(b, t) + 1)
                    dve.tensor_tensor(ol[:, t % 2], o[:], oh[:, t % 2].bitcast(F32), ALU.subtract).then_inc(o_lo, 1)

                def residual(b, t):
                    dve.wait_ge(o_ps, no(b, t) + 1)
                    dve.wait_ge(xb_done, no(b, t) + 1)
                    if old(b, t, 2):
                        dve.wait_ge(yb_done, no(b, t) - 1)
                        dve.wait_ge(z_done, no(b, t) - 1)
                    dve.tensor_tensor(y[:, t % 2], psO[t % 2][:], xin[:, t % D], ALU.add).then_inc(y_done, 1)
                    dve.wait_ge(y_done, no(b, t) + 1)
                    dve.bn_stats(stats[:], y[:, t % 2]).then_inc(bn_step, 1)
                    dve.wait_ge(bn_step, no(b, t) + 1)
                    if old(b, t, 1):
                        dve.wait_ge(norm_ready, no(b, t))
                    dve.sem_inc(passed, 1)
                    dve.bn_aggr(mv[:], stats[:]).then_inc(mv_done, 1)

                def z_low(b, t):
                    dve.wait_ge(z_hi, no(b, t) + 1)
                    dve.tensor_tensor(zl[:, t % 2], psT[t % 2][:], zh[:, t % 2].bitcast(F32), ALU.subtract).then_inc(z_lo, 1)

                def finish(b, t):
                    dve.wait_ge(ff_ps, no(b, t) + 1)
                    dve.wait_ge(yb_done, no(b, t) + 1)
                    if old(b, t, D):
                        dve.wait_ge(out_stored[t % D], 16 * (b * (N2 // D) + t // D))
                    dve.tensor_tensor(res[:, t % D], psF[t % 2][:], yb[:, t % D], ALU.add).then_inc(res_done, 1)

                pipelined(dve, B, N2, [(finish, 5), (bias_x, 0), (gate, 1), (o_low, 1), (residual, 2), (z_low, 3)])

    prep()
    front()
    middle()
    back()


_INS = ['L0_attn_x', 'L0_attn_in_proj_w', 'L0_attn_in_proj_b', 'L0_attn_short_w', 'L0_attn_short_b', 'L0_attn_fw1',
        'L0_attn_fb1', 'L0_attn_fw2', 'L0_attn_fb2', 'L0_attn_fw3', 'L0_attn_fb3', 'L0_attn_out_w', 'L0_attn_out_b',
        'L0_ffn_W', 'L0_ffn_b', 'L0_ffn_ids', 'L0_ffn_weights']


def kernel(**inputs):
    import concourse.bacc as _bacc
    from concourse.bass_utils import run_bass_kernel_spmd as _run

    nc = _bacc.Bacc("TRN2", target_bir_lowering=False, num_devices=1)
    arrays, args, consts = {}, [], {}
    for name in _INS:
        a = np.ascontiguousarray(inputs[name])
        arrays[f"in_{name}_dram"] = a
        args.append(nc.dram_tensor(f"in_{name}_dram", a.shape, mybir.dt.from_np(a.dtype), kind="ExternalInput").ap())
    for name, a in stage_matrices().items():
        a = np.ascontiguousarray(a)
        arrays[f"const_{name}_dram"] = a
        consts[name] = nc.dram_tensor(f"const_{name}_dram", a.shape, mybir.dt.from_np(a.dtype), kind="ExternalInput").ap()
    out = nc.dram_tensor("out_0_dram", (B, L, C), F32, kind="ExternalOutput").ap()
    hyena_adapter_kernel(nc, *args, consts, out)
    r = _run(nc, [arrays], core_ids=[0])
    return r.results[0]["out_0_dram"]
```

```python
from contextlib import ExitStack

import numpy as np

import concourse.bass as bass
from concourse import mybir

F32 = mybir.dt.float32
F32R = mybir.dt.float32r
I32 = mybir.dt.int32
ALU = mybir.AluOpType
ACT = mybir.ActivationFunctionType

P = 128
B = 8
L = 2048
C = 512
CT = C // P
N1H = P
N2 = L // N1H
N = 2 * L
SLOTS = P
ROWS = 2 * SLOTS
KG = 4
GROUPS = SLOTS // KG
GB = B + 1
NIDS = 8
NADAPT = 32
EPS = 1e-5
SUB = 4


def stage_matrices():
    n1 = np.arange(N1H)[:, None, None]
    n2 = np.arange(N2)[None, :, None]
    k1 = np.arange(SLOTS)[None, None, :]
    n = n1 * N2 + n2
    ang = 2 * np.pi * ((n * k1) % N) / N
    sign = np.where(n1[:, :, 0] % 2 == 0, 1.0, -1.0)
    s1 = np.zeros((N1H, N2, SLOTS, 2))
    s1[..., 0] = np.cos(ang)
    s1[..., 1] = -np.sin(ang)
    s1[:, :, 0, 0] = 1.0
    s1[:, :, 0, 1] = sign
    s1x = np.zeros((1, SLOTS, 2))
    ax = 2 * np.pi * (((N - 1) * np.arange(SLOTS)) % N) / N
    s1x[0, :, 0] = np.cos(ax)
    s1x[0, :, 1] = -np.sin(ax)
    s1x[0, 0] = [1.0, -1.0]
    s4 = np.zeros((SLOTS, 2, N2, N1H))
    a4 = ang.transpose(2, 1, 0)
    s4[:, 0] = 2 * np.cos(a4) / N
    s4[:, 1] = -2 * np.sin(a4) / N
    s4[0, 0] = 1.0 / N
    s4[0, 1] = sign.T / N

    m = np.arange(N2)
    a = 2 * np.pi * ((m[:, None] * m[None, :]) % N2) / N2
    c, s = np.cos(a), np.sin(a)
    fwd = np.zeros((2, N2, 2, N2))
    fwd[0, :, 0], fwd[1, :, 0] = c, s
    fwd[0, :, 1], fwd[1, :, 1] = -s, c
    inv = np.zeros((2, N2, 2, N2))
    inv[0, :, 0], inv[1, :, 0] = c, -s
    inv[0, :, 1], inv[1, :, 1] = s, c
    half = N2 // 2
    fsp = np.zeros((2, N2, 2, N2))
    isp = np.zeros((2, N2, 2, N2))
    fsp[0, :, 0, 0] = 1.0
    fsp[0, :, 1, 0] = (-1.0) ** m
    isp[0, 0, 0, :] = 1.0
    isp[1, 0, 0, :] = (-1.0) ** m
    for k in range(1, half):
        fsp[0, :, 0, k], fsp[0, :, 1, k] = c[:, k], -s[:, k]
        isp[0, k, 0, :], isp[1, k, 0, :] = 2 * c[:, k], -2 * s[:, k]
    for k in range(half):
        b = 2 * np.pi * m * (k + 0.5) / N2
        fsp[1, :, 0, half + k], fsp[1, :, 1, half + k] = np.cos(b), -np.sin(b)
        isp[0, half + k, 1, :], isp[1, half + k, 1, :] = 2 * np.cos(b), -2 * np.sin(b)

    def same(f):
        out = np.zeros_like(f)
        out[:, :, 0] = out[:, :, 1] = f[:, :, 0]
        return out

    def cross(f):
        out = np.zeros_like(f)
        out[:, :, 0], out[:, :, 1] = -f[:, :, 1], f[:, :, 1]
        return out

    same_sp, cross_sp = same(fsp), cross(fsp)
    same_sp[:, :, 1, 0] = fsp[:, :, 1, 0]
    cross_sp[:, :, :, 0] = 0.0

    def tile(first, rest):
        out = np.zeros((2, KG, N2, 2, KG, N2))
        for g in range(KG):
            out[:, g, :, :, g, :] = first if g == 0 else rest
        return out.reshape(P, P)

    mid = np.stack([tile(fsp, fwd), tile(same_sp, same(fwd)), tile(cross_sp, cross(fwd)), tile(isp, inv),
                    tile(fwd, fwd), tile(inv, inv)], axis=1)
    return {
        "pos": np.linspace(0.0, 1.0, L).astype(np.float32).reshape(1, L),
        "s1": in_groups(s1.reshape(N1H, N2, ROWS), 2).astype(np.float32),
        "s1x": in_groups(s1x.reshape(1, ROWS), 1).astype(np.float32),
        "s4": in_groups(s4.reshape(ROWS, N2, N1H), 0).astype(np.float32),
        "mid": mid.astype(np.float32),
        "ident": np.eye(P, dtype=np.float32),
    }


def in_groups(a, axis):
    shape = a.shape
    a = a.reshape(shape[:axis] + (GROUPS, KG, 2) + shape[axis + 1:])
    return np.ascontiguousarray(a.swapaxes(axis + 1, axis + 2)).reshape(shape)


def pipelined(eng, outer, tiles, stages):
    fill = max(lag for _, lag in stages)

    def step(i, s, last):
        for stage, lag in stages:
            t = s - lag
            if t >= tiles and not last:
                stage(i + 1, t - tiles)
            elif 0 <= t < tiles:
                stage(i, t)

    for s in range(fill):
        step(0, s, False)

    def one_pass(i, last):
        for s in range(fill, tiles + fill):
            step(i, s, last)

    one_pass(0, False)
    with eng.Fori(1, outer - 1) as i:
        one_pass(i, False)
    one_pass(outer - 1, True)


def old(b, t, n):
    return not (isinstance(b, int) and b * N2 + t < n)


def hyena_adapter_kernel(nc, x, in_w, in_b, short_w, short_b, fw1, fb1, fw2, fb2, fw3, fb3,
                         out_w, out_b, w_ad, b_ad, ids, weights, consts, out):
    ctx = ExitStack()
    spec1 = nc.dram_tensor("spec1", [GB, ROWS * N2, C], F32, kind="Internal").ap()
    spec3 = nc.dram_tensor("spec3", [B, ROWS * N2, C], F32, kind="Internal").ap()
    gate_t = nc.dram_tensor("gate_t", [B, N2, P, C], F32, kind="Internal").ap()
    first_v = nc.dram_tensor("first_v", [B, C], F32, kind="Internal").ap()
    edge_f = nc.dram_tensor("edge_f", [2, P, N2 * C], F32, kind="Internal").ap()
    ad_mix = nc.dram_tensor("ad_mix", [P, CT, C], F32, kind="Internal").ap()
    ad_bias = nc.dram_tensor("ad_bias", [P, C], F32, kind="Internal").ap()

    def sem(name):
        return ctx.enter_context(nc.semaphore(name))

    def mm3(pe, out_ps, w_hi, w_lo, d_hi, d_lo, first, last):
        pe.matmul(out_ps, w_hi, d_hi, start=first, stop=False)
        pe.matmul(out_ps, w_hi, d_lo, start=False, stop=False)
        return pe.matmul(out_ps, w_lo, d_hi, start=False, stop=last)

    def prep(fc):
        with ExitStack() as st:
            def sb(name, shape, dt=F32):
                return st.enter_context(nc.sbuf_tensor(name, shape, dt))

            def ps(name):
                return st.enter_context(nc.psum_tensor(name, [P, C], F32))

            LP = L + 2
            TQ = L // C
            HIGH_AT = (8, 10, 14, 17)
            LOW_AT = (7, 9, 13, 15)
            S1_LOW_AT = (10, 12, 14, 15)
            wide = sb("wide", [P, L])
            pos = wide[0:64]
            cum = wide
            w1c = sb("w1c", [64, 1])
            b1c = sb("b1c", [64, 1])
            w2s = sb("w2s", [64, P])
            b2c = sb("b2c", [P, 1])
            w3 = sb("w3", [P, 2 * C])
            w3s = sb("w3s", [P, C])
            BR = 32
            b3s = sb("b3s", [2 * BR, C])
            b3hl = sb("b3hl", [2 * BR, C], F32R)
            b3c = sb("b3c", [P, CT])
            tapr = sb("tapr", [P, 3 * C])
            tapc = sb("tapc", [P, CT, 3])
            minus_w2 = sb("minus_w2", [P, CT])
            sbc = sb("sbc", [P, CT])
            h1 = pos
            h2 = sb("h2", [P, LP])
            inside = sb("inside", [2 * BR, 3, P])
            inside_r = sb("inside_r", [2 * BR, 3, P], F32R)
            HR = 4
            GR = 3
            LAG = 5
            H = sb("H", [P, HR, C])
            wraw = sb("wraw", [P, 2, 3 * C])
            g = sb("g", [P, GR, C])
            gx = sb("gx", [P, C])
            gy = sb("gy", [P, 2, C])
            b3r = gy[0:2 * BR].rearrange("p k c -> p (k c)")
            g_before = sb("g_before", [1, C])
            s1 = sb("ps1", [P, N2, ROWS])
            s1x = sb("ps1x", [1, ROWS])
            s1o = sb("s1o", [P, 2, 2, C])
            ht = sb("ht", [P, 2, L + 1])
            edge = sb("edge", [P, N2, P])
            edge_sum = sb("edge_sum", [P, N2, P])
            pA = [ps("pA0"), ps("pA1")]
            pT = [ps("pT0"), ps("pT1")]
            pB = [ps(f"pB{i}") for i in range(4)]

            net_in = sem("p_net_in")
            w3_in = sem("p_w3_in")
            taps_in = sem("p_taps_in")
            mats_in = sem("p_mats_in")
            w_in = [sem(f"p_w_in{i}") for i in range(2)]
            w_high = sem("p_w_high")
            w_low = sem("p_w_low")
            bias_high = sem("p_bias_high")
            bias_low = sem("p_bias_low")
            s1_high = sem("p_s1_high")
            s1_low = sem("p_s1_low")
            consts_in = sem("p_consts_in")
            cols_in = sem("p_cols_in")
            zeroed = sem("p_zeroed")
            h1_done = sem("p_h1_done")
            h2_ps = sem("p_h2_ps")
            h2_done = sem("p_h2_done")
            sliced = sem("p_sliced")
            H_ps = sem("p_H_ps")
            H_done = sem("p_H_done")
            tap0 = sem("p_tap0")
            tap1 = sem("p_tap1")
            tap2 = sem("p_tap2")
            tap01 = sem("p_tap01")
            g_done = sem("p_g_done")
            before_done = sem("p_before_done")
            s1_ps = sem("p_s1_ps")
            s1_out = sem("p_s1_out")
            s1_stored = [sem(f"p_s1_stored{i}") for i in range(2)]
            ht_ps = sem("p_ht_ps")
            ht_done = sem("p_ht_done")
            neg_done = sem("p_neg_done")
            cum_done = sem("p_cum_done")
            edge_done = sem("p_edge_done")
            edge_stored = [sem(f"p_edge_stored{q}") for q in range(2)]

            block = st.enter_context(nc.Block())

            def store_edges(sp, ct, q):
                sp.wait_ge(edge_done, 2 * ct + q + 1)
                sp.dma_start(edge_f[q].rearrange("p (n c r) -> c p n r", n=N2, c=CT)[ct],
                             (edge, edge_sum)[q][:]).then_inc(edge_stored[q], 16)

            @block.sync
            def _(sp):
                sp.dma_start(w1c[:], fw1.rearrange("a (p b) -> p (a b)", b=1)).then_inc(net_in, 16)
                sp.dma_start(b1c[:], fb1.rearrange("(p b) -> p b", b=1)).then_inc(net_in, 16)
                sp.dma_start(pos, consts["pos"].partition_broadcast(64)).then_inc(net_in, 16)
                sp.dma_start(w2s[:], fw2).then_inc(net_in, 16)
                sp.dma_start(b2c[:], fb2.rearrange("(p b) -> p b", b=1)).then_inc(net_in, 16)
                sp.dma_start(w3[:], fw3).then_inc(w3_in, 16)
                sp.dma_start(b3r, fb3.rearrange("(a n) -> a n", a=1).partition_broadcast(2 * BR)).then_inc(w3_in, 16)
                sp.dma_start(tapr[:], short_w.rearrange("(o c) a w -> o (c a w)", o=1).partition_broadcast(P)).then_inc(taps_in, 16)
                sp.dma_start(s1[:], consts["s1"]).then_inc(mats_in, 16)
                sp.dma_start(s1x[:], consts["s1x"]).then_inc(mats_in, 16)
                with nc.allow_non_contiguous_dma(reason="words of bias and taps by channel, once"):
                    sp.dma_start(b3c[:], fb3.rearrange("(c p two) -> p c two", p=P, two=2)[:, :, 1]).then_inc(cols_in, 16)
                    sp.dma_start(tapc[:], short_w.rearrange("(c p) a w -> p c (a w)", p=P)).then_inc(cols_in, 16)
                    sp.dma_start(sbc[:], short_b.rearrange("(c p) -> p c", p=P)).then_inc(cols_in, 16)
                with nc.allow_non_contiguous_dma(reason="512 words of bias, once"):
                    sp.dma_start(fc["bgc"][:], in_b.rearrange("(c p w) -> p c w", p=P, w=3)[:, :, 2]).then_inc(consts_in, 16)
                sp.dma_start(fc["bv3"][:], in_b.rearrange("(a c) -> a c", a=1).partition_broadcast(P)).then_inc(consts_in, 16)
                sp.dma_start(fc["ident"][:], consts["ident"]).then_inc(consts_in, 16)
                sp.dma_start(fc["xg0"][:], x[0].rearrange("(p n) c -> p n c", n=N2)[:, 0:SUB, :]).then_inc(fc["x_in"][0], 16)
                for kt in range(2):
                    sp.dma_start(wraw[:, kt], in_w[kt * P:(kt + 1) * P, :]).then_inc(w_in[kt], 16)
                for q in range(2):
                    store_edges(sp, 0, q)
                for n2 in range(N2):
                    sp.wait_ge(s1_out, 2 * n2 + 2)
                    for j in range(2):
                        sp.dma_start(spec1[B].rearrange("(j p n) c -> n p j c", j=2, n=N2)[n2][:, j, :],
                                     s1o[:, n2 % 2, j, :]).then_inc(s1_stored[n2 % 2], 16)
                    if n2 in (6, 8):
                        kt = 2 + (6, 8).index(n2)
                        sp.wait_ge(w_low, 2 * (kt - 1))
                        sp.dma_start(wraw[:, kt % 2], in_w[kt * P:(kt + 1) * P, :]).then_inc(w_in[kt % 2], 16)
                    if n2 % TQ < 2 and n2 < N2 - TQ:
                        store_edges(sp, n2 // TQ + 1, n2 % TQ)
                for i in range(2):
                    sp.wait_ge(s1_stored[i], 16 * N2)
                for q in range(2):
                    sp.wait_ge(edge_stored[q], 16 * CT)
                sp.wait_ge(consts_in, 48)
                sp.wait_ge(fc["x_in"][0], 16)

            @block.gpsimd
            def _(pool):
                pool.memset(inside[:], 1.0 / BR).then_inc(zeroed, 1)
                pool.memset(h2[:, 0:1], 0.0).then_inc(zeroed, 1)
                pool.memset(h2[:, LP - 1:LP], 0.0).then_inc(zeroed, 1)
                pool.memset(ht[:, :, L:L + 1], 0.0).then_inc(zeroed, 1)
                pool.wait_ge(zeroed, 4)
                pool.memset(inside[:, 0, 0:1], 0.0).then_inc(zeroed, 1)
                pool.memset(inside[:, 1, P - 1:P], 0.0).then_inc(zeroed, 1)
                tap = tapr[:].rearrange("p (c w) -> p w c", w=3)
                pool.wait_ge(taps_in, 16)

                def s1_lows(k):
                    part = slice(k * (N2 // 4), (k + 1) * (N2 // 4))
                    pool.wait_ge(s1_high, k + 1)
                    pool.tensor_tensor(fc["s1l"][:, part], s1[:, part], fc["s1h"][:, part].bitcast(F32), ALU.subtract).then_inc(s1_low, 1)

                for n2 in range(N2):
                    pool.wait_ge(H_done, n2 + 3)
                    if n2 >= 2:
                        pool.wait_ge(g_done, n2 - 1)
                    pool.tensor_tensor(gy[:, n2 % 2], H[:, (n2 + 2) % HR], tap[:, 2], ALU.mult).then_inc(tap2, 1)
                    if n2 in S1_LOW_AT:
                        s1_lows(S1_LOW_AT.index(n2))

            @block.scalar
            def _(act):
                act.wait_ge(net_in, 16 * 5)
                for q in range(TQ):
                    cols = slice(q * C, (q + 1) * C)
                    act.activation(h1[:, cols], pos[:, cols], ACT.Gelu, bias=b1c[:], scale=w1c[:]).then_inc(h1_done, 1)
                for q in range(TQ):
                    act.wait_ge(h2_ps, q + 1)
                    act.activation(h2[:, 1 + q * C:1 + (q + 1) * C], pA[q % 2][:], ACT.Gelu, bias=b2c[:]).then_inc(h2_done, 1)

                def s1_copy(n2):
                    for j in range(2):
                        act.wait_ge(s1_ps, 2 * n2 + j + 1)
                        if n2 >= 2:
                            act.wait_ge(s1_stored[n2 % 2], 32 * (n2 // 2))
                        act.activation(s1o[:, n2 % 2, j, :], pB[2 * (n2 % 2) + j][:], ACT.Copy).then_inc(s1_out, 1)

                def ht_copy(n):
                    ct, q = n // TQ, n % TQ
                    act.wait_ge(ht_ps, n + 1)
                    if q == 0 and ct >= 2:
                        act.wait_ge(cum_done, ct - 1)
                    act.activation(ht[:, ct % 2, q * C:(q + 1) * C], pT[q % 2][:], ACT.Identity,
                                   bias=b3c[:, ct:ct + 1]).then_inc(ht_done, 1)

                def edges(ct, which):
                    if which == 0:
                        act.wait_ge(ht_done, (ct + 1) * TQ)
                        act.wait_ge(zeroed, 6)
                        if ct >= 1:
                            act.wait_ge(edge_stored[0], 16 * ct)
                        act.activation(edge[:], ht[:, ct % 2, 1:L + 1].rearrange("p (r n) -> p n r", n=N2), ACT.Copy,
                                       scale=minus_w2[:, ct:ct + 1]).then_inc(edge_done, 1)
                        return
                    act.wait_ge(cum_done, ct + 1)
                    if ct >= 1:
                        act.wait_ge(edge_stored[1], 16 * ct)
                    act.activation(edge_sum[:], cum[:].rearrange("p (r n) -> p n r", n=N2), ACT.Copy,
                                   scale=sbc[:, ct:ct + 1]).then_inc(edge_done, 1)

                act.wait_ge(zeroed, 6)
                act.activation(inside_r[:], inside[:], ACT.Copy).then_inc(bias_high, 1)
                act.wait_ge(sliced, 2)
                act.activation(b3hl[:], b3s[:], ACT.Copy).then_inc(bias_high, 1)
                act.wait_ge(cols_in, 48)
                act.activation(minus_w2[:], tapc[:, :, 2], ACT.Copy, scale=-1.0).then_inc(neg_done, 1)
                act.wait_ge(neg_done, 1)
                for n in range(TQ):
                    ht_copy(n)
                for e in range(N2 + LAG):
                    if e < N2 + 2:
                        act.wait_ge(H_ps, e + 1)
                        if e >= HR:
                            act.wait_ge(g_done, e - HR + 1)
                        act.activation(H[:, e % HR, :], pA[e % 2][:], ACT.Copy).then_inc(H_done, 1)
                    if e >= LAG:
                        s1_copy(e - LAG)
                    if e + TQ < CT * TQ:
                        ht_copy(e + TQ)
                    if e < N2 and e % TQ < 2:
                        edges(e // TQ, e % TQ)
                    if e == min(HIGH_AT):
                        act.wait_ge(mats_in, 32)
                    if e in HIGH_AT:
                        kt = HIGH_AT.index(e)
                        rows = wraw[:, kt % 2].rearrange("p (c w) -> p c w", w=3)
                        act.wait_ge(w_in[kt % 2], 16 * (kt // 2 + 1))
                        act.activation(fc["wvh"][:, kt], rows[:, :, 0], ACT.Copy).then_inc(w_high, 1)
                        act.activation(fc["wgh"][:, kt], rows[:, :, 2], ACT.Copy).then_inc(w_high, 1)
                    if e >= 11 and e % 2 == 1 and e < 19:
                        part = slice((e - 11) // 2 * (N2 // 4), ((e - 11) // 2 + 1) * (N2 // 4))
                        act.activation(fc["s1h"][:, part], s1[:, part], ACT.Copy).then_inc(s1_high, 1)

            @block.tensor
            def _(pe):
                def filter_rows(n):
                    ct, q = n // TQ, n % TQ
                    if n >= 2:
                        pe.wait_ge(ht_done, n - 1)
                    pe.matmul(pT[q % 2][:], w3s[:, ct * P:(ct + 1) * P], h2[:, 1 + q * C:1 + (q + 1) * C],
                              start=True, stop=True).then_inc(ht_ps, 1)

                pe.wait_ge(net_in, 16 * 5)
                for q in range(TQ):
                    pe.wait_ge(h1_done, q + 1)
                    if q >= 2:
                        pe.wait_ge(h2_done, q - 1)
                    pe.matmul(pA[q % 2][:], w2s[:], h1[:, q * C:(q + 1) * C], start=True, stop=True).then_inc(h2_ps, 1)
                pe.wait_ge(h2_done, TQ)
                pe.wait_ge(sliced, 2)
                pe.wait_ge(zeroed, 6)
                pe.wait_ge(bias_high, 2)
                pe.wait_ge(bias_low, 1)
                for n in range(TQ):
                    filter_rows(n)

                def stage1(n2):
                    edge_row = n2 == N2 - 1
                    pe.wait_ge(g_done, n2 + 1)
                    for j in range(2):
                        bank = pB[2 * (n2 % 2) + j]
                        if n2 >= 2:
                            pe.wait_ge(s1_out, 2 * (n2 - 1))
                        mm = pe.matmul(bank[:], s1[:, n2, j * P:(j + 1) * P], g[:, n2 % GR, :], start=True, stop=not edge_row)
                        if edge_row:
                            pe.wait_ge(before_done, 1)
                            mm = pe.matmul(bank[:], s1x[:, j * P:(j + 1) * P], g_before[:], start=False, stop=True)
                        mm.then_inc(s1_ps, 1)

                for e in range(N2 + LAG):
                    if e < N2 + 2:
                        if e >= 2:
                            pe.wait_ge(H_done, e - 1)
                        cols = slice(e, e + (N1H - 1) * N2 + 1, N2)
                        where = 0 if e == 0 else 1 if e == N2 + 1 else 2
                        pe.matmul(pA[e % 2][:], h2[:, cols], w3s[:], start=True, stop=False)
                        pe.matmul(pA[e % 2][:], inside_r[:, where], b3hl[:], start=False, stop=True).then_inc(H_ps, 1)
                    if e == LAG:
                        pe.wait_ge(mats_in, 32)
                    if e >= LAG:
                        stage1(e - LAG)
                    if e + TQ < CT * TQ:
                        filter_rows(e + TQ)

            @block.vector
            def _(dve):
                dve.wait_ge(w3_in, 32)
                dve.tensor_copy(w3s[:], w3[:].rearrange("p (c two) -> p c two", two=2)[:, :, 1]).then_inc(sliced, 1)
                dve.tensor_copy(b3s[:], b3r.rearrange("p (c two) -> p c two", two=2)[:, :, 1]).then_inc(sliced, 1)
                dve.wait_ge(bias_high, 2)
                dve.wait_ge(sliced, 2)
                low = slice(BR, 2 * BR)
                dve.tensor_tensor(b3hl[low], b3s[low], b3hl[low].bitcast(F32), ALU.subtract).then_inc(bias_low, 1)
                dve.wait_ge(taps_in, 16)
                tap = tapr[:].rearrange("p (c w) -> p w c", w=3)

                def running_sum(ct):
                    dve.wait_ge(ht_done, (ct + 1) * TQ)
                    if ct >= 1:
                        dve.wait_ge(edge_done, 2 * ct)
                    dve.tensor_tensor_scan(cum[:], ht[:, ct % 2, 0:L], ht[:, ct % 2, 0:L], 0.0, ALU.add, ALU.bypass).then_inc(cum_done, 1)

                def w_lows(kt):
                    rows = wraw[:, kt % 2].rearrange("p (c w) -> p c w", w=3)
                    dve.wait_ge(w_high, 2 * kt + 2)
                    dve.tensor_tensor(fc["wvl"][:, kt], rows[:, :, 0], fc["wvh"][:, kt].bitcast(F32), ALU.subtract).then_inc(w_low, 1)
                    dve.tensor_tensor(fc["wgl"][:, kt], rows[:, :, 2], fc["wgh"][:, kt].bitcast(F32), ALU.subtract).then_inc(w_low, 1)

                dve.wait_ge(zeroed, 6)
                running_sum(0)
                for n2 in range(N2):
                    k = n2 % GR
                    dve.wait_ge(H_done, n2 + 2)
                    if n2 >= GR:
                        dve.wait_ge(s1_ps, 2 * (n2 - GR + 1))
                    dve.tensor_tensor(g[:, k], H[:, n2 % HR], tap[:, 0], ALU.mult).then_inc(tap0, 1)
                    if n2 >= 1:
                        dve.wait_ge(g_done, n2)
                    dve.tensor_tensor(gx[:], H[:, (n2 + 1) % HR], tap[:, 1], ALU.mult).then_inc(tap1, 1)
                    dve.wait_ge(tap0, n2 + 1)
                    dve.wait_ge(tap1, n2 + 1)
                    dve.tensor_tensor(gx[:], g[:, k], gx[:], ALU.add).then_inc(tap01, 1)
                    dve.wait_ge(tap01, n2 + 1)
                    dve.wait_ge(tap2, n2 + 1)
                    dve.tensor_tensor(g[:, k], gx[:], gy[:, n2 % 2], ALU.add).then_inc(g_done, 1)
                    if n2 == 0:
                        dve.tensor_tensor(g_before[:], H[0:1, 1, :], tap[0:1, 2, :], ALU.mult).then_inc(before_done, 1)
                    if n2 % TQ == TQ - 2 and n2 + 2 < N2:
                        running_sum((n2 + 2) // TQ)
                    if n2 in LOW_AT:
                        w_lows(LOW_AT.index(n2))

    def front(fc):
        with ExitStack() as st:
            def sb(name, shape, dt=F32):
                return st.enter_context(nc.sbuf_tensor(name, shape, dt))

            def ps(name):
                return st.enter_context(nc.psum_tensor(name, [P, C], F32))

            s1h, s1l, wvh, wvl, wgh, wgl = (fc[k] for k in ("s1h", "s1l", "wvh", "wvl", "wgh", "wgl"))
            ident, bgc = fc["ident"], fc["bgc"]
            bvr = fc["bv3"][:].rearrange("p (c w) -> p w c", w=3)[:, 0, :]
            xg, x_in = (fc["xg0"], sb("xg1", [P, SUB, C])), fc["x_in"]
            stats = sb("fstats", [P, 2, SUB, 6])
            mv = sb("fmv", [P, 2, SUB, 2])
            rstd = sb("frstd", [P, 2, SUB])
            shift = sb("fshift", [P, 2, SUB])
            power = sb("fpower", [P, SUB])
            eps = sb("feps", [P, SUB])
            minus = sb("fminus", [P, SUB])
            xn = sb("xn", [P, 2, C])
            nth = sb("nth", [P, 2, CT, SUB * P], F32R)
            ntl = sb("ntl", [P, 2, CT, SUB * P], F32R)
            v = sb("v", [P, 2, C])
            vh = sb("vh", [P, 2, C], F32R)
            vl = sb("vl", [P, 2, C], F32R)
            s1o = sb("fs1o", [P, 2, 2, SUB, C])
            gto = sb("gto", [P, 2, SUB, CT, P])
            ad_load = sb("ad_load", [P, CT, C])
            ad_sum = sb("ad_sum", [P, CT, C])
            adb_load = sb("adb_load", [P, C])
            adb_sum = sb("adb_sum", [P, C])
            wgt = sb("wgt", [P, NIDS])
            idst = sb("idst", [1, NIDS], I32)
            psT = [ps("psT0"), ps("psT1")]
            psV = [ps("psV0"), ps("psV1")]
            psS = [ps("psS0"), ps("psS1")]
            psX = [ps("psX0"), ps("psX1")]

            ids_in = sem("f_ids_in")
            ad_in = sem("f_ad_in")
            ad_clear = sem("f_ad_clear")
            ad_used = sem("f_ad_used")
            ad_stored = sem("f_ad_stored")
            power_set = sem("f_power_set")
            passed = sem("f_passed")
            passed_sp = sem("f_passed_sp")
            x_free = sem("f_x_free")
            bn_step = sem("f_bn_step")
            mv_done = sem("f_mv_done")
            pow_step = sem("f_pow_step")
            norm_ready = sem("f_norm_ready")
            xn_done = sem("f_xn_done")
            t_ps = sem("f_t_ps")
            nt_hi = sem("f_nt_hi")
            nt_lo = sem("f_nt_lo")
            v_ps = sem("f_v_ps")
            v_done = sem("f_v_done")
            v0_out = sem("f_v0_out")
            v_hi = sem("f_v_hi")
            v_lo = sem("f_v_lo")
            s_ps = sem("f_s_ps")
            s_out0 = sem("f_s_out0")
            s_out1 = sem("f_s_out1")
            s_stored = [sem(f"f_s_stored{i}") for i in range(2)]
            x2_ps = sem("f_x2_ps")
            x2_out = sem("f_x2_out")
            x2_stored = [sem(f"f_x2_stored{i}") for i in range(2)]

            block = st.enter_context(nc.Block())
            Q = N2 // SUB
            MIX = CT + 1

            def tile_no(b, t):
                return b * N2 + t

            def group_no(b, t):
                return b * Q + t // SUB

            @block.sync
            def _(sp):
                sp.dma_start(wgt[:], weights.rearrange("(a n) -> a n", a=1).partition_broadcast(P)).then_inc(ids_in, 16)
                sp.dma_start(idst[:], ids.rearrange("(a n) -> a n", a=1)).then_inc(ids_in, 16)

                def load_adapter(b, t):
                    if t != 1:
                        return
                    if isinstance(b, int) and b == 0:
                        sp.wait_ge(ids_in, 32)
                    which = sp.value_load(idst[0:1, b:b + 1] if isinstance(b, int) else idst[0:1, bass.ds(b, 1)],
                                          min_val=0, max_val=NADAPT - 1)
                    if old(b, t, N2):
                        sp.wait_ge(ad_used, MIX * b)
                    sp.dma_start(ad_load[:], w_ad[bass.ds(which, 1)].rearrange("a (t p) d -> (a p) t d", p=P)).then_inc(ad_in, 16)
                    sp.dma_start(adb_load[:], b_ad[bass.ds(which, 1)].partition_broadcast(P)).then_inc(ad_in, 16)

                def load_x(b, t):
                    if t % SUB or (isinstance(b, int) and b == 0 and t == 0):
                        return
                    slot = (t // SUB) % 2
                    sp.wait_ge(x_free, group_no(b, t) + 1)
                    sp.dma_start(xg[slot][:], x[b].rearrange("(p n) c -> p n c", n=N2)[:, t:t + SUB, :]).then_inc(x_in[slot], 16)

                def save_v0(b, t):
                    if t == 0:
                        sp.wait_ge(v_done, tile_no(b, 0) + 1)
                        sp.dma_start(first_v[b].rearrange("(a c) -> a c", a=1), v[0:1, 0, :]).then_inc(v0_out, 16)

                def store(b, t):
                    if t % SUB != SUB - 1:
                        return
                    slot = (t // SUB) % 2
                    sp.wait_ge(s_out0, tile_no(b, t) + 1)
                    sp.wait_ge(s_out1, tile_no(b, t) + 1)
                    for j in range(2):
                        sp.dma_start(spec1[b].rearrange("(j p n) c -> j p n c", j=2, n=N2)[j, :, t - SUB + 1:t + 1, :],
                                     s1o[:, slot, j]).then_inc(s_stored[slot], 16)

                def store_x2(b, t):
                    if t % SUB != SUB - 1:
                        return
                    slot = (t // SUB) % 2
                    sp.wait_ge(x2_out, tile_no(b, t) + 1)
                    sp.sem_inc(passed_sp, 1)
                    sp.dma_start(gate_t[b].rearrange("n p c -> p n c")[:, t - SUB + 1:t + 1, :],
                                 gto[:, slot].rearrange("p n c r -> p n (c r)")).then_inc(x2_stored[slot], 16)

                def store_mix(b, t):
                    if isinstance(b, int) and b == B - 1 and t == MIX:
                        sp.wait_ge(ad_used, MIX * B)
                        sp.dma_start(ad_mix, ad_sum[:]).then_inc(ad_stored, 16)
                        sp.dma_start(ad_bias, adb_sum[:]).then_inc(ad_stored, 16)

                pipelined(sp, B, N2, [(load_x, 0), (save_v0, 4), (load_adapter, 5), (store, 8), (store_x2, 10), (store_mix, 10)])
                sp.wait_ge(ad_stored, 32)
                for slot in range(2):
                    sp.wait_ge(s_stored[slot], 16 * 2 * B * Q // 2)
                    sp.wait_ge(x2_stored[slot], 16 * B * Q // 2)
                sp.wait_ge(v0_out, 16 * B)

            @block.scalar
            def _(act):
                def norm(b, t):
                    slot = (t // SUB) % 2
                    act.wait_ge(norm_ready, group_no(b, t) + 1)
                    if old(b, t, 2):
                        act.wait_ge(t_ps, tile_no(b, t) - 1)
                    op = act.activation(xn[:, t % 2], xg[slot][:, t % SUB], ACT.Identity,
                                        bias=shift[:, slot, t % SUB:t % SUB + 1],
                                        scale=rstd[:, slot, t % SUB:t % SUB + 1])
                    op.then_inc(xn_done, 1)

                def nt_high(b, t):
                    g = (t // SUB) % 2
                    act.wait_ge(t_ps, tile_no(b, t) + 1)
                    if old(b, t, 2 * SUB):
                        act.wait_ge(x2_ps, (group_no(b, t) - 1) * SUB)
                    act.activation(nth[:, g, :, (t % SUB) * P:(t % SUB + 1) * P],
                                   psT[t % 2][:].rearrange("p (k r) -> p k r", k=CT), ACT.Copy).then_inc(nt_hi, 1)

                def v_high(b, t):
                    act.wait_ge(v_done, tile_no(b, t) + 1)
                    if old(b, t, 2):
                        act.wait_ge(s_ps, 2 * (tile_no(b, t) - 1))
                    act.activation(vh[:, t % 2], v[:, t % 2], ACT.Copy).then_inc(v_hi, 1)

                def s_copy(b, t):
                    slot = (t // SUB) % 2
                    act.wait_ge(s_ps, 2 * tile_no(b, t) + 1)
                    if t % SUB == 0 and old(b, t, 2 * SUB):
                        act.wait_ge(s_stored[slot], 32 * (b * (Q // 2) + t // (2 * SUB)))
                    act.activation(s1o[:, slot, 0, t % SUB], psS[0][:], ACT.Copy).then_inc(s_out0, 1)

                def x2_copy(b, t):
                    slot, ct = (t // SUB) % 2, t % SUB
                    act.wait_ge(x2_ps, tile_no(b, t) + 1)
                    if ct == 0 and old(b, t, 2 * SUB):
                        act.wait_ge(x2_stored[slot], 16 * (b * (Q // 2) + t // (2 * SUB)))
                    act.activation(gto[:, slot, :, ct, :], psX[ct % 2][:].rearrange("p (n r) -> p n r", n=SUB),
                                   ACT.Identity, bias=bgc[:, ct:ct + 1]).then_inc(x2_out, 1)

                pipelined(act, B, N2, [(nt_high, 2), (v_high, 3), (norm, 1), (x2_copy, 6), (s_copy, 4)])

            @block.gpsimd
            def _(pool):
                pool.memset(power[:], -0.5).then_inc(power_set, 1)
                pool.memset(eps[:], EPS).then_inc(power_set, 1)
                pool.memset(minus[:], -1.0).then_inc(power_set, 1)
                pool.memset(ad_sum[:], 0.0).then_inc(ad_clear, 1)
                pool.memset(adb_sum[:], 0.0).then_inc(ad_clear, 1)
                pool.wait_ge(power_set, 3)

                def scalars(b, t):
                    if t % SUB:
                        return
                    slot = (t // SUB) % 2
                    n = group_no(b, t)
                    pool.wait_ge(mv_done, (n + 1) * SUB)
                    if old(b, t, 2 * SUB):
                        pool.wait_ge(xn_done, (n - 1) * SUB)
                    pool.tensor_tensor(rstd[:, slot], mv[:, slot, :, 1], eps[:], ALU.add).then_inc(pow_step, 1)
                    pool.tensor_tensor(shift[:, slot], mv[:, slot, :, 0], minus[:], ALU.mult).then_inc(pow_step, 1)
                    pool.wait_ge(pow_step, 3 * n + 2)
                    pool.tensor_tensor(rstd[:, slot], rstd[:, slot], power[:], ALU.pow).then_inc(pow_step, 1)
                    pool.wait_ge(pow_step, 3 * n + 3)
                    pool.tensor_tensor(shift[:, slot], shift[:, slot], rstd[:, slot], ALU.mult).then_inc(norm_ready, 1)

                def v_low(b, t):
                    pool.wait_ge(v_hi, tile_no(b, t) + 1)
                    pool.tensor_tensor(vl[:, t % 2], v[:, t % 2], vh[:, t % 2].bitcast(F32), ALU.subtract).then_inc(v_lo, 1)

                pipelined(pool, B, N2, [(scalars, 0), (v_low, 3)])

            @block.tensor
            def _(pe):
                def turn(b, t):
                    pe.wait_ge(xn_done, tile_no(b, t) + 1)
                    if old(b, t, 2):
                        pe.wait_ge(nt_lo, tile_no(b, t) - 1)
                    for kt in range(CT):
                        mm = pe.transpose(psT[t % 2][:, kt * P:(kt + 1) * P], xn[:, t % 2, kt * P:(kt + 1) * P], ident[:])
                    mm.then_inc(t_ps, 1)

                def project_v(b, t):
                    g = (t // SUB) % 2
                    pe.wait_ge(nt_lo, tile_no(b, t) + 1)
                    if old(b, t, 2):
                        pe.wait_ge(v_done, tile_no(b, t) - 1)
                    cols = slice((t % SUB) * P, (t % SUB + 1) * P)
                    for kt in range(CT):
                        mm = mm3(pe, psV[t % 2][:], nth[:, g, kt, cols], ntl[:, g, kt, cols], wvh[:, kt], wvl[:, kt],
                                 kt == 0, kt == CT - 1)
                    mm.then_inc(v_ps, 1)

                def project_x2(b, t):
                    g, ct = (t // SUB) % 2, t % SUB
                    if old(b, t, 2):
                        pe.wait_ge(x2_out, tile_no(b, t) - 1)
                    for kt in range(CT):
                        mm = mm3(pe, psX[ct % 2][:], wgh[:, kt, ct * P:(ct + 1) * P], wgl[:, kt, ct * P:(ct + 1) * P],
                                 nth[:, g, kt], ntl[:, g, kt], kt == 0, kt == CT - 1)
                    mm.then_inc(x2_ps, 1)

                def stage1(b, t):
                    pe.wait_ge(v_lo, tile_no(b, t) + 1)
                    for j in range(2):
                        if old(b, t, 1):
                            pe.wait_ge((s_out0, s_out1)[j], tile_no(b, t))
                        mm = mm3(pe, psS[j][:], s1h[:, t, j * P:(j + 1) * P], s1l[:, t, j * P:(j + 1) * P],
                                 vh[:, t % 2], vl[:, t % 2], True, True)
                        mm.then_inc(s_ps, 1)

                pipelined(pe, B, N2, [(turn, 2), (project_v, 3), (project_x2, 6), (stage1, 4)])

            @block.vector
            def _(dve):
                dve.sem_inc(x_free, 2)

                def moments(b, t):
                    if t % SUB:
                        return
                    slot = (t // SUB) % 2
                    n = group_no(b, t)
                    dve.wait_ge(x_in[slot], 16 * (b * (Q // 2) + t // (2 * SUB) + 1))
                    for i in range(SUB):
                        dve.bn_stats(stats[:, slot, i], xg[slot][:, i]).then_inc(bn_step, 1)
                    dve.wait_ge(bn_step, n * SUB + SUB)
                    if old(b, t, 2 * SUB):
                        dve.wait_ge(norm_ready, n - 1)
                    dve.sem_inc(passed, 1)
                    for i in range(SUB):
                        dve.bn_aggr(mv[:, slot, i], stats[:, slot, i]).then_inc(mv_done, 1)

                def nt_low(b, t):
                    g = (t // SUB) % 2
                    cols = slice((t % SUB) * P, (t % SUB + 1) * P)
                    dve.wait_ge(nt_hi, tile_no(b, t) + 1)
                    dve.tensor_tensor(ntl[:, g, :, cols], psT[t % 2][:].rearrange("p (k r) -> p k r", k=CT),
                                      nth[:, g, :, cols].bitcast(F32), ALU.subtract).then_inc(nt_lo, 1)
                    if t % SUB == SUB - 1:
                        dve.sem_inc(x_free, 1)

                def v_bias(b, t):
                    dve.wait_ge(v_ps, tile_no(b, t) + 1)
                    if old(b, t, 2):
                        dve.wait_ge(v_lo, tile_no(b, t) - 1)
                    if t == 2:
                        dve.wait_ge(v0_out, 16 * (b + 1))
                    dve.tensor_tensor(v[:, t % 2], psV[t % 2][:], bvr, ALU.add).then_inc(v_done, 1)

                def mix(b, t):
                    if t >= MIX:
                        return
                    dve.wait_ge(ad_in, 32 * (b + 1))
                    dve.wait_ge(ad_clear, 2)
                    if old(b, t, 1):
                        dve.wait_ge(ad_used, MIX * b + t)
                    if isinstance(b, int) and b == 0:
                        dve.wait_ge(ids_in, 32)
                    w = wgt[:, b:b + 1] if isinstance(b, int) else wgt[:, bass.ds(b, 1)]
                    src, dst = (adb_load[:], adb_sum[:]) if t == CT else (ad_load[:, t], ad_sum[:, t])
                    dve.scalar_tensor_tensor(dst, src, w, dst, ALU.mult, ALU.add).then_inc(ad_used, 1)

                def s_copy(b, t):
                    slot = (t // SUB) % 2
                    dve.wait_ge(s_ps, 2 * tile_no(b, t) + 2)
                    if t % SUB == 0 and old(b, t, 2 * SUB):
                        dve.wait_ge(s_stored[slot], 32 * (b * (Q // 2) + t // (2 * SUB)))
                    dve.tensor_copy(s1o[:, slot, 1, t % SUB], psS[1][:]).then_inc(s_out1, 1)

                pipelined(dve, B, N2, [(nt_low, 2), (v_bias, 3), (moments, 0), (s_copy, 4), (mix, 8)])

    def middle(bc):
        with ExitStack() as st:
            def sb(name, shape, dt=F32):
                return st.enter_context(nc.sbuf_tensor(name, shape, dt))

            def ps(name):
                return st.enter_context(nc.psum_tensor(name, [P, C], F32))

            R = 4
            mats = sb("mats", [P, 6, P])
            xin = sb("m_xin", [P, 2, GB, C])
            spec = sb("m_spec", [P, 2, 2, C])
            zs = sb("m_zs", [P, R, C])
            m1 = sb("m_m1", [P, R, C])
            m2 = sb("m_m2", [P, R, C])
            u = sb("m_u", [P, R, C])
            wo = sb("m_wo", [P, 2, B, C])
            psZ = [ps(f"m_psZ{i}") for i in range(R)]
            psF = [ps("m_psF0"), ps("m_psF1")]
            psW = [ps("m_psW0"), ps("m_psW1")]
            wraw = sb("m_wraw", [P, CT, C])
            ad_raw = sb("m_ad_raw", [P, CT, C])
            small_in = sem("m_small_in")
            consts_in = sem("m_consts_in")
            turned = sem("m_turned")
            high = sem("m_high")
            low = sem("m_low")
            x_in = [sem(f"m_x_in{i}") for i in range(2)]
            first_in = [sem(f"m_first_in{i}") for i in range(4)]
            f_ps = sem("m_f_ps")
            f_done = sem("m_f_done")
            z_ps = sem("m_z_ps")
            zs_done = sem("m_zs_done")
            m1_done = sem("m_m1_done")
            m2_done = sem("m_m2_done")
            u_done = sem("m_u_done")
            w_ps = sem("m_w_ps")
            w_out = sem("m_w_out")
            stored = [sem(f"m_stored{i}") for i in range(2)]
            block = st.enter_context(nc.Block())

            CONSTS = 6 + CT
            PIECES = (slice(B, GB), slice(0, 2), slice(2, 4), slice(4, B))

            T = 2 * GB

            def group(i, t):
                return i * 2 + t // GB

            def data_no(i, t):
                return group(i, t) * B + t % GB - 1

            FWD, SAME, CROSS, INV = range(4)

            def kind(m, i, t):
                return mats[:, m if early(i, t, 1) else {FWD: 4, INV: 5}[m], :]

            def rows_of(spec_dram, g):
                by_group = spec_dram.rearrange("b (g p) c -> g p b c", p=P)
                if isinstance(g, int):
                    return by_group[g]
                return by_group[bass.ds(g, 1)].rearrange("g p b c -> (g p) b c")

            def early(i, t, first_groups=2):
                return isinstance(i, int) and i == 0 and t // GB < first_groups

            @block.sync
            def _(sp):
                sp.dma_start(mats[:], consts["mid"]).then_inc(small_in, 16)

                def load(i, t):
                    if t % GB:
                        return
                    par = t // GB
                    if early(i, t, 1):
                        for k, piece in enumerate(PIECES):
                            sp.dma_start(xin[:, par, piece], rows_of(spec1, 0)[:, piece]).then_inc(first_in[k], 16)
                        return
                    if not early(i, t):
                        sp.wait_ge(z_ps, (group(i, t) - 1) * B)
                    sp.dma_start(xin[:, par], rows_of(spec1, group(i, t))).then_inc(x_in[par], 16)

                def load_consts(i, t):
                    if not isinstance(i, int) or t != GB:
                        return
                    if i > 0:
                        sp.dma_start(wraw[:], out_w.rearrange("(k p) c -> p k c", p=P)).then_inc(consts_in, 16)
                        sp.dma_start(ad_raw[:], ad_mix).then_inc(consts_in, 16)
                        return
                    sp.dma_start(bc["s4"][:], consts["s4"].rearrange("(j p) n r -> p j n r", p=P)).then_inc(consts_in, 16)
                    with nc.allow_non_contiguous_dma(reason="4096 words, once"):
                        for ct in range(CT):
                            sp.dma_start(bc["v0"][:, ct], first_v.rearrange("b (c p) -> c p b", p=P)[ct]).then_inc(consts_in, 16)
                    sp.dma_start(bc["bor"][:], out_b.rearrange("(a c) -> a c", a=1).partition_broadcast(P)).then_inc(consts_in, 16)
                    sp.dma_start(bc["bfr"][:], ad_bias).then_inc(consts_in, 16)
                    sp.dma_start(bc["ident"][:], consts["ident"]).then_inc(consts_in, 16)

                pipelined(sp, GROUPS // 2, T, [(load, 0), (load_consts, 0)])
                sp.wait_ge(consts_in, 16 * CONSTS)

            @block.tensor
            def _(pe):
                pe.wait_ge(small_in, 16)

                def stage2(i, t):
                    par = t // GB
                    first = early(i, t, 1)
                    if t % GB == 0:
                        if first:
                            pe.wait_ge(first_in[0], 16)
                        else:
                            pe.wait_ge(x_in[par], 16 * (i + par))
                        if not early(i, t, 1):
                            pe.wait_ge(f_done, 4 * group(i, t))
                        if first:
                            for k, m in enumerate((SAME, CROSS)):
                                pe.matmul(psF[k][:], kind(m, i, t), xin[:, par, B, :], start=True, stop=True).then_inc(f_ps, 1)
                        else:
                            pe.matmul(psF[0][:], kind(FWD, i, t), xin[:, par, B, :], start=True, stop=True).then_inc(f_ps, 2)
                        return
                    n = data_no(i, t)
                    if first:
                        pe.wait_ge(first_in[1 if t <= 2 else 2 if t <= 4 else 3], 16)
                    if not (early(i, t, 1) and t <= R):
                        pe.wait_ge(zs_done, 2 * (n - 3))
                    pe.matmul(psZ[(t % GB - 1) % R][:], kind(FWD, i, t), xin[:, par, t % GB - 1, :],
                              start=True, stop=True).then_inc(z_ps, 1)

                def stage3(i, t):
                    if t % GB == 0:
                        return
                    n = data_no(i, t)
                    k = (t % GB - 1) % 2
                    pe.wait_ge(u_done, n + 1)
                    if not (early(i, t, 1) and t < 3):
                        pe.wait_ge(w_out, n - 1)
                    pe.matmul(psW[k][:], kind(INV, i, t), u[:, (t % GB - 1) % R, :], start=True, stop=True).then_inc(w_ps, 1)

                pipelined(pe, GROUPS // 2, T, [(stage2, 0), (stage3, 4)])
                pe.wait_ge(consts_in, 16 * CONSTS)
                pe.wait_ge(zs_done, 2 * GROUPS * B)
                for d in range(CT):
                    for ot in range(CT):
                        mm = pe.transpose(psZ[d][:, ot * P:(ot + 1) * P], ad_raw[:, ot, d * P:(d + 1) * P], bc["ident"][:])
                    mm.then_inc(turned, 1)

            @block.scalar
            def _(act):
                def spectrum(i, t, m):
                    if t % GB:
                        return
                    par = t // GB
                    if early(i, t, 1):
                        act.wait_ge(f_ps, m + 1)
                        act.activation(spec[:, par, m, :], psF[m][:], ACT.Copy).then_inc(f_done, 2)
                        return
                    act.wait_ge(f_ps, 2 * group(i, t) + 2)
                    if m == 0 and not early(i, t):
                        act.wait_ge(u_done, (group(i, t) - 1) * B)
                    for half in range(2):
                        act.activation(spec[half * 64:(half + 1) * 64, par, m, :], psF[0][m * 64:(m + 1) * 64, :],
                                       ACT.Copy, scale=-1.0 if (m, half) == (1, 0) else 1.0).then_inc(f_done, 1)

                def swap(i, t):
                    if t % GB == 0:
                        return
                    k = (t % GB - 1) % R
                    act.wait_ge(m1_done, data_no(i, t) + 1)
                    if not (early(i, t, 1) and t <= R):
                        act.wait_ge(m2_done, data_no(i, t) - R + 1)
                    for half in range(2):
                        act.activation(zs[(1 - half) * 64:(2 - half) * 64, k, :], psZ[(t % GB - 1) % R][half * 64:(half + 1) * 64, :],
                                       ACT.Copy).then_inc(zs_done, 1)

                def out_copy(i, t):
                    if t % GB == 0:
                        return
                    par, b = t // GB, t % GB - 1
                    act.wait_ge(w_ps, data_no(i, t) + 1)
                    if b == 0 and not early(i, t):
                        act.wait_ge(stored[par], 32 * i)
                    act.activation(wo[:, par, b, :], psW[b % 2][:], ACT.Copy).then_inc(w_out, 1)

                def store(i, t):
                    if t % GB not in (B // 2, B):
                        return
                    par = t // GB
                    batches = slice(t % GB - B // 2, t % GB)
                    act.wait_ge(w_out, data_no(i, t) + 1)
                    act.dma_start(rows_of(spec3, group(i, t))[:, batches], wo[:, par, batches]).then_inc(stored[par], 16)

                pipelined(act, GROUPS // 2, T, [(lambda i, t: spectrum(i, t, 0), 0), (out_copy, 4),
                                              (lambda i, t: spectrum(i, t, 1), 0), (swap, 0), (store, 5)])
                act.wait_ge(consts_in, 16 * CONSTS)
                act.activation(bc["woh"][:], wraw[:], ACT.Copy).then_inc(high, 1)
                for d in range(CT):
                    act.wait_ge(turned, d + 1)
                    act.activation(bc["wfh"][:, d], psZ[d][:], ACT.Copy).then_inc(high, 1)
                for par in range(2):
                    act.wait_ge(stored[par], 32 * GROUPS // 2)

            @block.gpsimd
            def _(pool):
                def cross_part(i, t):
                    if t % GB == 0:
                        return
                    par, b = t // GB, t % GB - 1
                    n = data_no(i, t)
                    if b == 0:
                        pool.wait_ge(f_done, 4 * group(i, t) + 4)
                    if not (early(i, t, 1) and b < R):
                        pool.wait_ge(u_done, n - R + 1)
                    pool.wait_ge(zs_done, 2 * n + 2)
                    pool.tensor_tensor(m2[:, b % R, :], zs[:, b % R, :], spec[:, par, 1, :], ALU.mult).then_inc(m2_done, 1)

                pipelined(pool, GROUPS // 2, T, [(cross_part, 0)])

            @block.vector
            def _(dve):
                def same_part(i, t):
                    if t % GB == 0:
                        return
                    par, b = t // GB, t % GB - 1
                    n = data_no(i, t)
                    dve.wait_ge(z_ps, n + 1)
                    if b == 0:
                        dve.wait_ge(f_done, 4 * group(i, t) + 2)
                    if not (early(i, t, 1) and b < R):
                        dve.wait_ge(u_done, n - R + 1)
                    dve.tensor_tensor(m1[:, b % R, :], psZ[b % R][:], spec[:, par, 0, :], ALU.mult).then_inc(m1_done, 1)

                def product(i, t):
                    if t % GB == 0:
                        return
                    b = t % GB - 1
                    n = data_no(i, t)
                    dve.wait_ge(m1_done, n + 1)
                    dve.wait_ge(m2_done, n + 1)
                    if not (early(i, t, 1) and b < R):
                        dve.wait_ge(w_ps, n - R + 1)
                    dve.tensor_tensor(u[:, b % R, :], m1[:, b % R, :], m2[:, b % R, :], ALU.add).then_inc(u_done, 1)

                pipelined(dve, GROUPS // 2, T, [(same_part, 0), (product, 2)])
                dve.wait_ge(high, 1)
                dve.tensor_tensor(bc["wol"][:], wraw[:], bc["woh"][:].bitcast(F32), ALU.subtract).then_inc(low, 1)
                for d in range(CT):
                    dve.wait_ge(high, d + 2)
                    dve.tensor_tensor(bc["wfl"][:, d], psZ[d][:], bc["wfh"][:, d].bitcast(F32), ALU.subtract).then_inc(low, 1)

    def back(bc):
        with ExitStack() as st:
            def sb(name, shape, dt=F32):
                return st.enter_context(nc.sbuf_tensor(name, shape, dt))

            def ps(name):
                return st.enter_context(nc.psum_tensor(name, [P, C], F32))

            s4, woh, wol, wfh, wfl, v0, bor, bfr, ident = (
                bc[k] for k in ("s4", "woh", "wol", "wfh", "wfl", "v0", "bor", "bfr", "ident"))
            edge = sb("b_edge", [P, 2, N2, C])
            D = 4
            fin = sb("b_fin", [P, 2, 2, C])
            gin = sb("b_gin", [P, 2, CT, P])
            xin = sb("b_xin", [P, D, C])
            corr = sb("b_corr", [P, 2, C])
            o = sb("b_o", [P, C])
            oh = sb("b_oh", [P, 2, C], F32R)
            ol = sb("b_ol", [P, 2, C], F32R)
            y = sb("b_y", [P, 2, C])
            stats = sb("b_stats", [P, 6])
            mv = sb("b_mv", [P, 2])
            rstd = sb("b_rstd", [P, 2])
            shift = sb("b_shift", [P, 2])
            power = sb("b_power", [P, 1])
            eps = sb("b_eps", [P, 1])
            minus = sb("b_minus", [P, 1])
            z = sb("b_z", [P, 2, C])
            yb = sb("b_yb", [P, D, C])
            zh = sb("b_zh", [P, 2, C], F32R)
            zl = sb("b_zl", [P, 2, C], F32R)
            res = sb("b_res", [P, D, C])
            psC = [ps("b_psC0"), ps("b_psC1")]
            psO = [ps("b_psO0"), ps("b_psO1")]
            psT = [ps("b_psT0"), ps("b_psT1")]
            psF = [ps("b_psF0"), ps("b_psF1")]

            EQ = 1
            edge_in = [sem(f"b_edge_in{i}") for i in range(N2 // EQ)]
            power_set = sem("b_power_set")
            passed = sem("b_passed")
            passed_pool = sem("b_passed_pool")
            f_in = [sem(f"b_f_in{i}") for i in range(2)]
            g_in = [sem(f"b_g_in{i}") for i in range(2)]
            x_in = [sem(f"b_x_in{i}") for i in range(D)]
            corr_step = sem("b_corr_step")
            corr_done = sem("b_corr_done")
            xb_done = sem("b_xb_done")
            c_ps = sem("b_c_ps")
            a_done = sem("b_a_done")
            o_done = sem("b_o_done")
            o_hi = sem("b_o_hi")
            o_lo = sem("b_o_lo")
            o_ps = sem("b_o_ps")
            y_done = sem("b_y_done")
            bn_step = sem("b_bn_step")
            mv_done = sem("b_mv_done")
            pow_step = sem("b_pow_step")
            norm_ready = sem("b_norm_ready")
            z_done = sem("b_z_done")
            yb_done = sem("b_yb_done")
            t_ps = sem("b_t_ps")
            z_hi = sem("b_z_hi")
            z_lo = sem("b_z_lo")
            ff_ps = sem("b_ff_ps")
            res_done = sem("b_res_done")
            out_stored = [sem(f"b_out_stored{i}") for i in range(D)]
            block = st.enter_context(nc.Block())

            def no(b, t):
                return b * N2 + t

            @block.sync
            def _(sp):
                def load_edges(b, t):
                    if not (isinstance(b, int) and b == 0) or t % EQ:
                        return
                    for q in range(2):
                        sp.dma_start(edge[:, q, t:t + EQ], edge_f[q].rearrange("p (n c) -> p n c", n=N2)[:, t:t + EQ]).then_inc(
                            edge_in[t // EQ], 16)

                def load_conv(b, t):
                    if old(b, t, 2):
                        sp.wait_ge(c_ps, no(b, t) - 1)
                    sp.dma_start(fin[:, t % 2], spec3[b].rearrange("(j p n) c -> n p j c", j=2, n=N2)[t]).then_inc(f_in[t % 2], 16)

                def load_gate(b, t):
                    if old(b, t, 2):
                        sp.wait_ge(o_done, no(b, t) - 1)
                    sp.dma_start(gin[:, t % 2], gate_t[b, t].rearrange("p (c r) -> p c r", c=CT)).then_inc(g_in[t % 2], 16)

                def load_x(b, t):
                    if old(b, t, D):
                        sp.wait_ge(y_done, no(b, t) - D + 1)
                    sp.dma_start(xin[:, t % D], x[b].rearrange("(p n) c -> n p c", n=N2)[t]).then_inc(x_in[t % D], 16)

                pipelined(sp, B, N2, [(load_conv, 0), (load_edges, 0), (load_gate, 0), (load_x, 0)])

            @block.gpsimd
            def _(pool):
                pool.memset(power[:], -0.5).then_inc(power_set, 1)
                pool.memset(eps[:], EPS).then_inc(power_set, 1)
                pool.memset(minus[:], -1.0).then_inc(power_set, 1)
                pool.wait_ge(power_set, 3)

                def scalars(b, t):
                    pool.wait_ge(mv_done, no(b, t) + 1)
                    if old(b, t, 2):
                        pool.wait_ge(z_done, no(b, t) - 1)
                    r, m = rstd[:, t % 2:t % 2 + 1], shift[:, t % 2:t % 2 + 1]
                    pool.tensor_tensor(r, mv[:, 1:2], eps[:], ALU.add).then_inc(pow_step, 1)
                    pool.tensor_tensor(m, mv[:, 0:1], minus[:], ALU.mult).then_inc(pow_step, 1)
                    pool.wait_ge(pow_step, 3 * no(b, t) + 2)
                    pool.tensor_tensor(r, r, power[:], ALU.pow).then_inc(pow_step, 1)
                    pool.wait_ge(pow_step, 3 * no(b, t) + 3)
                    pool.tensor_tensor(m, m, r, ALU.mult).then_inc(norm_ready, 1)

                def correct(b, t):
                    if old(b, t, 2):
                        pool.wait_ge(o_done, no(b, t) - 1)
                    pool.sem_inc(passed_pool, 1)
                    if t % EQ == 0:
                        pool.wait_ge(edge_in[t // EQ], 32)
                    v0b = v0[:, :, b:b + 1] if isinstance(b, int) else v0[:, :, bass.ds(b, 1)]
                    pool.tensor_tensor(corr[:, t % 2].rearrange("p (c r) -> p c r", c=CT),
                                       edge[:, 0, t].rearrange("p (c r) -> p c r", c=CT),
                                       v0b.to_broadcast([P, CT, P]), ALU.mult).then_inc(corr_step, 1)
                    pool.wait_ge(corr_step, no(b, t) + 1)
                    pool.tensor_tensor(corr[:, t % 2], corr[:, t % 2], edge[:, 1, t], ALU.add).then_inc(corr_done, 1)

                def bias_y(b, t):
                    pool.wait_ge(y_done, no(b, t) + 1)
                    if old(b, t, D):
                        pool.wait_ge(res_done, no(b, t) - D + 1)
                    pool.tensor_tensor(yb[:, t % D], y[:, t % 2], bfr[:], ALU.add).then_inc(yb_done, 1)

                pipelined(pool, B, N2, [(correct, 0), (scalars, 2), (bias_y, 2)])

            @block.scalar
            def _(act):
                def o_high(b, t):
                    act.wait_ge(o_done, no(b, t) + 1)
                    if old(b, t, 2):
                        act.wait_ge(o_ps, no(b, t) - 1)
                    act.activation(oh[:, t % 2], o[:], ACT.Copy).then_inc(o_hi, 1)

                def norm(b, t):
                    act.wait_ge(norm_ready, no(b, t) + 1)
                    if old(b, t, 2):
                        act.wait_ge(t_ps, no(b, t) - 1)
                    act.activation(z[:, t % 2], y[:, t % 2], ACT.Identity, bias=shift[:, t % 2:t % 2 + 1],
                                   scale=rstd[:, t % 2:t % 2 + 1]).then_inc(z_done, 1)

                def z_high(b, t):
                    act.wait_ge(t_ps, no(b, t) + 1)
                    if old(b, t, 2):
                        act.wait_ge(ff_ps, no(b, t) - 1)
                    act.activation(zh[:, t % 2], psT[t % 2][:], ACT.Copy).then_inc(z_hi, 1)

                def store(b, t):
                    act.wait_ge(res_done, no(b, t) + 1)
                    act.dma_start(out[b].rearrange("(p n) c -> n p c", n=N2)[t], res[:, t % D]).then_inc(out_stored[t % D], 16)

                pipelined(act, B, N2, [(o_high, 1), (z_high, 3), (norm, 2), (store, 6)])
                for i in range(D):
                    act.wait_ge(out_stored[i], 16 * B * N2 // D)

            @block.tensor
            def _(pe):
                def conv(b, t):
                    pe.wait_ge(f_in[t % 2], 16 * (b * (N2 // 2) + t // 2 + 1))
                    if old(b, t, 2):
                        pe.wait_ge(a_done, no(b, t) - 1)
                    for ct in range(CT):
                        for j in range(2):
                            mm = pe.matmul(psC[t % 2][:, ct * P:(ct + 1) * P], fin[:, t % 2, j, ct * P:(ct + 1) * P],
                                           s4[:, j, t, :], start=(j == 0), stop=(j == 1))
                    mm.then_inc(c_ps, 1)

                def project(b, t):
                    pe.wait_ge(o_lo, no(b, t) + 1)
                    if old(b, t, 2):
                        pe.wait_ge(y_done, no(b, t) - 1)
                    for ct in range(CT):
                        mm = mm3(pe, psO[t % 2][:], oh[:, t % 2, ct * P:(ct + 1) * P], ol[:, t % 2, ct * P:(ct + 1) * P],
                                 woh[:, ct], wol[:, ct], ct == 0, ct == CT - 1)
                    mm.then_inc(o_ps, 1)

                def turn(b, t):
                    pe.wait_ge(z_done, no(b, t) + 1)
                    if old(b, t, 2):
                        pe.wait_ge(z_lo, no(b, t) - 1)
                    for ct in range(CT):
                        mm = pe.transpose(psT[t % 2][:, ct * P:(ct + 1) * P], z[:, t % 2, ct * P:(ct + 1) * P], ident[:])
                    mm.then_inc(t_ps, 1)

                def adapt(b, t):
                    pe.wait_ge(z_lo, no(b, t) + 1)
                    if old(b, t, 2):
                        pe.wait_ge(res_done, no(b, t) - 1)
                    for ct in range(CT):
                        mm = mm3(pe, psF[t % 2][:], zh[:, t % 2, ct * P:(ct + 1) * P], zl[:, t % 2, ct * P:(ct + 1) * P],
                                 wfh[:, ct], wfl[:, ct], ct == 0, ct == CT - 1)
                    mm.then_inc(ff_ps, 1)

                pipelined(pe, B, N2, [(conv, 1), (project, 2), (turn, 3), (adapt, 4)])

            @block.vector
            def _(dve):
                def bias_x(b, t):
                    dve.wait_ge(x_in[t % D], 16 * (b * (N2 // D) + t // D + 1))
                    dve.tensor_tensor(xin[:, t % D], xin[:, t % D], bor[:], ALU.add).then_inc(xb_done, 1)

                def gate(b, t):
                    dve.wait_ge(corr_done, no(b, t) + 1)
                    dve.wait_ge(c_ps, no(b, t) + 1)
                    dve.tensor_tensor(corr[:, t % 2], psC[t % 2][:], corr[:, t % 2], ALU.add).then_inc(a_done, 1)
                    dve.wait_ge(a_done, no(b, t) + 1)
                    dve.wait_ge(g_in[t % 2], 16 * (b * (N2 // 2) + t // 2 + 1))
                    if old(b, t, 1):
                        dve.wait_ge(o_lo, no(b, t))
                    dve.tensor_tensor(o[:], corr[:, t % 2], gin[:, t % 2].rearrange("p c r -> p (c r)"),
                                      ALU.mult).then_inc(o_done, 1)

                def o_low(b, t):
                    dve.wait_ge(o_hi, no(b, t) + 1)
                    dve.tensor_tensor(ol[:, t % 2], o[:], oh[:, t % 2].bitcast(F32), ALU.subtract).then_inc(o_lo, 1)

                def residual(b, t):
                    dve.wait_ge(o_ps, no(b, t) + 1)
                    dve.wait_ge(xb_done, no(b, t) + 1)
                    if old(b, t, 2):
                        dve.wait_ge(yb_done, no(b, t) - 1)
                        dve.wait_ge(z_done, no(b, t) - 1)
                    dve.tensor_tensor(y[:, t % 2], psO[t % 2][:], xin[:, t % D], ALU.add).then_inc(y_done, 1)
                    dve.wait_ge(y_done, no(b, t) + 1)
                    dve.bn_stats(stats[:], y[:, t % 2]).then_inc(bn_step, 1)
                    dve.wait_ge(bn_step, no(b, t) + 1)
                    if old(b, t, 1):
                        dve.wait_ge(norm_ready, no(b, t))
                    dve.sem_inc(passed, 1)
                    dve.bn_aggr(mv[:], stats[:]).then_inc(mv_done, 1)

                def z_low(b, t):
                    dve.wait_ge(z_hi, no(b, t) + 1)
                    dve.tensor_tensor(zl[:, t % 2], psT[t % 2][:], zh[:, t % 2].bitcast(F32), ALU.subtract).then_inc(z_lo, 1)

                def finish(b, t):
                    dve.wait_ge(ff_ps, no(b, t) + 1)
                    dve.wait_ge(yb_done, no(b, t) + 1)
                    if old(b, t, D):
                        dve.wait_ge(out_stored[t % D], 16 * (b * (N2 // D) + t // D))
                    dve.tensor_tensor(res[:, t % D], psF[t % 2][:], yb[:, t % D], ALU.add).then_inc(res_done, 1)

                pipelined(dve, B, N2, [(finish, 5), (bias_x, 0), (gate, 1), (o_low, 1), (residual, 2), (z_low, 3)])

    with ExitStack() as st:
        def hold(name, shape, dt=F32):
            return st.enter_context(nc.sbuf_tensor(name, shape, dt))

        fc = {
            "s1h": hold("s1h", [P, N2, ROWS], F32R), "s1l": hold("s1l", [P, N2, ROWS], F32R),
            "wvh": hold("wvh", [P, CT, C], F32R), "wvl": hold("wvl", [P, CT, C], F32R),
            "wgh": hold("wgh", [P, CT, C], F32R), "wgl": hold("wgl", [P, CT, C], F32R),
            "ident": hold("fident", [P, P]), "bv3": hold("bv3", [P, 3 * C]), "bgc": hold("bgc", [P, CT]),
            "xg0": hold("xg0", [P, SUB, C]), "x_in": [sem(f"f_x_in{i}") for i in range(2)],
        }
        prep(fc)
        front(fc)
    with ExitStack() as st:
        def hold(name, shape, dt=F32):
            return st.enter_context(nc.sbuf_tensor(name, shape, dt))

        bc = {
            "s4": hold("b_s4", [P, 2, N2, P]),
            "woh": hold("woh", [P, CT, C], F32R), "wol": hold("wol", [P, CT, C], F32R),
            "wfh": hold("wfh", [P, CT, C], F32R), "wfl": hold("wfl", [P, CT, C], F32R),
            "v0": hold("b_v0", [P, CT, B]), "bor": hold("bor", [P, C]), "bfr": hold("bfr", [P, C]),
            "ident": hold("b_ident", [P, P]),
        }
        middle(bc)
        back(bc)


_INS = ['L0_attn_x', 'L0_attn_in_proj_w', 'L0_attn_in_proj_b', 'L0_attn_short_w', 'L0_attn_short_b', 'L0_attn_fw1',
        'L0_attn_fb1', 'L0_attn_fw2', 'L0_attn_fb2', 'L0_attn_fw3', 'L0_attn_fb3', 'L0_attn_out_w', 'L0_attn_out_b',
        'L0_ffn_W', 'L0_ffn_b', 'L0_ffn_ids', 'L0_ffn_weights']


def kernel(**inputs):
    import concourse.bacc as _bacc
    from concourse.bass_utils import run_bass_kernel_spmd as _run

    nc = _bacc.Bacc("TRN2", target_bir_lowering=False, num_devices=1)
    arrays, args, consts = {}, [], {}
    for name in _INS:
        a = np.ascontiguousarray(inputs[name])
        arrays[f"in_{name}_dram"] = a
        args.append(nc.dram_tensor(f"in_{name}_dram", a.shape, mybir.dt.from_np(a.dtype), kind="ExternalInput").ap())
    for name, a in stage_matrices().items():
        a = np.ascontiguousarray(a)
        arrays[f"const_{name}_dram"] = a
        consts[name] = nc.dram_tensor(f"const_{name}_dram", a.shape, mybir.dt.from_np(a.dtype), kind="ExternalInput").ap()
    out = nc.dram_tensor("out_0_dram", (B, L, C), F32, kind="ExternalOutput").ap()
    hyena_adapter_kernel(nc, *args, consts, out)
    r = _run(nc, [arrays], core_ids=[0])
    return r.results[0]["out_0_dram"]
```
